# Optimizing a Trainium2 kernel written in Bass

```python
import numpy as np
import jax
import jax.numpy as jnp

def _softmax(x, axis=-1):
    return jax.nn.softmax(x, axis=axis)

def _gelu(x):
    return jax.nn.gelu(x, approximate=True)

def _silu(x):
    return jax.nn.silu(x)

def _sigmoid(x):
    return jax.nn.sigmoid(x)

def _layernorm(x, axis=-1, eps=1e-05):
    m = jnp.mean(x, axis=axis, keepdims=True)
    v = jnp.var(x, axis=axis, keepdims=True)
    return (x - m) / jnp.sqrt(v + eps)

def _scatter_add(tgt, idx, src, axis=0):
    return tgt.at[idx].add(src)

def _segment_sum(src, seg, n):
    return jax.ops.segment_sum(src, seg, n)
kernel_name = 'mk_adaln_d2_jaxref_r8_d86b5f'

def setup_inputs(seed: int=0):
    np.random.seed(seed)
    _w = jnp.asarray

    def _L0_attn_setup():
        import jax, jax.numpy as jnp
        import numpy as np
        HIDDEN = 128
        N_HEAD = 16
        HEAD_DIM = HIDDEN // N_HEAD

        def _rope(q, k):
            S, D = (q.shape[-2], q.shape[-1])
            pos = jnp.arange(S, dtype=jnp.float32)[:, None]
            ids = jnp.arange(D // 2, dtype=jnp.float32)
            theta = jnp.power(jnp.float32(10000.0), 2.0 * ids / D)
            ang = pos / theta
            sin = jnp.repeat(jnp.sin(ang), 2, axis=-1)
            cos = jnp.repeat(jnp.cos(ang), 2, axis=-1)

            def rot(t):
                t2 = jnp.stack([-t[..., 1::2], t[..., 0::2]], axis=-1).reshape(t.shape)
                return t * cos + t2 * sin
            return (rot(q), rot(k))
        key = jax.random.key(seed)
        k1, k2, k3 = jax.random.split(key, 3)
        B, S = (4, 256)
        x = jax.random.normal(k1, (B, S, HIDDEN), dtype=jnp.float32)
        w_qkv = jax.random.normal(k2, (3 * HIDDEN, HIDDEN), dtype=jnp.float32) * HIDDEN ** (-0.5)
        w_out = jax.random.normal(k3, (HIDDEN, HIDDEN), dtype=jnp.float32) * HIDDEN ** (-0.5)
        return {'x': x, 'w_qkv': w_qkv, 'w_out': w_out}
    _L0_attn_in = _L0_attn_setup()

    def _L0_ffn_setup():
        import jax, jax.numpy as jnp
        import numpy as np
        NUM_EXPERTS = 8
        TOP_K = 2
        key = jax.random.key(seed)
        ks = jax.random.split(key, 5)
        B, L, E, H, N = (2, 256, 128, 256, NUM_EXPERTS)
        return {'x': jax.random.normal(ks[0], (B, L, E), dtype=jnp.float32), 'gate_kernel': jax.random.normal(ks[1], (E, N), dtype=jnp.float32) / np.sqrt(E), 'w0_kernel': jax.random.normal(ks[2], (N, E, H), dtype=jnp.float32) / np.sqrt(E), 'w1_kernel': jax.random.normal(ks[3], (N, E, H), dtype=jnp.float32) / np.sqrt(E), 'wo_kernel': jax.random.normal(ks[4], (N, H, E), dtype=jnp.float32) / np.sqrt(H)}
    _L0_ffn_in = _L0_ffn_setup()
    _L0_c = _w((lambda *s: np.random.randn(*s).astype(np.float32) * 0.05)(8, 128))
    _L0_wmod = _w((lambda *s: np.random.randn(*s).astype(np.float32) * 0.05)(128, 6 * 128) * 128 ** (-0.5))

    def _L1_attn_setup():
        import jax, jax.numpy as jnp
        import numpy as np
        DIM = 128
        HIDDEN = 256
        QK_DIM = 256
        LN_EPS = 1e-05
        key = jax.random.key(seed)
        ks = jax.random.split(key, 10)
        B, N = (4, 512)
        s = 0.02
        return {'x': jax.random.normal(ks[0], (B, N, DIM), dtype=jnp.float32), 'ln_g': jnp.ones((DIM,), jnp.float32), 'ln_b': jnp.zeros((DIM,), jnp.float32), 'W_hidden': jax.random.normal(ks[1], (DIM, HIDDEN * 2), jnp.float32) * s, 'b_hidden': jnp.zeros((HIDDEN * 2,), jnp.float32), 'W_qk': jax.random.normal(ks[2], (DIM, QK_DIM), jnp.float32) * s, 'b_qk': jnp.zeros((QK_DIM,), jnp.float32), 'os_gamma': jax.random.normal(ks[3], (2, QK_DIM), jnp.float32) * s, 'os_beta': jnp.zeros((2, QK_DIM), jnp.float32), 'W_out': jax.random.normal(ks[4], (HIDDEN, DIM), jnp.float32) * s, 'b_out': jnp.zeros((DIM,), jnp.float32)}
    _L1_attn_in = _L1_attn_setup()

    def _L1_ffn_setup():
        import jax, jax.numpy as jnp
        import numpy as np
        NUM_EXPERTS = 8
        D_MODEL = 128
        D_FF = 512
        BATCH, SEQ = (2, 512)
        key = jax.random.key(seed)
        k_x, k_w1, k_w2 = jax.random.split(key, 3)
        x = jax.random.normal(k_x, (BATCH, SEQ, D_MODEL), dtype=jnp.float32)
        w1 = jax.random.normal(k_w1, (NUM_EXPERTS, D_MODEL, D_FF), dtype=jnp.float32) * (1.0 / np.sqrt(D_MODEL))
        b1 = jnp.zeros((NUM_EXPERTS, D_FF), dtype=jnp.float32)
        w2 = jax.random.normal(k_w2, (NUM_EXPERTS, D_FF, D_MODEL), dtype=jnp.float32) * (1.0 / np.sqrt(D_FF))
        b2 = jnp.zeros((NUM_EXPERTS, D_MODEL), dtype=jnp.float32)
        return {'x': x, 'w1': w1, 'b1': b1, 'w2': w2, 'b2': b2}
    _L1_ffn_in = _L1_ffn_setup()
    _L1_c = _w((lambda *s: np.random.randn(*s).astype(np.float32) * 0.05)(8, 128))
    _L1_wmod = _w((lambda *s: np.random.randn(*s).astype(np.float32) * 0.05)(128, 6 * 128) * 128 ** (-0.5))
    _d = {'L0_attn_x': _L0_attn_in['x'], 'L0_attn_w_qkv': _L0_attn_in['w_qkv'], 'L0_attn_w_out': _L0_attn_in['w_out'], 'L0_ffn_gate_kernel': _L0_ffn_in['gate_kernel'], 'L0_ffn_w0_kernel': _L0_ffn_in['w0_kernel'], 'L0_ffn_w1_kernel': _L0_ffn_in['w1_kernel'], 'L0_ffn_wo_kernel': _L0_ffn_in['wo_kernel'], 'L0_c': _L0_c, 'L0_wmod': _L0_wmod, 'L1_attn_ln_g': _L1_attn_in['ln_g'], 'L1_attn_ln_b': _L1_attn_in['ln_b'], 'L1_attn_W_hidden': _L1_attn_in['W_hidden'], 'L1_attn_b_hidden': _L1_attn_in['b_hidden'], 'L1_attn_W_qk': _L1_attn_in['W_qk'], 'L1_attn_b_qk': _L1_attn_in['b_qk'], 'L1_attn_os_gamma': _L1_attn_in['os_gamma'], 'L1_attn_os_beta': _L1_attn_in['os_beta'], 'L1_attn_W_out': _L1_attn_in['W_out'], 'L1_attn_b_out': _L1_attn_in['b_out'], 'L1_ffn_w1': _L1_ffn_in['w1'], 'L1_ffn_b1': _L1_ffn_in['b1'], 'L1_ffn_w2': _L1_ffn_in['w2'], 'L1_ffn_b2': _L1_ffn_in['b2'], 'L1_c': _L1_c, 'L1_wmod': _L1_wmod}
    _x0 = _d['L0_attn_x']
    _d['L0_attn_x'] = jax.random.normal(jax.random.fold_in(jax.random.key(seed), 1), (8, 512, 128), dtype=_x0.dtype)
    del _x0
    return _d

def reference(L0_attn_x, L0_attn_w_qkv, L0_attn_w_out, L0_ffn_gate_kernel, L0_ffn_w0_kernel, L0_ffn_w1_kernel, L0_ffn_wo_kernel, L0_c, L0_wmod, L1_attn_ln_g, L1_attn_ln_b, L1_attn_W_hidden, L1_attn_b_hidden, L1_attn_W_qk, L1_attn_b_qk, L1_attn_os_gamma, L1_attn_os_beta, L1_attn_W_out, L1_attn_b_out, L1_ffn_w1, L1_ffn_b1, L1_ffn_w2, L1_ffn_b2, L1_c, L1_wmod):

    def _L0_attn_ref(x, w_qkv, w_out):
        import jax, jax.numpy as jnp
        import numpy as np
        HIDDEN = 128
        N_HEAD = 16
        HEAD_DIM = HIDDEN // N_HEAD

        def _rope(q, k):
            S, D = (q.shape[-2], q.shape[-1])
            pos = jnp.arange(S, dtype=jnp.float32)[:, None]
            ids = jnp.arange(D // 2, dtype=jnp.float32)
            theta = jnp.power(jnp.float32(10000.0), 2.0 * ids / D)
            ang = pos / theta
            sin = jnp.repeat(jnp.sin(ang), 2, axis=-1)
            cos = jnp.repeat(jnp.cos(ang), 2, axis=-1)

            def rot(t):
                t2 = jnp.stack([-t[..., 1::2], t[..., 0::2]], axis=-1).reshape(t.shape)
                return t * cos + t2 * sin
            return (rot(q), rot(k))
        B, S, _ = x.shape
        qkv = jnp.einsum('bsd,ed->bse', x, w_qkv)
        qkv = qkv.reshape(B, S, N_HEAD, 3 * HEAD_DIM).transpose(0, 2, 1, 3)
        q, k, v = jnp.split(qkv, 3, axis=-1)
        q, k = _rope(q, k)
        scores = jnp.einsum('bhqd,bhkd->bhqk', q, k)
        probs = jax.nn.softmax(scores, axis=-1)
        out = jnp.einsum('bhqk,bhkd->bhqd', probs, v)
        out = out.transpose(0, 2, 1, 3).reshape(B, S, HIDDEN)
        return jnp.einsum('bsd,ed->bse', out, w_out)

    def _L0_ffn_ref(x, gate_kernel, w0_kernel, w1_kernel, wo_kernel):
        import jax, jax.numpy as jnp
        import numpy as np
        NUM_EXPERTS = 8
        TOP_K = 2
        B, L, E = x.shape
        gate_logits = jnp.einsum('ble,en->bln', x, gate_kernel)
        top_k_weights, top_k_indices = jax.lax.top_k(gate_logits, TOP_K)
        softmax_probs = jax.nn.softmax(top_k_weights.astype(jnp.float32), axis=-1)
        weights = jnp.zeros_like(gate_logits)
        b_idx = jnp.arange(B)[:, None, None]
        l_idx = jnp.arange(L)[:, None]
        weights = weights.at[b_idx, l_idx, top_k_indices].set(softmax_probs)
        layer_w0 = jnp.einsum('ble,neh->blnh', x, w0_kernel)
        layer_w1 = jnp.einsum('ble,neh->blnh', x, w1_kernel)
        layer_mult = jax.nn.silu(layer_w0) * layer_w1
        intermediate = jnp.einsum('blnh,nhe->blne', layer_mult, wo_kernel)
        output = jnp.einsum('blne,bln->ble', intermediate, weights)
        return output

    def _L1_attn_ref(x, ln_g, ln_b, W_hidden, b_hidden, W_qk, b_qk, os_gamma, os_beta, W_out, b_out):
        import jax, jax.numpy as jnp
        import numpy as np
        DIM = 128
        HIDDEN = 256
        QK_DIM = 256
        LN_EPS = 1e-05
        seq_len = x.shape[-2]
        mu = jnp.mean(x, axis=-1, keepdims=True)
        var = jnp.mean(jnp.square(x - mu), axis=-1, keepdims=True)
        normed = (x - mu) * jax.lax.rsqrt(var + LN_EPS) * ln_g + ln_b
        h = jax.nn.silu(normed @ W_hidden + b_hidden)
        v, gate = (h[..., :HIDDEN], h[..., HIDDEN:])
        qk = jax.nn.silu(normed @ W_qk + b_qk)
        q = qk * os_gamma[0] + os_beta[0]
        k = qk * os_gamma[1] + os_beta[1]
        sim = jnp.einsum('bid,biD->bdD', q, k) / seq_len
        attn = jax.nn.softmax(sim, axis=-1)
        out = v * jnp.sum(attn, axis=-1)[:, None, :]
        out = out * gate
        out = out @ W_out + b_out
        return out + x

    def _L1_ffn_ref(x, w1, b1, w2, b2):
        import jax, jax.numpy as jnp
        import numpy as np
        NUM_EXPERTS = 8
        D_MODEL = 128
        D_FF = 512
        BATCH, SEQ = (2, 512)
        B, S, D = x.shape
        E = w1.shape[0]
        T = B * S // E
        tokens = x.reshape(E, T, D)
        h = jnp.einsum('etd,edf->etf', tokens, w1) + b1[:, None, :]
        h = jax.nn.gelu(h)
        y = jnp.einsum('etf,efd->etd', h, w2) + b2[:, None, :]
        return y.reshape(B, S, D)
    x = L0_attn_x
    mod = (_silu(L0_c) @ L0_wmod).reshape(L0_c.shape[0], 6, 1, -1)
    sa, ca, ga, sb, cb, gb = (mod[:, 0], mod[:, 1], mod[:, 2], mod[:, 3], mod[:, 4], mod[:, 5])
    ga = (2 * (ga >= 0) - 1) * jnp.maximum(jnp.abs(ga), 0.25)
    gb = (2 * (gb >= 0) - 1) * jnp.maximum(jnp.abs(gb), 0.25)
    h = _layernorm(x, axis=-1) * (1 + ca) + sa
    x = x + ga * _L0_attn_ref(h, L0_attn_w_qkv, L0_attn_w_out)
    h = _layernorm(x, axis=-1) * (1 + cb) + sb
    x = x + gb * _L0_ffn_ref(h, L0_ffn_gate_kernel, L0_ffn_w0_kernel, L0_ffn_w1_kernel, L0_ffn_wo_kernel)
    mod = (_silu(L1_c) @ L1_wmod).reshape(L1_c.shape[0], 6, 1, -1)
    sa, ca, ga, sb, cb, gb = (mod[:, 0], mod[:, 1], mod[:, 2], mod[:, 3], mod[:, 4], mod[:, 5])
    ga = (2 * (ga >= 0) - 1) * jnp.maximum(jnp.abs(ga), 0.25)
    gb = (2 * (gb >= 0) - 1) * jnp.maximum(jnp.abs(gb), 0.25)
    h = _layernorm(x, axis=-1) * (1 + ca) + sa
    x = x + ga * _L1_attn_ref(h, L1_attn_ln_g, L1_attn_ln_b, L1_attn_W_hidden, L1_attn_b_hidden, L1_attn_W_qk, L1_attn_b_qk, L1_attn_os_gamma, L1_attn_os_beta, L1_attn_W_out, L1_attn_b_out)
    h = _layernorm(x, axis=-1) * (1 + cb) + sb
    x = x + gb * _L1_ffn_ref(h, L1_ffn_w1, L1_ffn_b1, L1_ffn_w2, L1_ffn_b2)
    return x

_drawn_inputs = setup_inputs


def setup_inputs(seed=0):
    import zlib

    import numpy as np

    out = dict(_drawn_inputs(seed))
    spreads = {'L1_attn_ln_g': (1.0, 0.6),
     'L1_attn_ln_b': (0.0, 0.8),
     'L1_attn_b_hidden': (0.0, 0.8),
     'L1_attn_b_qk': (0.0, 0.8),
     'L1_attn_os_beta': (0.0, 0.8),
     'L1_attn_b_out': (0.0, 0.344),
     'L1_ffn_b1': (0.0, 0.488),
     'L1_ffn_b2': (0.0, 0.329)}
    factors = {'L1_attn_W_hidden': 8.0,
     'L1_attn_W_qk': 8.0,
     'L1_attn_os_gamma': 8.0,
     'L1_attn_W_out': 8.0}
    for name, (base, spread) in spreads.items():
        noise = np.random.default_rng([zlib.crc32(name.encode()), seed]).standard_normal(out[name].shape)
        drawn = base * np.exp(spread * noise) if base else spread * noise
        out[name] = jnp.asarray(drawn.astype(out[name].dtype))
    for name, factor in factors.items():
        out[name] = (out[name] * factor).astype(out[name].dtype)
    return out
```

```python
import numpy as np
import concourse.bass as bass
from concourse import mybir
from contextlib import ExitStack

NB, S, D = 8, 512, 128
P = 128
NT = S // P
HEADS, HD = 16, 8
GH = 4
GROUPS = HEADS // GH
PARTS = 3
STACK = HD * PARTS * PARTS
NEX, HID = 8, 256
HALVES = HID // P
UNITS = NEX * HALVES
QK = 256
HCH = 4
FCH = 4
EPS = 1e-5
GELU_C, GELU_A = 0.7978845608028654, 0.044715

LAG = {"P": -1, "A": 0, "B": 1, "C": 2}


def step_order():
    at = []

    def put(time, stage, step, *args):
        at.append((time, len(at), stage, step, args))

    for n in range(64):
        g, kt, j = n // 16, n % 16 // 4, n % 4
        put(n, "A", "exp", g, kt, j)
        if j == 3 and n < 63:
            put(n + 1.6, "A", "pv", g, kt)
        if g < GROUPS - 1:
            put(n + 0.3, "A", "max", g + 1, n % 16)
    for g in range(1, GROUPS):
        put(16 * g - 0.69, "A", "mparts", g)
        put(16 * g - 0.68, "A", "mT", g)
        put(16 * g - 0.67, "A", "mrow", g)
    for g in range(GROUPS - 1):
        put(16 * g + 17.8, "A", "pvs", g)
        put(16 * g + 18.7, "A", "pvT", g)
        put(16 * g + 19.6, "A", "onorm", g)
    put(25.1, "A", "load")
    put(1.8, "A", "vcopy")
    put(30.2, "A", "wog")
    tail = ["pvlast", "pvs3", "pvT3", "onorm3", "oT", "ot", "y", "x1", "stats", "rstd", "xn", "xT", "hT", "hi",
            "lo", "gate", "logits", "top", "route", "weights"]
    put(0.1, "B", "load")
    for n, name in enumerate(tail):
        put(0.5 + 1.1 * n, "B", name)
    first, every = 18.0, 2.85
    for u in range(UNITS):
        put(first + every * u, "B", "unit", u)
        if u % 2:
            put(first + every * u + 2.4, "B", "down", u // 2)
    put(63.9, "B", "x2")
    put(10, "P", "load")
    for n, name in enumerate(["stats", "rstd", "xn", "xT", "hT", "hi", "lo"]):
        put(13.2 + 1.1 * n, "P", name)
    for n in range(4):
        put(27.3 + 1.5 * n, "P", "proj", n)
        put(27.9 + 1.5 * n, "P", "rot", n)
    put(33.2, "P", "v")
    put(29.5, "P", "split", 0)
    put(33.5, "P", "store", 0)
    put(34.4, "P", "split", 1)
    put(38, "P", "store", 1)
    put(40.5, "P", "stack", 0)
    put(41, "P", "stack", 1)
    put(49, "P", "stack", 2)
    put(64, "P", "stack", 3)
    for n in range(16):
        put(48.3 + n * 0.97, "P", "max", 0, n)
    put(63.5, "P", "mparts", 0)
    put(63.6, "P", "mT", 0)
    put(63.7, "P", "mrow", 0)
    put(0.2, "C", "load")
    chain = ["stats", "rstd", "xn", "mod", "stats2", "rstd2", "xn2", "xT", "nT", "hi", "lo"]
    for n, name in enumerate(chain):
        put(1.15 + 1.1 * n, "C", name)
    t = 13.3
    for p in range(2):
        put(t + 1.5 * p, "C", "qk", p)
        put(t + 1.5 * p + 1.0, "C", "qkz", p)
        put(t + 1.5 * p + 2.2, "C", "qks", p)
        put(t + 1.5 * p + 2.9, "C", "qkgb", p)
    for n, c in enumerate((0, 2, 1, 3)):
        put(17.7 + 2.0 * n, "C", "hid", c)
        put(17.7 + 2.0 * n + 1.3, "C", "hids", c)
    put(24.6, "C", "sim")
    put(25.7, "C", "simmax")
    put(26.8, "C", "simexp")
    put(28.2, "C", "simsum")
    put(34.2, "C", "out")
    for n, name in enumerate(["res", "stats3", "rstd3", "xn3", "xT3", "nT3"]):
        put(35.3 + 1.3 * n, "C", name)
    for c in range(FCH):
        put(45.2 + 3.0 * c, "C", "up", c)
        put(45.2 + 3.0 * c + 1.4, "C", "upa", c)
        put(45.2 + 3.0 * c + 2.9, "C", "upg", c)
    put(59.3, "C", "dn")
    put(60.6, "C", "fin")
    put(63.0, "C", "outp")
    return [(stage, step, args) for _, _, stage, step, args in sorted(at)]


ORDER = step_order()

M0_USES = {
    ("A", "mT"): ("a_mrow", lambda g: g + 1), ("P", "mT"): ("a_mrow", lambda g: g + 1),
    ("A", "pvT"): ("a_o", lambda g: g + 1), ("B", "pvT3"): ("a_o", lambda: GROUPS),
    ("B", "oT"): ("a_ot", lambda: 1), ("B", "y"): ("a_x1", lambda: 1),
    ("B", "xT"): ("b_hT", lambda: 1), ("B", "gate"): ("b_lg", lambda: 1),
    ("B", "down"): ("b_acc", lambda e: e + 1),
}
M1_USES = {
    ("P", "xT"): ("p_hT", lambda: 1), ("P", "proj"): ("p_rot", lambda n: n + 1), ("P", "v"): ("p_vn", lambda: 1),
    ("C", "xT"): ("c_nT", lambda: 1), ("C", "qk"): ("c_qz", lambda p: p + 1),
    ("C", "hid"): ("c_hz", lambda c: (0, 2, 1, 3).index(c) + 1), ("C", "sim"): ("c_ea", lambda: 2),
    ("C", "out"): ("c_o1", lambda: 1), ("C", "xT3"): ("c_nT3", lambda: 1), ("C", "up"): ("c_u2", lambda c: c + 1),
    ("C", "dn"): ("c_y1", lambda: 1),
}

PER_BATCH = {
    "p_in": 32, "p_mv": 1, "p_eps": 1, "p_rstd": 1, "p_xn": 1, "p_xT": 1, "p_hT": 1, "p_hi": 1, "p_lo": 1,
    "p_proj": 4, "p_rot": 4, "p_v": 1, "p_vn": 1, "p_sum": 2, "p_part0": 2, "p_rem": 2, "p_part1": 2, "p_part2": 2,
    "p_stored0": 16, "p_stored1": 16 * PARTS, "p_stack0": 32, "p_stack1": 32, "p_stack2": 32, "p_stack3": 32,
    "a_in": 16, "a_xin": 16, "a_wog": 1, "a_vc": 1, "a_smf": 64, "a_max": 64, "a_mp": 4 * GROUPS, "a_mT": GROUPS, "a_mrow": GROUPS,
    "a_row": 16 * PARTS * GROUPS, "a_sef": 64, "a_exp": 64, "a_pv": 16, "a_pvs": GROUPS, "a_pvT": GROUPS,
    "a_rc": GROUPS, "a_o": GROUPS, "a_oT": 1, "a_ot": 1, "a_y": 1, "a_x1": 1,
    "b_in": 32, "b_mv": 1, "b_eps": 1, "b_rstd": 1, "b_xn": 1, "b_xT": 1, "b_hT": 1, "b_hi": 1, "b_lo": 1,
    "b_gate": 1, "b_lg": 1, "b_top": 1, "b_dif": 1, "b_e2": 1, "b_route": 7, "b_w0": UNITS, "b_w1": UNITS,
    "b_tanh": UNITS, "b_u": UNITS, "b_mu": UNITS, "b_down": NEX, "b_acc": NEX, "b_t": 1, "b_x2": 1,
    "c_in": 16 * 7, "c_mv": 1, "c_eps": 1, "c_rstd": 1, "c_xn": 1, "c_m1": 1, "c_h": 1, "c_mv2": 1, "c_eps2": 1,
    "c_rstd2": 1, "c_xn2": 1, "c_xT": 1, "c_nT": 1, "c_hi": 1, "c_lo": 1, "c_qk": 2, "c_qz": 2, "c_qt": 2,
    "c_qs": 2, "c_g": 4, "c_kq": 2, "c_hp": 4, "c_ht": 4, "c_hz": 4, "c_hs": 4, "c_vg": 2, "c_sim": 1, "c_nm": 1,
    "c_nms": 1, "c_ea": 2, "c_r": 1, "c_rs": 1, "c_wo": 1, "c_o": 1, "c_o1": 1, "c_res": 2, "c_x3": 1,
    "c_mv3": 1, "c_eps3": 1, "c_rstd3": 1, "c_xn3": 1, "c_xT3": 1, "c_nT3": 1, "c_up": 4, "c_uz": 4, "c_u2": 4, "c_ua": 4, "c_ub": 4, "c_ut": 4, "c_gl": 4,
    "c_dn": 1, "c_y1": 1, "c_yg": 1, "c_out": 1, "c_stored": 16,
}


def adaln_two_layers(nc, a, out):
    dt = mybir.dt
    f32, f32r, bf16, u32 = dt.float32, dt.float32r, dt.bfloat16, dt.uint32
    ALU = mybir.AluOpType
    ACT = mybir.ActivationFunctionType
    AX = mybir.AxisListType.X
    ctx = ExitStack()
    with ctx:
        used = []

        def sb(name, shape, dtype=f32):
            used.append((name, int(np.prod(shape[1:])) * (2 if dtype == bf16 else 4)))
            return ctx.enter_context(nc.sbuf_tensor(name, shape, dtype))

        def bank(name):
            return ctx.enter_context(nc.psum_tensor(name, [P, 512], f32))

        sig = {name: ctx.enter_context(nc.semaphore(name)) for name in PER_BATCH}

        def after(eng, name, b, k):
            value = b * PER_BATCH[name] + k
            if isinstance(value, int) and value <= 0:
                return
            eng.wait_ge(sig[name], value)

        def after_all(eng, *waits):
            counts = [(sig[name], b * PER_BATCH[name] + k) for name, b, k in waits]
            counts = [(s, v if isinstance(v, int) else eng.to_reg(v)) for s, v in counts
                      if not isinstance(v, int) or v > 0]
            eng.wait_ge(s_c, 16 * N_CONST)
            for s, v in counts:
                eng.wait_ge(s, v)

        mod_d = nc.dram_tensor("mod_d", [2, NB, 6 * D], f32).ap()
        parts_d = nc.dram_tensor("parts_d", [2, HEADS, HD, PARTS, PARTS, S], bf16).ap()

        cosT, sinT = sb("cosT", [P, S]), sb("sinT", [P, S])
        ident, identb = sb("ident", [P, P]), sb("identb", [P, P], bf16)
        nhalf = sb("nhalf", [P, NT])
        iota8 = sb("iota8", [P, NEX])
        wp_hi, wp_lo = sb("wp_hi", [P, 5, P], f32r), sb("wp_lo", [P, 5, P], f32r)
        wo0T = sb("wo0T", [P, D])
        e0_hi, e0_lo = sb("e0_hi", [P, NEX * HID], f32r), sb("e0_lo", [P, NEX * HID], f32r)
        e1_hi, e1_lo = sb("e1_hi", [P, NEX * HID], f32r), sb("e1_lo", [P, NEX * HID], f32r)
        eo = sb("eo", [P, NEX, HALVES, D])
        gate_w = sb("gate_w", [P, NEX])
        wh_hi, wh_lo = sb("wh_hi", [P, HCH * P], f32r), sb("wh_lo", [P, HCH * P], f32r)
        wqk = sb("wqk", [P, QK])
        bh, bhh = sb("bh", [P, HCH]), sb("bhh", [P, HCH])
        bqk = sb("bqk", [P, QK])
        gam, bet = sb("gam", [P, 2, QK]), sb("bet", [P, 2, QK])
        ln_gb = sb("ln_gb", [P, 2])
        wout = sb("wout", [P, 2, D])
        bout = sb("bout", [P, D])

        xp, xpn = sb("xp", [P, NT, D]), sb("xpn", [P, NT, D])
        hp = xpn[:, :, :].rearrange("p t d -> p (t d)")
        hp_hi, hp_lo = sb("hp_hi", [P, S], f32r), sb("hp_lo", [P, S], f32r)
        pmod = sb("pmod", [P, 2])
        rot1, rot2, rem = sb("rot1", [P, S]), sb("rot2", [P, S]), sb("rem", [P, S])
        parts = sb("parts", [P, PARTS, S], bf16)
        vtok = sb("vtok", [P, NT, D])
        qs, ks = sb("qs", [STACK + PARTS, HEADS, S], bf16), sb("ks", [STACK + PARTS, HEADS, S], bf16)
        vaug = sb("vaug", [P, NT, HEADS, 32])
        probs = sb("probs", [P, 2, GH, S])
        ga, wog = sb("ga", [P, D]), sb("wog", [P, D])
        negmax, mrem = sb("negmax", [P, 2, 16]), sb("mrem", [P, 16])
        mpart = sb("mpart", [P, PARTS, 16], bf16)
        mrow = sb("mrow", [PARTS * 16, P], bf16)
        pvs, rsum, otok, x1 = sb("pvs", [P, S]), sb("rsum", [P, 16]), sb("otok", [P, NT, D]), sb("x1", [P, NT, D])
        oT = pvs
        xbn = sb("xbn", [P, NT, D])
        hb = xbn[:, :, :].rearrange("p t d -> p (t d)")
        hb_hi, hb_lo = sb("hb_hi", [P, S], f32r), sb("hb_lo", [P, S], f32r)
        bmod, gb0 = sb("bmod", [P, 2]), sb("gb0", [P, D])
        logits, top, topi = sb("logits", [P, NT, NEX]), sb("top", [P, NT, 8]), sb("topi", [P, NT, 8], u32)
        pick = sb("pick", [P, 6, NT, NEX])
        pw = sb("pw", [P, 5, NT, 1])
        th, uu = sb("th", [P, S]), sb("uu", [P, S])
        mu = sb("mu", [P, 4, S])
        acc, x2 = sb("acc", [P, NT, D]), sb("x2", [P, NT, D])
        cmod, crow, cgb = sb("cmod", [P, 2]), sb("crow", [P, 3, D]), sb("cgb", [P, D])
        b1, b2 = sb("b1", [P, FCH]), sb("b2", [P, D])
        w1, w2 = sb("w1", [P, FCH * P]), sb("w2", [P, FCH, D])
        xcn, hc = sb("xcn", [P, NT, D]), sb("hc", [P, NT, D])
        nt = xcn[:, :, :].rearrange("p t d -> p (t d)")
        n_hi, n_lo = sb("n_hi", [P, S], f32r), sb("n_lo", [P, S], f32r)
        qz, qt = sb("qz", [P, 2, QK]), sb("qt", [P, 2, QK])
        sil = [z[:, :, :].rearrange("p n c -> p (n c)") for z in (qz, qt)]
        kq = sb("kq", [P, 2, NT, QK])
        gl = kq[:, :, :, :].rearrange("p a t n -> p (a t n)").rearrange("p (c s) -> p c s", c=FCH)
        vg = sb("vg", [P, 2, S])
        cst = sb("cst", [P, 5, 2])
        wos = sb("wos", [P, 2, D])
        tc, x3, yout = xcn, hc, hc
        uz, u2, ut = sb("uz", [P, S]), sb("u2", [P, S]), sb("ut", [P, S])
        hth, hz = ut, u2
        ea = ut[:, :].rearrange("p (n c) -> p n c", n=2)
        stats = {n: sb(f"stats_{n}", [P, NT, 6]) for n in "pbc"}
        mv = {n: sb(f"mv_{n}", [P, NT, 2]) for n in "pbc"}
        rstd = {n: sb(f"rstd_{n}", [P, NT]) for n in "pbc"}

        sm = bank("scores_for_max")
        se = [bank("scores0"), bank("scores1")]
        pv = bank("weighted_values")
        w0p, w1p = bank("expert_gate"), bank("expert_up")
        m0, m1 = bank("shared_ab"), bank("shared_pc")

        s_c = ctx.enter_context(nc.semaphore("constants_loaded"))
        s_sx = ctx.enter_context(nc.semaphore("setup_pe"))
        s_sv = ctx.enter_context(nc.semaphore("setup_vector"))
        s_sa = ctx.enter_context(nc.semaphore("setup_scalar"))
        s_sg = ctx.enter_context(nc.semaphore("setup_gpsimd"))
        s_md = ctx.enter_context(nc.semaphore("mod_stored"))
        s_ones = ctx.enter_context(nc.semaphore("ones_rows_loaded"))

        raw0 = probs[:, :, :, :].rearrange("p a g s -> p (a g s)")[:, 0:2048]
        raw1 = probs[:, :, :, :].rearrange("p a g s -> p (a g s)")[:, 2048:4096]
        raw_qkv = x1
        raw_h = otok[:, :, :].rearrange("p t d -> p (t d)")
        rawc = [acc[:, 0, 0:NB], acc[:, 1, 0:NB]]
        tanc = [acc[:, 2, 0:NB], acc[:, 3, 0:NB]]
        silc = [acc[:, 0, 64:64 + NB], acc[:, 1, 64:64 + NB]]
        wmod = [kq[:, 0, :, :].rearrange("p t n -> p (t n)")[:, 0:6 * D],
                kq[:, 1, :, :].rearrange("p t n -> p (t n)")[:, 0:6 * D]]
        mu_f = mu[:, :, :].rearrange("p a s -> p (a s)")
        modr = [mu_f[0:NB, L * 2 * S:L * 2 * S + 6 * D] for L in range(2)]
        modt = [uu[0:NB, 0:2 * D], th[0:NB, 0:2 * D]]
        wqT, w2T = x2, hc

        x_d = a["L0_attn_x"].rearrange("b (t p) d -> b p t d", p=P)
        out_d = out.rearrange("b (t p) d -> b p t d", p=P)

        block = ctx.enter_context(nc.Block())

        def walk(eng, do):
            def iteration(i, live):
                at = {s: i - LAG[s] for s in live}
                for stage, step, args in ORDER:
                    if stage in live and (stage, step) in do:
                        do[stage, step](at[stage], *args)

            def alive(i):
                return [s for s in LAG if 0 <= i - LAG[s] < NB]

            first = max(LAG.values()) + 1
            last = NB + min(LAG.values())
            for i in range(min(LAG.values()), first):
                iteration(i, alive(i))
            with eng.Fori(first, last) as i:
                iteration(i, list(LAG))
            for i in range(last, NB + max(LAG.values())):
                iteration(i, alive(i))

        def bank_waits(uses, b, stage, step, *args):
            waits = []
            seq = [(s, n, g) for s, n, g in ORDER if (s, n) in uses]
            at = seq.index((stage, step, args))
            i = b + LAG[stage]
            before = seq[:at]
            if not isinstance(i, int):
                live = [before[-1]] if before else []
            else:
                live = [u for u in before if 0 <= i - LAG[u[0]] < NB][-1:]
            for s, n, g in live:
                name, count = uses[s, n]
                waits.append((name, i - LAG[s], count(*g)))
            if not live:
                for s in {u[0] for u in seq}:
                    prior = [u for u in seq if u[0] == s][-1]
                    name, count = uses[s, prior[1]]
                    pb = i - 1 - LAG[s]
                    if isinstance(pb, int) and not 0 <= pb < NB:
                        if pb < 0:
                            continue
                        pb = NB - 1
                    waits.append((name, pb, count(*prior[2])))
            return waits

        def bank_free(eng, uses, b, stage, step, *args):
            for wait in bank_waits(uses, b, stage, step, *args):
                after(eng, *wait)

        def mm3(out_ap, w_hi, w_lo, x_hi, x_lo):
            nc.tensor.matmul(out_ap, w_lo, x_hi, start=True, stop=False)
            nc.tensor.matmul(out_ap, w_hi, x_lo, start=False, stop=False)
            return nc.tensor.matmul(out_ap, w_hi, x_hi, start=False, stop=True)

        def as_f32(ap):
            return ap.bitcast(f32)


        @block.sync
        def _(sp):
            count = [0]

            def const(dst, src, **kw):
                sp.dma_start(dst, src, **kw).then_inc(s_c, 16)
                count[0] += 1

            for L in range(2):
                with nc.allow_non_contiguous_dma("column forms of small vectors"):
                    const(rawc[L], a[f"L{L}_c"].rearrange("b d -> d b"), allow_slow_non_contiguous=True)
                const(wmod[L], a[f"L{L}_wmod"])
            const(ident[:, :], a["ident"])
            rows = a["L0_attn_w_qkv"].rearrange("(h c d) i -> c h d i", c=3, d=HD)
            for c in range(3):
                const(raw_qkv[:, c, :], rows[c])
            const(raw_qkv[:, 3, :], a["L0_attn_w_out"])
            const(cosT[:, :], a["cosT"])
            const(sinT[:, :], a["sinT"])
            const(nhalf[:, :], a["nhalf"])
            const(iota8[:, :], a["iota8"])
            const(raw0.rearrange("p (e h) -> p e h", e=NEX), a["L0_ffn_w0_kernel"].rearrange("e p h -> p e h"))
            const(raw1.rearrange("p (e h) -> p e h", e=NEX), a["L0_ffn_w1_kernel"].rearrange("e p h -> p e h"))
            const(eo[:, :, :, :], a["L0_ffn_wo_kernel"].rearrange("e (f p) d -> p e f d", p=P))
            const(gate_w[:, :], a["L0_ffn_gate_kernel"])
            const(raw_h, a["L1_attn_W_hidden"])
            const(wqk[:, :], a["L1_attn_W_qk"])
            const(bh[:, :], a["L1_attn_b_hidden"].rearrange("(c p) -> p c", p=P), allow_slow_non_contiguous=True)
            row = lambda name: a[name].rearrange("(o n) -> o n", o=1)
            const(bqk[:, :], row("L1_attn_b_qk").to_broadcast([P, QK]))
            for n in range(2):
                const(gam[:, n, :], a["L1_attn_os_gamma"][n:n + 1, :].to_broadcast([P, QK]))
                const(bet[:, n, :], a["L1_attn_os_beta"][n:n + 1, :].to_broadcast([P, QK]))
            const(ln_gb[:, 0:1], a["L1_attn_ln_g"].rearrange("(p o) -> p o", o=1))
            const(ln_gb[:, 1:2], a["L1_attn_ln_b"].rearrange("(p o) -> p o", o=1))
            const(wout[:, :, :], a["L1_attn_W_out"].rearrange("(c p) d -> p c d", p=P))
            const(bout[:, :], row("L1_attn_b_out").to_broadcast([P, D]))
            assert count[0] == N_CONST, count[0]
            sp.wait_ge(s_sv, SV_ONES)
            for n in range(PARTS):
                sp.dma_start(ks[STACK + n:STACK + n + 1, :, :], parts[0:HEADS, n, :]).then_inc(s_ones, 16)
            for L in range(2):
                sp.wait_ge(s_sv, SV_MOD[L])
                sp.dma_start(mod_d[L], modr[L]).then_inc(s_md, 16)
            sp.wait_ge(s_md, 32)
            sp.wait_ge(s_sv, SV_END)
            sp.wait_ge(s_sa, SA_END)
            sp.wait_ge(s_sg, SG_END)
            sp.wait_ge(s_sx, SX_END)

            def mod_cols(L, b, n):
                return mod_d[L, b, n * D:(n + 2) * D].rearrange("(n d) -> d n", d=D)

            def mod_row(L, b, n):
                return mod_d[L, b, n * D:(n + 1) * D].rearrange("(o d) -> o d", o=1).to_broadcast([P, D])

            def p_load(b):
                after_all(sp, ("p_xn", b - 1, 1))
                sp.dma_start(xp[:, :, :], x_d[b]).then_inc(sig["p_in"], 16)
                after_all(sp, ("p_hT", b - 1, 1))
                sp.dma_start(pmod[:, :], mod_cols(0, b, 0), allow_slow_non_contiguous=True)\
                    .then_inc(sig["p_in"], 16)

            def p_store(b, which):
                after_all(sp, ("p_part2", b, which + 1))
                if which == 1:
                    for n in range(PARTS):
                        sp.dma_start(parts_d[1].rearrange("h d a b s -> (h d) a b s")[:, :, n, :],
                                     parts[:, :, :]).then_inc(sig["p_stored1"], 16)
                    return
                after_all(sp, *((f"p_stack{g}", b - 1, 32) for g in range(GROUPS)))
                sp.dma_start(parts_d[0].rearrange("h d a b s -> (h d) a b s"),
                             parts[:, :, :].unsqueeze(1).to_broadcast([P, PARTS, PARTS, S]))\
                    .then_inc(sig["p_stored0"], 16)

            def p_stack(b, g):
                after_all(sp, ("p_stored0", b, 16), ("p_stored1", b, 16 * PARTS), ("a_sef", b - 1, 16 * (g + 1)))
                for n, dst in enumerate((qs, ks)):
                    sp.dma_start(dst[0:STACK, GH * g:GH * (g + 1), :],
                                 parts_d[n, GH * g:GH * (g + 1)].rearrange("h d a b s -> (d a b) h s"))\
                        .then_inc(sig[f"p_stack{g}"], 16)

            def a_load(b):
                after_all(sp, ("a_wog", b - 1, 1))
                sp.dma_start(ga[:, :], mod_row(0, b, 2)).then_inc(sig["a_in"], 16)

            def mrow_out(b, g):
                after_all(sp, ("a_mrow", b, g + 1))
                for n in range(PARTS):
                    sp.dma_start(qs[STACK + n:STACK + n + 1, GH * g:GH * (g + 1), :]
                                 .rearrange("o h (t s) -> o (h t) s", s=P),
                                 mrow[16 * n:16 * n + 16, :]).then_inc(sig["a_row"], 16)

            def b_load(b):
                after_all(sp, ("b_hT", b - 1, 1))
                sp.dma_start(bmod[:, :], mod_cols(0, b, 3), allow_slow_non_contiguous=True)\
                    .then_inc(sig["b_in"], 16)
                after_all(sp, ("b_x2", b - 1, 1))
                sp.dma_start(x1[:, :, :], x_d[b]).then_inc(sig["a_xin"], 16)
                sp.dma_start(gb0[:, :], mod_row(0, b, 5)).then_inc(sig["b_in"], 16)

            def c_load(b):
                after_all(sp, ("c_out", b - 1, 1))
                sp.dma_start(crow[:, :, :].rearrange("p n d -> p (n d)"), mod_d[1, b, 0:3 * D]
                             .rearrange("(o d) -> o d", o=1).to_broadcast([P, 3 * D])).then_inc(sig["c_in"], 16)
                sp.dma_start(cgb[:, :], mod_row(1, b, 5)).then_inc(sig["c_in"], 16)
                sp.dma_start(cmod[:, :], mod_cols(1, b, 3), allow_slow_non_contiguous=True)\
                    .then_inc(sig["c_in"], 16)
                sp.dma_start(b1[:, :], a["L1_ffn_b1"][b].rearrange("(c p) -> p c", p=P),
                             allow_slow_non_contiguous=True).then_inc(sig["c_in"], 16)
                sp.dma_start(b2[:, :], a["L1_ffn_b2"][b].rearrange("(o d) -> o d", o=1).to_broadcast([P, D]))\
                    .then_inc(sig["c_in"], 16)
                sp.dma_start(w1[:, :], a["L1_ffn_w1"][b]).then_inc(sig["c_in"], 16)
                sp.dma_start(w2[:, :, :], a["L1_ffn_w2"][b].rearrange("(c p) d -> p c d", p=P))\
                    .then_inc(sig["c_in"], 16)

            def c_outp(b):
                after_all(sp, ("c_out", b, 1))
                sp.dma_start(out_d[b], yout[:, :, :]).then_inc(sig["c_stored"], 16)

            walk(sp, {("P", "load"): p_load, ("P", "store"): p_store, ("P", "stack"): p_stack,
                      ("P", "mrow"): mrow_out, ("A", "load"): a_load, ("A", "mrow"): mrow_out,
                      ("B", "load"): b_load, ("C", "load"): c_load, ("C", "outp"): c_outp})
            sp.wait_ge(sig["c_stored"], 16 * NB)

        @block.tensor
        def _(pe):
            pe.wait_ge(s_c, 16 * N_CONST)
            for n in range(4):
                last = nc.tensor.transpose(m0[:, n * P:(n + 1) * P], raw_qkv[:, n, :], ident[:, :])
            last.then_inc(s_sx, 1)
            pe.wait_ge(s_sv, SV_SILU)
            for L in range(2):
                for half in range(2):
                    dst = (w0p, w1p, se[0], se[1])[2 * L + half]
                    last = nc.tensor.matmul(dst[0:NB, 0:3 * D], silc[L], wmod[L][:, half * 3 * D:(half + 1) * 3 * D],
                                            start=True, stop=True)
            last.then_inc(s_sx, 1)
            pe.wait_ge(s_sv, SV_END)
            pe.wait_ge(s_sa, SA_END)
            pe.wait_ge(s_sg, SG_END)
            pe.wait_ge(s_ones, 16 * PARTS)

            def transposes(bank_ap, src, name, wait, uses, *step):
                def run(b, *g):
                    after(pe, wait[0], b, wait[1] + (g[0] if g else 0))
                    bank_free(pe, uses, b, *step, *g)
                    for t in range(NT):
                        last = nc.tensor.transpose(bank_ap[:, t * P:(t + 1) * P], src[:, t, :], ident[:, :])
                    last.then_inc(sig[name], 1)
                return run

            p_xT = transposes(m1, xpn, "p_xT", ("p_xn", 1), M1_USES, "P", "xT")
            b_xT = transposes(m0, xbn, "b_xT", ("b_xn", 1), M0_USES, "B", "xT")
            c_xT = transposes(m1, xcn, "c_xT", ("c_xn2", 1), M1_USES, "C", "xT")
            c_xT3 = transposes(m1, xcn, "c_xT3", ("c_xn3", 1), M1_USES, "C", "xT3")
            oT_t = transposes(m0, otok, "a_oT", ("a_o", GROUPS), M0_USES, "B", "oT")
            pvs4 = pvs[:, :].rearrange("p (t q) -> p t q", t=NT)

            def proj(b, n):
                after(pe, "p_lo", b, 1)
                bank_free(pe, M1_USES, b, "P", "proj", n)
                mm3(m1[:, :], wp_hi[:, n, :], wp_lo[:, n, :], hp_hi[:, :], hp_lo[:, :]).then_inc(sig["p_proj"], 1)

            def v(b):
                bank_free(pe, M1_USES, b, "P", "v")
                for t in range(NT):
                    at = slice(t * P, (t + 1) * P)
                    last = mm3(m1[:, at], hp_hi[:, at], hp_lo[:, at], wp_hi[:, 4, :], wp_lo[:, 4, :])
                last.then_inc(sig["p_v"], 1)

            def smax(b, g, n):
                h, t = GH * g + n // NT, n % NT
                if n == 0:
                    after(pe, f"p_stack{g}", b, 32)
                after(pe, "a_max", b, 16 * g + n)
                nc.tensor.matmul(sm[:, :], qs[0:STACK, h, t * P:(t + 1) * P], ks[0:STACK, h, :],
                                 start=True, stop=True).then_inc(sig["a_smf"], 1)

            def mT(stage):
                def run(b, g):
                    after_all(pe, ("a_mp", b, 4 * (g + 1)), *bank_waits(M0_USES, b, stage, "mT", g))
                    nc.tensor.transpose(m0[0:PARTS * 16, 0:P // 2].bitcast(bf16),
                                        mpart[:, :, :].rearrange("p n c -> p (n c)"),
                                        identb[:, :]).then_inc(sig["a_mT"], 1)
                return run

            def sexp(b, g, kt, j):
                n = 16 * g + 4 * kt + j
                if n % 16 == 0:
                    after(pe, "a_row", b, 16 * PARTS * (g + 1))
                after(pe, "a_exp", b, max(n - 1, 0))
                h = GH * g + j
                nc.tensor.matmul(se[n % 2][:, :], ks[:, h, kt * P:(kt + 1) * P], qs[:, h, :],
                                 start=True, stop=True).then_inc(sig["a_sef"], 1)

            def pvm(b, g, kt):
                if kt == 0:
                    after(pe, "a_pvs", b, g)
                    after(pe, "a_vc", b, 1)
                after(pe, "a_exp", b, 16 * g + 4 * kt + 4)
                for j in range(GH):
                    last = nc.tensor.matmul(pv[32 * j:32 * j + 32, :], vaug[:, kt, GH * g + j, :],
                                            probs[:, kt % 2, j, :], start=(kt == 0), stop=(kt == NT - 1))
                last.then_inc(sig["a_pv"], 1)

            def pvT(stage, step):
                def run(b, *g):
                    n = g[0] if g else GROUPS - 1
                    after(pe, "a_pvs", b, n + 1)
                    bank_free(pe, M0_USES, b, stage, step, *g)
                    for t in range(NT):
                        last = nc.tensor.transpose(m0[:, t * P:(t + 1) * P], pvs4[:, t, :], ident[:, :])
                    last.then_inc(sig["a_pvT"], 1)
                return run

            def y(b):
                after(pe, "a_ot", b, 1)
                after(pe, "a_wog", b, 1)
                bank_free(pe, M0_USES, b, "B", "y")
                for t in range(NT):
                    at = slice(t * P, (t + 1) * P)
                    last = nc.tensor.matmul(m0[:, at], oT[:, at], wog[:, :], start=True, stop=True)
                last.then_inc(sig["a_y"], 1)

            def gate(b):
                after(pe, "b_hT", b, 1)
                bank_free(pe, M0_USES, b, "B", "gate")
                for t in range(NT):
                    last = nc.tensor.matmul(m0[:, t * NEX:(t + 1) * NEX], hb[:, t * P:(t + 1) * P], gate_w[:, :],
                                            start=True, stop=True)
                last.then_inc(sig["b_gate"], 1)

            def unit(b, u):
                if u == 0:
                    after(pe, "b_lo", b, 1)
                at = slice(u * P, (u + 1) * P)
                after(pe, "b_u", b, u)
                mm3(w0p[:, :], e0_hi[:, at], e0_lo[:, at], hb_hi[:, :], hb_lo[:, :]).then_inc(sig["b_w0"], 1)
                after(pe, "b_mu", b, u)
                mm3(w1p[:, :], e1_hi[:, at], e1_lo[:, at], hb_hi[:, :], hb_lo[:, :]).then_inc(sig["b_w1"], 1)

            def down(b, e):
                after(pe, "b_mu", b, 2 * e + 2)
                bank_free(pe, M0_USES, b, "B", "down", e)
                for t in range(NT):
                    at = slice(t * P, (t + 1) * P)
                    for f in range(HALVES):
                        last = nc.tensor.matmul(m0[:, at], mu[:, (2 * e + f) % 4, at], eo[:, e, f, :],
                                                start=(f == 0), stop=(f == HALVES - 1))
                last.then_inc(sig["b_down"], 1)

            def qk(b, p):
                after(pe, "c_nT", b, 1)
                bank_free(pe, M1_USES, b, "C", "qk", p)
                for n in range(2):
                    at = slice((2 * p + n) * P, (2 * p + n + 1) * P)
                    last = nc.tensor.matmul(m1[:, n * QK:(n + 1) * QK], nt[:, at], wqk[:, :], start=True, stop=True)
                last.then_inc(sig["c_qk"], 1)

            def hid(b, c):
                after(pe, "c_lo", b, 1)
                bank_free(pe, M1_USES, b, "C", "hid", c)
                at = slice(c * P, (c + 1) * P)
                mm3(m1[:, :], wh_hi[:, at], wh_lo[:, at], n_hi[:, :], n_lo[:, :]).then_inc(sig["c_hp"], 1)

            def sim(b):
                after(pe, "c_kq", b, 2)
                bank_free(pe, M1_USES, b, "C", "sim")
                for n in range(2):
                    for t in range(NT):
                        last = nc.tensor.matmul(m1[:, n * QK:(n + 1) * QK], kq[:, 0, t, n * P:(n + 1) * P],
                                                kq[:, 1, t, :], start=(t == 0), stop=(t == NT - 1))
                last.then_inc(sig["c_sim"], 1)

            def c_out(b):
                after(pe, "c_vg", b, 2)
                after(pe, "c_wo", b, 1)
                bank_free(pe, M1_USES, b, "C", "out")
                for t in range(NT):
                    at = slice(t * P, (t + 1) * P)
                    for n in range(2):
                        last = nc.tensor.matmul(m1[:, at], vg[:, n, at], wos[:, n, :], start=(n == 0), stop=(n == 1))
                last.then_inc(sig["c_o"], 1)

            def up(b, c):
                if c == 0:
                    after(pe, "c_nT3", b, 1)
                    after(pe, "c_in", b, 112)
                bank_free(pe, M1_USES, b, "C", "up", c)
                at = slice(c * P, (c + 1) * P)
                nc.tensor.matmul(m1[:, :], w1[:, at], nt, start=True, stop=True).then_inc(sig["c_up"], 1)

            def dn(b):
                after(pe, "c_gl", b, FCH)
                bank_free(pe, M1_USES, b, "C", "dn")
                for t in range(NT):
                    at = slice(t * P, (t + 1) * P)
                    for c in range(FCH):
                        last = nc.tensor.matmul(m1[:, at], gl[:, c, at], w2[:, c, :], start=(c == 0),
                                                stop=(c == FCH - 1))
                last.then_inc(sig["c_dn"], 1)

            walk(pe, {("P", "xT"): p_xT, ("P", "proj"): proj, ("P", "v"): v, ("P", "max"): smax, ("P", "mT"): mT("P"),
                      ("A", "max"): smax, ("A", "mT"): mT("A"), ("A", "exp"): sexp, ("A", "pv"): pvm,
                      ("A", "pvT"): pvT("A", "pvT"), ("B", "pvlast"): lambda b: pvm(b, GROUPS - 1, NT - 1),
                      ("B", "pvT3"): pvT("B", "pvT3"), ("B", "oT"): oT_t, ("B", "y"): y, ("B", "xT"): b_xT,
                      ("B", "gate"): gate, ("B", "unit"): unit, ("B", "down"): down, ("C", "xT"): c_xT,
                      ("C", "qk"): qk, ("C", "hid"): hid, ("C", "sim"): sim, ("C", "out"): c_out,
                      ("C", "xT3"): c_xT3, ("C", "up"): up, ("C", "dn"): dn})

        @block.scalar
        def _(act):
            act.wait_ge(s_c, 16 * N_CONST)
            for L in range(2):
                nc.scalar.activation(tanc[L], rawc[L], ACT.Tanh, scale=0.5).then_inc(s_sa, 1)
            nc.scalar.activation(e0_hi[:, :], raw0, ACT.Copy).then_inc(s_sa, 1)
            nc.scalar.activation(e1_hi[:, :], raw1, ACT.Copy).then_inc(s_sa, 1)
            nc.scalar.activation(wh_hi[:, :], raw_h, ACT.Copy).then_inc(s_sa, 1)
            nc.scalar.activation(bhh[:, :], bh[:, :], ACT.Copy, scale=0.5).then_inc(s_sa, 1)
            for n in range(2):
                nc.scalar.activation(gam[:, n, :], gam[:, n, :], ACT.Copy, scale=0.5).then_inc(s_sa, 1)
            act.wait_ge(s_sv, SV_END)
            act.wait_ge(s_sg, SG_END)
            act.wait_ge(s_sx, SX_END)

            def copy_in(name, src, dst, wait, free):
                def run(b):
                    after(act, wait, b, 1)
                    after(act, free, b - 1, 1)
                    nc.scalar.activation(dst, src, ACT.Copy).then_inc(sig[name], 1)
                return run

            def modulate(name, src, dst, mod, wait, free):
                shift, scale = mod
                def run(b):
                    after(act, wait, b, 1)
                    after(act, *free(b))
                    nc.scalar.activation(dst, src, ACT.Identity, bias=shift, scale=scale).then_inc(sig[name], 1)
                return run

            def mrow_in(b, g):
                after(act, "a_mT", b, g + 1)
                after(act, "a_row", b, 16 * PARTS * g)
                nc.scalar.activation(mrow[:, :], m0[0:PARTS * 16, 0:P // 2].bitcast(bf16), ACT.Copy)\
                    .then_inc(sig["a_mrow"], 1)

            def exp(b, g, kt, j):
                n = 16 * g + 4 * kt + j
                after(act, "a_sef", b, n + 1)
                if j == 0:
                    after(act, "a_pv", b, max(4 * g + kt - 1, 0))
                nc.scalar.activation(probs[:, kt % 2, j, :], se[n % 2][:, :], ACT.Exp).then_inc(sig["a_exp"], 1)

            def pvcopy(b, g=GROUPS - 1):
                after(act, "a_pv", b, NT * (g + 1))
                after(act, "a_pvT", b, g)
                nc.scalar.activation(pvs[:, :], pv[:, :], ACT.Copy).then_inc(sig["a_pvs"], 1)

            def vcopy_out(b):
                after(act, "p_v", b, 1)
                after(act, "a_vc", b - 1, 1)
                nc.scalar.activation(vtok[:, :, :].rearrange("p t d -> p (t d)"), m1[:, :], ACT.Copy)\
                    .then_inc(sig["p_vn"], 1)

            def route(b):
                after(act, "b_dif", b, 1)
                nc.scalar.activation(pw[:, 1, :, :], pw[:, 0, :, :], ACT.Exp).then_inc(sig["b_e2"], 1)

            def unit(b, u):
                after(act, "b_w0", b, u + 1)
                after(act, "b_u", b, u)
                nc.scalar.activation(th[:, :], w0p[:, :], ACT.Tanh, scale=0.5).then_inc(sig["b_tanh"], 1)

            def qkt(b, p):
                after(act, "c_qz", b, p + 1)
                after(act, "c_qs", b, p)
                nc.scalar.activation(qt[:, :, :], qz[:, :, :], ACT.Tanh, scale=0.5).then_inc(sig["c_qt"], 1)

            def hid(b, c):
                n = (0, 2, 1, 3).index(c)
                after(act, "c_hp", b, n + 1)
                after(act, "c_hs", b, n)
                if n == 0:
                    after(act, "c_gl", b - 1, FCH)
                nc.scalar.activation(hth[:, :], m1[:, :], ACT.Tanh, scale=0.5, bias=bhh[:, c:c + 1])\
                    .then_inc(sig["c_ht"], 1)
                nc.scalar.activation(hz[:, :], m1[:, :], ACT.Identity, bias=bh[:, c:c + 1]).then_inc(sig["c_hz"], 1)

            def simexp(b):
                after(act, "c_nms", b, 1)
                after(act, "c_hs", b, HCH)
                for n in range(2):
                    nc.scalar.activation(ea[:, n, :], m1[:, n * QK:(n + 1) * QK], ACT.Exp, scale=1.0 / S,
                                         bias=cst[:, 1, n:n + 1], accum_out=cst[:, 2, n:n + 1])\
                        .then_inc(sig["c_ea"], 1)

            def up(b, c):
                after(act, "c_up", b, c + 1)
                after(act, "c_gl", b, c)
                nc.scalar.activation(uz[:, :], m1[:, :], ACT.Identity, bias=b1[:, c:c + 1]).then_inc(sig["c_uz"], 1)
                nc.scalar.activation(u2[:, :], m1[:, :], ACT.Square, bias=b1[:, c:c + 1]).then_inc(sig["c_u2"], 1)

            def upg(b, c):
                after(act, "c_ub", b, c + 1)
                after(act, "c_wo", b, 1)
                nc.scalar.activation(ut[:, :], u2[:, :], ACT.Tanh, scale=GELU_C).then_inc(sig["c_ut"], 1)

            walk(act, {
                ("P", "hT"): modulate("p_hT", m1[:, :], hp, (pmod[:, 0:1], pmod[:, 1:2]), "p_xT",
                                      lambda b: ("p_in", b, 32)),
                ("P", "v"): vcopy_out, ("P", "mrow"): mrow_in, ("A", "mrow"): mrow_in, ("A", "exp"): exp,
                ("A", "pvs"): pvcopy, ("B", "pvs3"): pvcopy,
                ("B", "ot"): copy_in("a_ot", m0[:, :], oT[:, :], "a_oT", "a_y"),
                ("B", "hT"): modulate("b_hT", m0[:, :], hb, (bmod[:, 0:1], bmod[:, 1:2]), "b_xT",
                                      lambda b: ("b_in", b, 32)),
                ("B", "route"): route, ("B", "unit"): unit,
                ("C", "nT"): modulate("c_nT", m1[:, :], nt, (ln_gb[:, 1:2], ln_gb[:, 0:1]), "c_xT",
                                      lambda b: ("c_xT", b, 1)),
                ("C", "nT3"): modulate("c_nT3", m1[:, :], nt, (cmod[:, 0:1], cmod[:, 1:2]), "c_xT3",
                                       lambda b: ("c_in", b, 112)),
                ("C", "qkz"): qkt, ("C", "hid"): hid, ("C", "simexp"): simexp, ("C", "up"): up, ("C", "upg"): upg})

        @block.vector
        def _(dve):
            V = nc.vector
            done = [0]

            def link(ins):
                ins.then_inc(s_sv, 1)
                done[0] += 1
                dve.wait_ge(s_sv, done[0])

            link(V.memset(vaug[:, :, :, :], 0.0))
            link(V.memset(vaug[:, :, :, HD:HD + 1], 1.0))
            link(V.memset(parts[:, :, :], 1.0))
            assert done[0] == SV_ONES
            dve.wait_ge(s_c, 16 * N_CONST)
            link(V.tensor_copy(identb[:, :], ident[:, :]))
            dve.wait_ge(s_sa, 2)
            for L in range(2):
                link(V.scalar_tensor_tensor(out=tanc[L], in0=tanc[L], scalar=1.0, in1=rawc[L], op0=ALU.add,
                                            op1=ALU.mult))
                link(V.tensor_scalar(silc[L], tanc[L], 0.5, None, ALU.mult))
            assert done[0] == SV_SILU
            dve.wait_ge(s_sx, 1)
            link(V.tensor_copy(wqT[:, :, :].rearrange("p n c -> p (n c)"), m0[:, :]))
            link(V.tensor_copy(wo0T[:, :], wqT[:, 3, :]))
            for n in range(2):
                pair = wqT[:, n, :].rearrange("p (i two) -> p i two", two=2)
                turned = w2T[:, n, :].rearrange("p (i two) -> p i two", two=2)
                link(V.tensor_scalar(turned[:, :, 0:1], pair[:, :, 1:2], -1.0, None, ALU.mult))
                link(V.tensor_copy(turned[:, :, 1:2], pair[:, :, 0:1]))
            for n, src in enumerate((wqT[:, 0, :], w2T[:, 0, :], wqT[:, 1, :], w2T[:, 1, :], wqT[:, 2, :])):
                link(V.tensor_copy(wp_hi[:, n, :], src))
                link(V.tensor_tensor(wp_lo[:, n, :], src, as_f32(wp_hi[:, n, :]), ALU.subtract))
            dve.wait_ge(s_sx, 2)
            for L in range(2):
                r, t = modr[L], modt[L]
                for half in range(2):
                    link(V.tensor_copy(r[:, half * 3 * D:(half + 1) * 3 * D],
                                       (w0p, w1p, se[0], se[1])[2 * L + half][0:NB, 0:3 * D]))
                for n in (1, 4):
                    link(V.tensor_scalar(r[:, n * D:(n + 1) * D], r[:, n * D:(n + 1) * D], 1.0, None, ALU.add))
                for n in (2, 5):
                    gt, sg = r[:, n * D:(n + 1) * D], t[:, 0:D]
                    mg = t[:, D:2 * D]
                    link(V.tensor_scalar(sg, gt, 0.0, 2.0, ALU.is_ge, ALU.mult))
                    link(V.tensor_scalar(sg, sg, -1.0, None, ALU.add))
                    link(V.tensor_scalar(mg, gt, -1.0, None, ALU.mult))
                    link(V.tensor_tensor(mg, mg, gt, ALU.max))
                    link(V.tensor_scalar(mg, mg, 0.25, None, ALU.max))
                    link(V.tensor_tensor(gt, mg, sg, ALU.mult))
                assert done[0] == SV_MOD[L], (L, done[0])
            dve.wait_ge(s_sa, SA_END)
            link(V.tensor_tensor(wh_lo[:, :], raw_h, as_f32(wh_hi[:, :]), ALU.subtract))
            link(V.tensor_tensor(e0_lo[:, :], raw0, as_f32(e0_hi[:, :]), ALU.subtract))
            assert done[0] == SV_END, done[0]
            dve.wait_ge(s_sg, SG_END)
            dve.wait_ge(s_md, 32)

            def norm_stats(key, src, wait, name):
                def run(b):
                    for w in wait:
                        after(dve, w[0], b, w[1])
                    for t in range(NT):
                        last = V.bn_stats(stats[key][:, t, :], src[:, t, :])
                    last.then_inc(sig[name + "s"], 1)
                    after_all(dve, (name + "s", b, 1))
                    for t in range(NT):
                        last = V.bn_aggr(mv[key][:, t, :], stats[key][:, t, :])
                    last.then_inc(sig[name], 1)
                return run

            def normalise(key, src, dst, wait, name, free):
                def run(b):
                    after(dve, wait, b, 1)
                    after(dve, *free(b))
                    for t in range(NT):
                        last = V.tensor_scalar(dst[:, t, :], src[:, t, :], mv[key][:, t, 0:1], rstd[key][:, t:t + 1],
                                               ALU.subtract, ALU.mult)
                    last.then_inc(sig[name], 1)
                return run

            def rot(b, n):
                kind, part = n // 2, n % 2
                after(dve, "p_proj", b, n + 1)
                after(dve, "p_sum", b, kind)
                V.tensor_tensor((rot1, rot2)[part][:, :], m1[:, :], (cosT, sinT)[part][:, :], ALU.mult)\
                    .then_inc(sig["p_rot"], 1)

            def smax(b, g, n):
                after(dve, "a_smf", b, 16 * g + n + 1)
                if n == 0:
                    after(dve, "a_mp", b, max(4 * (g - 1), 0))
                V.tensor_reduce(negmax[:, g % 2, n:n + 1], sm[:, :], AX, ALU.max, negate=True)\
                    .then_inc(sig["a_max"], 1)

            def mparts(b, g):
                nm = negmax[:, g % 2, :]
                after(dve, "a_max", b, 16 * (g + 1))
                after(dve, "a_mT", b, g)
                V.tensor_copy(mpart[:, 0, :], nm).then_inc(sig["a_mp"], 1)
                after(dve, "a_mp", b, 4 * g + 1)
                V.tensor_tensor(mrem[:, :], nm, mpart[:, 0, :], ALU.subtract).then_inc(sig["a_mp"], 1)
                after(dve, "a_mp", b, 4 * g + 2)
                V.tensor_copy(mpart[:, 1, :], mrem[:, :]).then_inc(sig["a_mp"], 1)
                after(dve, "a_mp", b, 4 * g + 3)
                V.tensor_tensor(mpart[:, 2, :], mrem[:, :], mpart[:, 1, :], ALU.subtract).then_inc(sig["a_mp"], 1)

            def onorm(b, g=GROUPS - 1):
                after(dve, "a_pvT", b, g + 1)
                got = m0[:, :].rearrange("p (t j c) -> p t j c", t=NT, j=GH)
                r = rsum[:, :].rearrange("p (t j o) -> p t j o", t=NT, j=GH)
                V.reciprocal(r, got[:, :, :, HD:HD + 1]).then_inc(sig["a_rc"], 1)
                after(dve, "a_rc", b, g + 1)
                if g == 0:
                    after(dve, "a_oT", b - 1, 1)
                V.tensor_tensor(otok[:, :, GH * HD * g:GH * HD * (g + 1)].rearrange("p t (j d) -> p t j d", j=GH),
                                got[:, :, :, 0:HD], r.to_broadcast([P, NT, GH, HD]), ALU.mult)\
                    .then_inc(sig["a_o"], 1)

            def over_t(row):
                return row.unsqueeze(1).to_broadcast([P, NT, D])

            def bank_t(b_):
                return b_[:, :].rearrange("p (t d) -> p t d", t=NT)

            def do_x1(b):
                after(dve, "a_y", b, 1)
                after(dve, "a_xin", b, 16)
                V.tensor_tensor(x1[:, :, :], bank_t(m0), x1[:, :, :], ALU.add).then_inc(sig["a_x1"], 1)

            def do_wog(b):
                after(dve, "a_in", b, 16)
                after(dve, "a_y", b - 1, 1)
                V.tensor_tensor(wog[:, :], wo0T[:, :], ga[:, :], ALU.mult).then_inc(sig["a_wog"], 1)

            def do_logits(b):
                after(dve, "b_gate", b, 1)
                V.tensor_copy(logits[:, :, :].rearrange("p t n -> p (t n)"), m0[:, 0:NT * NEX])\
                    .then_inc(sig["b_lg"], 1)

            def do_top(b):
                after_all(dve, ("b_lg", b, 1))
                for t in range(NT):
                    last = V.max(top[:, t, :], logits[:, t, :])
                last.then_inc(sig["b_tops"], 1)
                after_all(dve, ("b_tops", b, 1))
                for t in range(NT):
                    last = V.max_index(topi[:, t, :], top[:, t, :], logits[:, t, :])
                last.then_inc(sig["b_top"], 1)
                V.tensor_tensor(pw[:, 0, :, :], top[:, :, 1:2], top[:, :, 0:1], ALU.subtract)\
                    .then_inc(sig["b_dif"], 1)

            def do_weights(b):
                n = [0]

                def link_b(ins):
                    ins.then_inc(sig["b_route"], 1)
                    n[0] += 1
                    after(dve, "b_route", b, n[0])

                bc = lambda ap: ap.to_broadcast([P, NT, NEX])
                after(dve, "b_e2", b, 1)
                after(dve, "b_top", b, 1)
                after(dve, "b_acc", b - 1, NEX)
                link_b(V.tensor_scalar(pw[:, 2, :, :], pw[:, 1, :, :], 1.0, 2.0, ALU.add, ALU.mult))
                link_b(V.reciprocal(pw[:, 3, :, :], pw[:, 2, :, :]))
                V.tensor_tensor(pw[:, 4, :, :], pw[:, 3, :, :], pw[:, 1, :, :], ALU.mult)
                io = iota8[:, :].unsqueeze(1).to_broadcast([P, NT, NEX])
                link_b(V.tensor_copy(pick[:, 4, :, :], topi[:, :, :]))
                V.tensor_tensor(pick[:, 0, :, :], io, bc(pick[:, 4, :, 0:1]), ALU.is_equal)
                link_b(V.tensor_tensor(pick[:, 1, :, :], io, bc(pick[:, 4, :, 1:2]), ALU.is_equal))
                V.tensor_tensor(pick[:, 2, :, :], pick[:, 0, :, :], bc(pw[:, 3, :, :]), ALU.mult)\
                    .then_inc(sig["b_route"], 1)
                V.tensor_tensor(pick[:, 3, :, :], pick[:, 1, :, :], bc(pw[:, 4, :, :]), ALU.mult)\
                    .then_inc(sig["b_route"], 1)
                n[0] += 2
                after(dve, "b_route", b, n[0])
                link_b(V.tensor_tensor(pick[:, 5, :, :], pick[:, 2, :, :], pick[:, 3, :, :], ALU.add))

            def unit(b, u):
                after(dve, "b_tanh", b, u + 1)
                after(dve, "b_mu", b, u)
                V.scalar_tensor_tensor(out=uu[:, :], in0=th[:, :], scalar=1.0, in1=w0p[:, :],
                                       op0=ALU.add, op1=ALU.mult).then_inc(sig["b_u"], 1)
                after(dve, "b_w1", b, u + 1)
                after(dve, "b_u", b, u + 1)
                after(dve, "b_down", b, max(u // 2 - 1, 0))
                V.tensor_tensor(mu[:, u % 4, :], uu[:, :], w1p[:, :], ALU.mult).then_inc(sig["b_mu"], 1)

            def down(b, e):
                after(dve, "b_down", b, e + 1)
                if e == 0:
                    after(dve, "b_route", b, 7)
                else:
                    after(dve, "b_acc", b, e)
                for t in range(NT):
                    w, got = pick[:, 5, t, e:e + 1], m0[:, t * D:(t + 1) * D]
                    if e == 0:
                        last = V.tensor_scalar(acc[:, t, :], got, w, None, ALU.mult)
                    else:
                        last = V.scalar_tensor_tensor(out=acc[:, t, :], in0=got, scalar=w, in1=acc[:, t, :],
                                                      op0=ALU.mult, op1=ALU.add)
                last.then_inc(sig["b_acc"], 1)

            def do_x2(b):
                after(dve, "b_acc", b, NEX)
                after(dve, "b_in", b, 32)
                V.tensor_tensor(acc[:, :, :], acc[:, :, :], over_t(gb0[:, :]), ALU.mult).then_inc(sig["b_t"], 1)
                after(dve, "b_t", b, 1)
                after(dve, "c_x3", b - 1, 1)
                V.tensor_tensor(x2[:, :, :], acc[:, :, :], x1[:, :, :], ALU.add).then_inc(sig["b_x2"], 1)

            def qkz(b, p):
                after(dve, "c_qk", b, p + 1)
                after(dve, "c_qs", b, p)
                if p == 1:
                    after(dve, "c_kq", b, 1)
                V.tensor_tensor(qz[:, :, :], m1[:, :].rearrange("p (n c) -> p n c", n=2),
                                bqk[:, :].unsqueeze(1).to_broadcast([P, 2, QK]), ALU.add).then_inc(sig["c_qz"], 1)

            def qks(b, p):
                after(dve, "c_qt", b, p + 1)
                V.scalar_tensor_tensor(out=qz[:, :, :], in0=qt[:, :, :], scalar=1.0, in1=qz[:, :, :], op0=ALU.add,
                                       op1=ALU.mult).then_inc(sig["c_qs"], 1)

            def hids(b, c):
                n = (0, 2, 1, 3).index(c)
                after(dve, "c_hz", b, n + 1)
                after(dve, "c_vg", b, n // 2)
                after(dve, "c_kq", b, 2)
                V.scalar_tensor_tensor(out=sil[n % 2], in0=hth[:, :], scalar=1.0, in1=hz[:, :], op0=ALU.add,
                                       op1=ALU.mult).then_inc(sig["c_hs"], 1)
                if n % 2:
                    after(dve, "c_hs", b, n + 1)
                    after(dve, "c_o", b - 1, 1)
                    V.tensor_tensor(vg[:, n // 2, :], sil[0], sil[1], ALU.mult).then_inc(sig["c_vg"], 1)

            def simmax(b):
                after(dve, "c_sim", b, 1)
                V.tensor_reduce(cst[:, 0, :], m1[:, :].rearrange("p (n c) -> p n c", n=2), AX, ALU.max, negate=True)\
                    .then_inc(sig["c_nm"], 1)
                after(dve, "c_nm", b, 1)
                V.tensor_scalar(cst[:, 1, :], cst[:, 0, :], 1.0 / S, None, ALU.mult).then_inc(sig["c_nms"], 1)

            def simsum(b):
                after(dve, "c_ea", b, 2)
                V.reciprocal(cst[:, 3, :], cst[:, 2, :]).then_inc(sig["c_r"], 1)
                after(dve, "c_r", b, 1)
                for n in range(2):
                    last = V.tensor_scalar(ea[:, n, :], ea[:, n, :], cst[:, 3, n:n + 1], 0.0, ALU.mult, ALU.add,
                                           accum_out=cst[:, 4, n:n + 1])
                last.then_inc(sig["c_rs"], 1)
                after(dve, "c_rs", b, 1)
                after(dve, "c_o", b - 1, 1)
                for n in range(2):
                    last = V.tensor_scalar(wos[:, n, :], wout[:, n, :], cst[:, 4, n:n + 1], 0.25, ALU.mult, ALU.mult)
                last.then_inc(sig["c_wo"], 1)

            def res(b):
                after(dve, "c_o", b, 1)
                after(dve, "c_lo", b, 1)
                after(dve, "c_qk", b, 2)
                V.tensor_tensor(tc[:, :, :], bank_t(m1), over_t(bout[:, :]), ALU.add).then_inc(sig["c_o1"], 1)

            def upa(b, c):
                after(dve, "c_u2", b, c + 1)
                V.tensor_scalar(u2[:, :], u2[:, :], GELU_A, 1.0, ALU.mult, ALU.add).then_inc(sig["c_ua"], 1)

            def upg(b, c):
                after(dve, "c_ut", b, c + 1)
                V.scalar_tensor_tensor(out=gl[:, c, :], in0=ut[:, :], scalar=1.0, in1=uz[:, :], op0=ALU.add,
                                       op1=ALU.mult).then_inc(sig["c_gl"], 1)

            def fin(b):
                after(dve, "c_dn", b, 1)
                V.scalar_tensor_tensor(out=tc[:, :, :], in0=bank_t(m1), scalar=0.5, in1=over_t(b2[:, :]),
                                       op0=ALU.mult, op1=ALU.add).then_inc(sig["c_y1"], 1)

            walk(dve, {
                ("P", "stats"): norm_stats("p", xp, [("p_in", 32)], "p_mv"),
                ("P", "xn"): normalise("p", xp, xpn, "p_rstd", "p_xn", lambda b: ("p_lo", b - 1, 1)),
                ("P", "rot"): rot, ("P", "max"): smax, ("P", "mparts"): mparts,
                ("A", "max"): smax, ("A", "mparts"): mparts, ("A", "onorm"): onorm, ("B", "onorm3"): onorm,
                ("B", "x1"): do_x1, ("A", "wog"): do_wog, ("B", "stats"): norm_stats("b", x1, [("a_x1", 1)], "b_mv"),
                ("B", "xn"): normalise("b", x1, xbn, "b_rstd", "b_xn", lambda b: ("b_gate", b - 1, 1)),
                ("B", "logits"): do_logits, ("B", "top"): do_top, ("B", "weights"): do_weights,
                ("B", "unit"): unit, ("B", "down"): down, ("B", "x2"): do_x2,
                ("C", "stats"): norm_stats("c", x2, [("b_x2", 1)], "c_mv"),
                ("C", "xn"): normalise("c", x2, xcn, "c_rstd", "c_xn", lambda b: ("c_out", b - 1, 1)),
                ("C", "stats2"): norm_stats("c", hc, [("c_h", 1)], "c_mv2"),
                ("C", "xn2"): normalise("c", hc, xcn, "c_rstd2", "c_xn2", lambda b: ("c_h", b, 1)),
                ("C", "qkz"): qkz, ("C", "qks"): qks, ("C", "hids"): hids, ("C", "simmax"): simmax,
                ("C", "simsum"): simsum, ("C", "res"): res,
                ("C", "stats3"): norm_stats("c", x3, [("c_x3", 1)], "c_mv3"),
                ("C", "xn3"): normalise("c", x3, xcn, "c_rstd3", "c_xn3", lambda b: ("c_x3", b, 1)),
                ("C", "upa"): upa, ("C", "upg"): upg, ("C", "fin"): fin})

        @block.gpsimd
        def _(pool):
            G = nc.gpsimd
            pool.wait_ge(s_c, 16 * N_CONST)
            pool.wait_ge(s_sa, 4)
            G.tensor_tensor(e1_lo[:, :], raw1, as_f32(e1_hi[:, :]), ALU.subtract).then_inc(s_sg, 1)
            pool.wait_ge(s_sv, SV_END)
            pool.wait_ge(s_sa, SA_END)
            pool.wait_ge(s_sx, SX_END)

            def deviation(key, wait, eps, name):
                def run(b):
                    after_all(pool, (wait, b, 1))
                    G.tensor_scalar(rstd[key][:, :].unsqueeze(2), mv[key][:, :, 1:2], EPS, None, ALU.add)\
                        .then_inc(sig[eps], 1)
                    after(pool, eps, b, 1)
                    G.tensor_tensor(rstd[key][:, :], rstd[key][:, :], nhalf[:, :], ALU.pow).then_inc(sig[name], 1)
                return run

            def upper(src, dst, wait, name, free):
                def run(b):
                    after_all(pool, (wait(b)), (free(b)))
                    G.tensor_copy(dst[:, :], src).then_inc(sig[name], 1)
                return run

            def lower(src, hi_, dst, wait, name):
                def run(b):
                    after(pool, wait, b, 1)
                    G.tensor_tensor(dst[:, :], src, as_f32(hi_[:, :]), ALU.subtract).then_inc(sig[name], 1)
                return run

            def split(b, n):
                dst = parts
                after(pool, "p_rot", b, 2 * n + 2)
                if n == 1:
                    after(pool, "p_stored0", b, 16)
                else:
                    after(pool, "p_stored1", b - 1, 16 * PARTS)
                G.tensor_tensor(rem[:, :], rot1[:, :], rot2[:, :], ALU.add).then_inc(sig["p_sum"], 1)
                after_all(pool, ("p_sum", b, n + 1))
                G.tensor_copy(dst[:, 0, :], rem[:, :]).then_inc(sig["p_part0"], 1)
                after(pool, "p_part0", b, n + 1)
                G.tensor_tensor(rem[:, :], rem[:, :], dst[:, 0, :], ALU.subtract).then_inc(sig["p_rem"], 1)
                after_all(pool, ("p_rem", b, n + 1))
                G.tensor_copy(dst[:, 1, :], rem[:, :]).then_inc(sig["p_part1"], 1)
                after(pool, "p_part1", b, n + 1)
                G.tensor_tensor(dst[:, 2, :], rem[:, :], dst[:, 1, :], ALU.subtract).then_inc(sig["p_part2"], 1)

            def vcopy(b):
                after_all(pool, ("p_vn", b, 1), ("a_pv", b - 1, 16))
                G.tensor_copy(vaug[:, :, :, 0:HD], vtok[:, :, :].rearrange("p t (h d) -> p t h d", h=HEADS))\
                    .then_inc(sig["a_vc"], 1)

            def over_t(row):
                return row.unsqueeze(1).to_broadcast([P, NT, D])

            def mod(b):
                after(pool, "c_in", b, 112)
                after(pool, "c_xn", b, 1)
                after(pool, "c_stored", b - 1, 16)
                G.tensor_tensor(hc[:, :, :], xcn[:, :, :], over_t(crow[:, 1, :]), ALU.mult).then_inc(sig["c_m1"], 1)
                after(pool, "c_m1", b, 1)
                G.tensor_tensor(hc[:, :, :], hc[:, :, :], over_t(crow[:, 0, :]), ALU.add).then_inc(sig["c_h"], 1)

            def qkgb(b, p):
                after(pool, "c_qs", b, p + 1)
                if p == 0:
                    after(pool, "c_dn", b - 1, 1)
                at = slice(2 * p, 2 * p + 2)
                for n in range(2):
                    G.tensor_tensor(kq[:, n, at, :], qz[:, :, :], gam[:, n, :].unsqueeze(1).to_broadcast([P, 2, QK]),
                                    ALU.mult).then_inc(sig["c_g"], 1)
                after(pool, "c_g", b, 2 * p + 2)
                for n in range(2):
                    last = G.tensor_tensor(kq[:, n, at, :], kq[:, n, at, :],
                                           bet[:, n, :].unsqueeze(1).to_broadcast([P, 2, QK]), ALU.add)
                last.then_inc(sig["c_kq"], 1)

            def res(b):
                after(pool, "c_o1", b, 1)
                G.tensor_tensor(tc[:, :, :], tc[:, :, :], hc[:, :, :], ALU.add).then_inc(sig["c_res"], 1)
                after(pool, "c_res", b, 1)
                G.tensor_tensor(tc[:, :, :], tc[:, :, :], over_t(crow[:, 2, :]), ALU.mult).then_inc(sig["c_res"], 1)
                after(pool, "c_res", b, 2)
                after(pool, "b_x2", b, 1)
                G.tensor_tensor(x3[:, :, :], tc[:, :, :], x2[:, :, :], ALU.add).then_inc(sig["c_x3"], 1)

            def upa(b, c):
                after(pool, "c_ua", b, c + 1)
                after(pool, "c_uz", b, c + 1)
                G.tensor_tensor(u2[:, :], u2[:, :], uz[:, :], ALU.mult).then_inc(sig["c_ub"], 1)

            def fin(b):
                after(pool, "c_y1", b, 1)
                G.tensor_tensor(tc[:, :, :], tc[:, :, :], over_t(cgb[:, :]), ALU.mult).then_inc(sig["c_yg"], 1)
                after(pool, "c_yg", b, 1)
                G.tensor_tensor(yout[:, :, :], tc[:, :, :], x3[:, :, :], ALU.add).then_inc(sig["c_out"], 1)

            walk(pool, {
                ("P", "rstd"): deviation("p", "p_mv", "p_eps", "p_rstd"),
                ("P", "hi"): upper(hp, hp_hi, lambda b: ("p_hT", b, 1), "p_hi", lambda b: ("p_v", b - 1, 1)),
                ("P", "lo"): lower(hp, hp_hi, hp_lo, "p_hi", "p_lo"), ("P", "split"): split,
                ("A", "vcopy"): vcopy, ("B", "rstd"): deviation("b", "b_mv", "b_eps", "b_rstd"),
                ("B", "hi"): upper(hb, hb_hi, lambda b: ("b_hT", b, 1), "b_hi", lambda b: ("b_w1", b - 1, UNITS)),
                ("B", "lo"): lower(hb, hb_hi, hb_lo, "b_hi", "b_lo"),
                ("C", "rstd"): deviation("c", "c_mv", "c_eps", "c_rstd"), ("C", "mod"): mod,
                ("C", "rstd2"): deviation("c", "c_mv2", "c_eps2", "c_rstd2"),
                ("C", "hi"): upper(nt, n_hi, lambda b: ("c_nT", b, 1), "c_hi", lambda b: ("c_hp", b - 1, HCH)),
                ("C", "lo"): lower(nt, n_hi, n_lo, "c_hi", "c_lo"),
                ("C", "qkgb"): qkgb, ("C", "res"): res,
                ("C", "rstd3"): deviation("c", "c_mv3", "c_eps3", "c_rstd3"),
                ("C", "upa"): upa, ("C", "fin"): fin})


N_CONST = 29
SV_ONES = 3
SV_SILU = 8
SV_MOD = (40, 56)
SV_END = 58
SA_END = 8
SG_END = 1
SX_END = 2
PER_BATCH.update({n + "s": 1 for n in ("p_mv", "b_mv", "c_mv", "c_mv2", "c_mv3", "b_top")})

_INS = ['L0_attn_x', 'L0_attn_w_qkv', 'L0_attn_w_out', 'L0_ffn_gate_kernel', 'L0_ffn_w0_kernel', 'L0_ffn_w1_kernel',
        'L0_ffn_wo_kernel', 'L0_c', 'L0_wmod', 'L1_attn_ln_g', 'L1_attn_ln_b', 'L1_attn_W_hidden',
        'L1_attn_b_hidden', 'L1_attn_W_qk', 'L1_attn_b_qk', 'L1_attn_os_gamma', 'L1_attn_os_beta', 'L1_attn_W_out',
        'L1_attn_b_out', 'L1_ffn_w1', 'L1_ffn_b1', 'L1_ffn_w2', 'L1_ffn_b2', 'L1_c', 'L1_wmod']


def shape_constants():
    ids = np.arange(HD // 2, dtype=np.float32)
    theta = np.power(np.float32(10000.0), np.float32(2.0) * ids / np.float32(HD)).astype(np.float32)
    ang = (np.arange(S, dtype=np.float32)[:, None] / theta).astype(np.float32)
    rows = [np.repeat(f(ang).astype(np.float32), 2, axis=1).T for f in (np.cos, np.sin)]
    cosT, sinT = (np.ascontiguousarray(np.tile(r, (HEADS, 1))) for r in rows)
    return {"cosT": cosT, "sinT": sinT, "ident": np.eye(P, dtype=np.float32),
            "nhalf": np.full((P, NT), -0.5, np.float32),
            "iota8": np.tile(np.arange(NEX, dtype=np.float32), (P, 1))}


def kernel(**inputs):
    import concourse.bacc as bacc
    from concourse.bass_utils import run_bass_kernel_spmd

    nc = bacc.Bacc("TRN2", target_bir_lowering=False, num_devices=1)
    arrays, args = {}, {}
    given = {name: np.ascontiguousarray(inputs[name]) for name in _INS}
    for name, value in {**given, **shape_constants()}.items():
        arrays[f"in_{name}"] = value
        args[name] = nc.dram_tensor(f"in_{name}", value.shape, mybir.dt.from_np(value.dtype), kind="ExternalInput").ap()
    out = nc.dram_tensor("out", (NB, S, D), mybir.dt.float32, kind="ExternalOutput").ap()
    adaln_two_layers(nc, args, out)
    r = run_bass_kernel_spmd(nc, [arrays], core_ids=[0])
    return r.results[0]["out"]
```

```python
import numpy as np
import concourse.bass as bass
from concourse import mybir
from contextlib import ExitStack

NB, S, D = 8, 512, 128
P = 128
NT = S // P
HEADS, HD = 16, 8
GH = 4
GROUPS = HEADS // GH
PARTS = 3
STACK = HD * PARTS * PARTS
NEX, HID = 8, 256
HALVES = HID // P
UNITS = NEX * HALVES
QK = 256
HCH = 4
FCH = 4
EPS = 1e-5
HID_ORDER = (0, 2, 1, 3)
GELU_C, GELU_A = 0.7978845608028654, 0.044715

LAG = {"P": -1, "A": 0, "B": 1, "C": 2}

INSTANCES = {
    ("A", "exp"): [(g, kt, j) for g in range(GROUPS) for kt in range(NT) for j in range(GH)],
    ("A", "max"): [(g, n) for g in range(1, GROUPS) for n in range(16)],
    ("A", "pv"): [(g, kt) for g in range(GROUPS) for kt in range(NT)][:-1],
    ("A", "mparts"): [(g,) for g in range(1, GROUPS)],
    ("A", "mT"): [(g,) for g in range(1, GROUPS)],
    ("A", "mrow"): [(g,) for g in range(1, GROUPS)],
    ("A", "pvs"): [(g,) for g in range(GROUPS - 1)],
    ("A", "pvT"): [(g,) for g in range(GROUPS - 1)],
    ("A", "onorm"): [(g,) for g in range(GROUPS - 1)],
    ("B", "unit"): [(u,) for u in range(UNITS)],
    ("B", "down"): [(e,) for e in range(NEX)],
    ("B", "acc"): [(e,) for e in range(1, NEX)],
    ("P", "proj"): [(n,) for n in range(4)],
    ("P", "rot"): [(n,) for n in range(4)],
    ("P", "split"): [(n,) for n in range(2)],
    ("P", "store"): [(n,) for n in range(2)],
    ("P", "stack"): [(g,) for g in range(GROUPS)],
    ("P", "max"): [(0, n) for n in range(16)],
    ("P", "mparts"): [(0,)], ("P", "mT"): [(0,)], ("P", "mrow"): [(0,)],
    ("C", "qk"): [(p,) for p in range(2)],
    ("C", "qkz"): [(p,) for p in range(2)],
    ("C", "qks"): [(p,) for p in range(2)],
    ("C", "qkgb"): [(p,) for p in range(2)],
    ("C", "hid"): [(c,) for c in HID_ORDER],
    ("C", "hids"): [(c,) for c in HID_ORDER],
    ("C", "up"): [(c,) for c in range(FCH)],
    ("C", "upa"): [(c,) for c in range(FCH)],
    ("C", "upg"): [(c,) for c in range(FCH)],
}

SLOTS = {
    ("P", "load"): dict(sp=(-110.743,)),
    ("P", "stats"): dict(dve=(-0.95,)),
    ("P", "rstd"): dict(pool=(-56.758,)),
    ("P", "xn"): dict(act=(9.184,)),
    ("P", "xT"): dict(pe=(13.84,)),
    ("P", "hT"): dict(act=(14.243,)),
    ("P", "lo"): dict(pool=(26.541,)),
    ("P", "proj"): dict(pe=(27.265, 1.623)),
    ("P", "rot"): dict(dve=(27.858, 1.449)),
    ("P", "v"): dict(pe=(41.126,), act=(41.635,)),
    ("P", "split"): dict(pool=(59.586, 11.22)),
    ("P", "store"): dict(sp=(42.77, 19.64)),
    ("P", "stack"): dict(sp=(67.394, 32.228)),
    ("P", "max"): dict(pe=(46, 1.054), dve=(46.905, 1.093)),
    ("P", "mparts"): dict(dve=(118.82,)),
    ("P", "mT"): dict(pe=(114.742,)),
    ("P", "mrow"): dict(sp=(221.818,), act=(284.615,)),
    ("A", "exp"): dict(pe=(-0.826, 1.014), act=(-1.331, 1.029)),
    ("A", "max"): dict(pe=(-4.056, 0.996), dve=(-4.315, 1.008)),
    ("A", "pv"): dict(pe=(4.038, 4.114)),
    ("A", "mparts"): dict(dve=(11.777, 16.963)),
    ("A", "mT"): dict(pe=(13.154, 16.628)),
    ("A", "mrow"): dict(sp=(-6.323, 39.827), act=(11.818, 17.202)),
    ("A", "pvs"): dict(act=(16.32, 17.943)),
    ("A", "pvT"): dict(pe=(20.572, 18.404)),
    ("A", "onorm"): dict(dve=(23.928, 17.706)),
    ("A", "load"): dict(sp=(-112.956,)),
    ("A", "vcopy"): dict(pool=(-114.449,)),
    ("A", "wog"): dict(dve=(5.56,)),
    ("B", "load"): dict(sp=(-71.512,)),
    ("B", "pvlast"): dict(pe=(-72.786,)),
    ("B", "pvs3"): dict(act=(-69.816,)),
    ("B", "pvT3"): dict(pe=(-21.556,)),
    ("B", "onorm3"): dict(dve=(-2.594,)),
    ("B", "oT"): dict(pe=(2.2,)),
    ("B", "ot"): dict(act=(0.741,)),
    ("B", "y"): dict(pe=(3.308,)),
    ("B", "x1"): dict(dve=(4.041,)),
    ("B", "stats"): dict(dve=(5.821,)),
    ("B", "rstd"): dict(pool=(-23.41,)),
    ("B", "xn"): dict(act=(7.594,)),
    ("B", "xT"): dict(pe=(10.018,)),
    ("B", "hT"): dict(act=(10.921,)),
    ("B", "lo"): dict(pool=(16.618,)),
    ("B", "gate"): dict(pe=(14.558,)),
    ("B", "logits"): dict(dve=(17.35,)),
    ("B", "top"): dict(dve=(18.239,)),
    ("B", "route"): dict(act=(19.31,)),
    ("B", "weights"): dict(dve=(24.802,)),
    ("B", "unit"): dict(pe=(18.098, 2.827), act=(17.962, 2.841), dve=(19.61, 2.869)),
    ("B", "down"): dict(pe=(25.479, 5.531), act=(27.839, 5.457)),
    ("B", "acc"): dict(pool=(61.78, 13.795)),
    ("B", "x2"): dict(dve=(183.782,)),
    ("C", "load"): dict(sp=(-177.05,)),
    ("C", "stats"): dict(dve=(-187.848,)),
    ("C", "rstd"): dict(pool=(-173.838,)),
    ("C", "xn"): dict(act=(-41.505,)),
    ("C", "mod"): dict(pool=(-145.57,)),
    ("C", "stats2"): dict(dve=(0.94,)),
    ("C", "rstd2"): dict(pool=(-73.655,)),
    ("C", "xn2"): dict(act=(3.284,)),
    ("C", "xT"): dict(pe=(5.079,)),
    ("C", "nT"): dict(act=(5.804,)),
    ("C", "lo"): dict(pool=(9.72,)),
    ("C", "qk"): dict(pe=(7.676, 4.127)),
    ("C", "qkz"): dict(act=(7.201, 5.486), dve=(7.554, 4.67)),
    ("C", "qks"): dict(dve=(7.873, 6.659)),
    ("C", "qkgb"): dict(pool=(-9.437, 34.404)),
    ("C", "hid"): dict(pe=(17.274, 1.746), act=(16.851, 1.942)),
    ("C", "hids"): dict(dve=(18.614, 1.474)),
    ("C", "sim"): dict(pe=(24.186,)),
    ("C", "simmax"): dict(dve=(24.963,)),
    ("C", "simexp"): dict(act=(24.927,)),
    ("C", "simsum"): dict(dve=(30.192,)),
    ("C", "out"): dict(pe=(34.348,)),
    ("C", "res"): dict(dve=(34.676,), pool=(65.918,)),
    ("C", "stats3"): dict(dve=(40.24,)),
    ("C", "rstd3"): dict(pool=(73.766,)),
    ("C", "xn3"): dict(act=(42.419,)),
    ("C", "xT3"): dict(pe=(44.264,)),
    ("C", "nT3"): dict(act=(45.693,)),
    ("C", "up"): dict(pe=(47.327, 2.996), act=(47.027, 3.575)),
    ("C", "upa"): dict(dve=(48.456, 4.102)),
    ("C", "upg"): dict(act=(47.682, 4.565), dve=(49.62, 4.445)),
    ("C", "dn"): dict(pe=(76.084,)),
    ("C", "fin"): dict(dve=(223.571,), pool=(176.181,)),
    ("C", "outp"): dict(sp=(185.164,)),
}


def order_of(engine):
    at = []
    for (stage, step), slots in SLOTS.items():
        if engine in slots:
            first, *every = slots[engine]
            for n, args in enumerate(INSTANCES.get((stage, step), [()])):
                at.append((first + n * (every[0] if every else 0), len(at), stage, step, args))
    return [(stage, step, args) for _, _, stage, step, args in sorted(at)]


M0_USES = {
    ("A", "mT"): ("a_mrow", lambda g: g + 1), ("P", "mT"): ("a_mrow", lambda g: g + 1),
    ("A", "pvT"): ("a_o", lambda g: g + 1), ("B", "pvT3"): ("a_o", lambda: GROUPS),
    ("B", "oT"): ("a_ot", lambda: 1), ("B", "y"): ("a_x1", lambda: 1),
    ("B", "xT"): ("b_hi", lambda: 1), ("B", "gate"): ("b_lg", lambda: 1),
    ("B", "down"): ("b_sc", lambda e: e + 1),
}
M1_USES = {
    ("P", "xT"): ("p_hi", lambda: 1), ("P", "proj"): ("p_rot", lambda n: n + 1), ("P", "v"): ("p_vn", lambda: 1),
    ("C", "xT"): ("c_hi", lambda: 1), ("C", "qk"): ("c_qz", lambda p: p + 1),
    ("C", "hid"): ("c_hz", lambda c: HID_ORDER.index(c) + 1), ("C", "sim"): ("c_ea", lambda: 2),
    ("C", "out"): ("c_o1", lambda: 1), ("C", "xT3"): ("c_nT3", lambda: 1), ("C", "up"): ("c_u2", lambda c: c + 1),
    ("C", "dn"): ("c_y1", lambda: 1),
}

PER_BATCH = {
    "p_nm": 1, "b_nm": 1, "c_nm1": 1, "c_nm2": 1, "c_nm3": 1,
    "p_in": 32, "p_mv": 1, "p_eps": 2, "p_rstd": 1, "p_xn": 1, "p_xT": 1, "p_hT": 1, "p_hi": 1, "p_lo": 1,
    "p_proj": 4, "p_rot": 4, "p_v": 1, "p_vn": 1, "p_sum": 2, "p_part0": 2, "p_rem": 2, "p_part1": 2, "p_part2": 2,
    "p_stored0": 16, "p_stored1": 16 * PARTS, "p_stack0": 32, "p_stack1": 32, "p_stack2": 32, "p_stack3": 32,
    "a_in": 16, "a_xin": 16, "a_wog": 1, "a_vc": 1, "a_smf": 64, "a_max": 64, "a_mp": 4 * GROUPS, "a_mT": GROUPS, "a_mrow": GROUPS,
    "a_row": 16 * PARTS * GROUPS, "a_sef": 64, "a_exp": 64, "a_pv": 16, "a_pvs": GROUPS, "a_pvT": GROUPS,
    "a_rc": GROUPS, "a_o": GROUPS, "a_oT": 1, "a_ot": 1, "a_y": 1, "a_x1": 1,
    "b_in": 32, "b_mv": 1, "b_eps": 2, "b_rstd": 1, "b_xn": 1, "b_xT": 1, "b_hT": 1, "b_hi": 1, "b_lo": 1,
    "b_gate": 1, "b_lg": 1, "b_top": 1, "b_dif": 1, "b_e2": 1, "b_route": 7, "b_w0": UNITS, "b_w1": UNITS,
    "b_tanh": UNITS, "b_u": UNITS, "b_mu": UNITS, "b_down": NEX, "b_sc": NEX, "b_acc": NEX - 1, "b_t": 1, "b_x2": 1,
    "c_in": 16 * 7, "c_mv": 1, "c_eps": 2, "c_rstd": 1, "c_xn": 1, "c_m1": 1, "c_h": 1, "c_mv2": 1, "c_eps2": 2,
    "c_rstd2": 1, "c_xn2": 1, "c_xT": 1, "c_nT": 1, "c_hi": 1, "c_lo": 1, "c_qk": 2, "c_qz": 2, "c_qt": 2,
    "c_qs": 2, "c_g": 4, "c_kq": 2, "c_hp": 4, "c_ht": 4, "c_hz": 4, "c_hs": 4, "c_vg": 2, "c_sim": 1, "c_nm": 1,
    "c_nms": 1, "c_ea": 2, "c_r": 1, "c_rs": 1, "c_wo": 1, "c_o": 1, "c_o1": 1, "c_res": 2, "c_x3": 1,
    "c_mv3": 1, "c_eps3": 2, "c_rstd3": 1, "c_xn3": 1, "c_xT3": 1, "c_nT3": 1, "c_up": 4, "c_uz": 4, "c_u2": 4, "c_bs": 1, "c_ub": 4, "c_ut": 4, "c_gl": 4,
    "c_dn": 1, "c_y1": 1, "c_yg": 1, "c_out": 1, "c_stored": 16,
}


def adaln_two_layers(nc, a, out):
    dt = mybir.dt
    f32, f32r, bf16, u32 = dt.float32, dt.float32r, dt.bfloat16, dt.uint32
    ALU = mybir.AluOpType
    ACT = mybir.ActivationFunctionType
    AX = mybir.AxisListType.X
    ctx = ExitStack()
    with ctx:
        used = []

        def sb(name, shape, dtype=f32):
            used.append((name, int(np.prod(shape[1:])) * (2 if dtype == bf16 else 4)))
            return ctx.enter_context(nc.sbuf_tensor(name, shape, dtype))

        def bank(name):
            return ctx.enter_context(nc.psum_tensor(name, [P, 512], f32))

        sig = {name: ctx.enter_context(nc.semaphore(name)) for name in PER_BATCH}

        def after(eng, name, b, k):
            value = b * PER_BATCH[name] + k
            if isinstance(value, int) and value <= 0:
                return
            eng.wait_ge(sig[name], value)

        def after_all(eng, *waits):
            counts = [(sig[name], b * PER_BATCH[name] + k) for name, b, k in waits]
            counts = [(s, v if isinstance(v, int) else eng.to_reg(v)) for s, v in counts
                      if not isinstance(v, int) or v > 0]
            eng.wait_ge(s_c, 16 * N_CONST)
            for s, v in counts:
                eng.wait_ge(s, v)

        mod_d = nc.dram_tensor("mod_d", [2, NB, 6 * D], f32).ap()
        parts_d = nc.dram_tensor("parts_d", [2, HEADS, HD, PARTS, PARTS, S], bf16).ap()

        cosT, sinT = sb("cosT", [P, S]), sb("sinT", [P, S])
        ident, identb = sb("ident", [P, P]), sb("identb", [P, P], bf16)
        nhalf = sb("nhalf", [P, NT])
        iota8 = sb("iota8", [P, NEX])
        wp_hi, wp_lo = sb("wp_hi", [P, 5, P], f32r), sb("wp_lo", [P, 5, P], f32r)
        wo0T = sb("wo0T", [P, D])
        e0_hi, e0_lo = sb("e0_hi", [P, NEX * HID], f32r), sb("e0_lo", [P, NEX * HID], f32r)
        e1_hi, e1_lo = sb("e1_hi", [P, NEX * HID], f32r), sb("e1_lo", [P, NEX * HID], f32r)
        eo = sb("eo", [P, NEX, HALVES, D])
        gate_w = sb("gate_w", [P, NEX])
        wh_hi, wh_lo = sb("wh_hi", [P, HCH * P], f32r), sb("wh_lo", [P, HCH * P], f32r)
        wqk = sb("wqk", [P, QK])
        bh, bhh = sb("bh", [P, HCH]), sb("bhh", [P, HCH])
        bqk = sb("bqk", [P, QK])
        gam, bet = sb("gam", [P, 2, QK]), sb("bet", [P, 2, QK])
        ln_gb = sb("ln_gb", [P, 2])
        wout = sb("wout", [P, 2, D])
        bout = sb("bout", [P, D])

        xp = sb("xp", [P, NT, D])
        xpn = xp
        hp = xpn[:, :, :].rearrange("p t d -> p (t d)")
        hp_hi, hp_lo = sb("hp_hi", [P, S], f32r), sb("hp_lo", [P, S], f32r)
        pmod = sb("pmod", [P, 2])
        rot1, rot2, rem = sb("rot1", [P, S]), sb("rot2", [P, S]), sb("rem", [P, S])
        parts = sb("parts", [P, PARTS, S], bf16)
        vtok = sb("vtok", [P, NT, D])
        qs, ks = sb("qs", [STACK + PARTS, HEADS, S], bf16), sb("ks", [STACK + PARTS, HEADS, S], bf16)
        vaug = sb("vaug", [P, NT, HEADS, 32])
        probs = sb("probs", [P, 2, GH, S])
        ga, wog = sb("ga", [P, D]), sb("wog", [P, D])
        negmax, mrem = sb("negmax", [P, 2, 16]), sb("mrem", [P, 16])
        mpart = sb("mpart", [P, PARTS, 16], bf16)
        mrow = sb("mrow", [PARTS * 16, P], bf16)
        pvs, rsum, otok, x1 = sb("pvs", [P, S]), sb("rsum", [P, 16]), sb("otok", [P, NT, D]), sb("x1", [P, NT, D])
        oT = pvs
        xbn = sb("xbn", [P, NT, D])
        hb = xbn[:, :, :].rearrange("p t d -> p (t d)")
        hb_hi, hb_lo = sb("hb_hi", [P, S], f32r), sb("hb_lo", [P, S], f32r)
        bmod, gb0 = sb("bmod", [P, 2]), sb("gb0", [P, D])
        logits, top, topi = sb("logits", [P, NT, NEX]), sb("top", [P, NT, 8]), sb("topi", [P, NT, 8], u32)
        pick = sb("pick", [P, 6, NT, NEX])
        pw = sb("pw", [P, 5, NT, 1])
        th, uu = sb("th", [P, S]), sb("uu", [P, S])
        mu = sb("mu", [P, 4, S])
        acc, scaled, x2 = sb("acc", [P, NT, D]), sb("scaled", [P, NT, D]), sb("x2", [P, NT, D])
        cmod, crow, cgb = sb("cmod", [P, 2]), sb("crow", [P, 3, D]), sb("cgb", [P, D])
        b1, b1s, b2 = sb("b1", [P, FCH]), sb("b1s", [P, FCH]), sb("b2", [P, D])
        w1, w2 = sb("w1", [P, FCH * P]), sb("w2", [P, FCH, D])
        xcn, hc = sb("xcn", [P, NT, D]), sb("hc", [P, NT, D])
        nt = xcn[:, :, :].rearrange("p t d -> p (t d)")
        n_hi, n_lo = sb("n_hi", [P, S], f32r), sb("n_lo", [P, S], f32r)
        qz, qt = sb("qz", [P, 2, QK]), sb("qt", [P, 2, QK])
        sil = [z[:, :, :].rearrange("p n c -> p (n c)") for z in (qz, qt)]
        kq = sb("kq", [P, 2, NT, QK])
        gl = kq[:, :, :, :].rearrange("p a t n -> p (a t n)").rearrange("p (c s) -> p c s", c=FCH)
        vg = sb("vg", [P, 2, S])
        cst = sb("cst", [P, 5, 2])
        wos = sb("wos", [P, 2, D])
        tc, x3, yout = xcn, hc, hc
        uz, u2, ut = sb("uz", [P, S]), sb("u2", [P, S]), sb("ut", [P, S])
        hth, hz = ut, u2
        ea = ut[:, :].rearrange("p (n c) -> p n c", n=2)
        stats = {n: sb(f"stats_{n}", [P, NT, 6]) for n in "pbc"}
        mv = {n: sb(f"mv_{n}", [P, NT, 2]) for n in "pbc"}
        rstd = {n: sb(f"rstd_{n}", [P, NT]) for n in "pbc"}
        shift_n = {n: sb(f"shift_{n}", [P, NT]) for n in "pbc"}

        sm = bank("scores_for_max")
        se = [bank("scores0"), bank("scores1")]
        pv = bank("weighted_values")
        w0p, w1p = bank("expert_gate"), bank("expert_up")
        m0, m1 = bank("shared_ab"), bank("shared_pc")

        s_c = ctx.enter_context(nc.semaphore("constants_loaded"))
        s_c2 = ctx.enter_context(nc.semaphore("late_constants_loaded"))
        s_sx = ctx.enter_context(nc.semaphore("setup_pe"))
        s_sv = ctx.enter_context(nc.semaphore("setup_vector"))
        s_sa = ctx.enter_context(nc.semaphore("setup_scalar"))
        s_sg = ctx.enter_context(nc.semaphore("setup_gpsimd"))
        s_md = ctx.enter_context(nc.semaphore("mod_stored"))
        s_ones = ctx.enter_context(nc.semaphore("ones_rows_loaded"))

        raw0 = probs[:, :, :, :].rearrange("p a g s -> p (a g s)")[:, 0:2048]
        raw1 = probs[:, :, :, :].rearrange("p a g s -> p (a g s)")[:, 2048:4096]
        raw_qkv = x1
        raw_h = otok[:, :, :].rearrange("p t d -> p (t d)")
        rawc = [acc[:, 0, 0:NB], acc[:, 1, 0:NB]]
        tanc = [acc[:, 2, 0:NB], acc[:, 3, 0:NB]]
        silc = [acc[:, 0, 64:64 + NB], acc[:, 1, 64:64 + NB]]
        wmod = [kq[:, 0, :, :].rearrange("p t n -> p (t n)")[:, 0:6 * D],
                kq[:, 1, :, :].rearrange("p t n -> p (t n)")[:, 0:6 * D]]
        mu_f = mu[:, :, :].rearrange("p a s -> p (a s)")
        modr = [mu_f[0:NB, L * 2 * S:L * 2 * S + 6 * D] for L in range(2)]
        modt = [uu[0:NB, 0:2 * D], th[0:NB, 0:2 * D]]
        wqT, w2T = x2, hc

        x_d = a["L0_attn_x"].rearrange("b (t p) d -> b p t d", p=P)
        out_d = out.rearrange("b (t p) d -> b p t d", p=P)

        block = ctx.enter_context(nc.Block())

        def walk(eng, name, do, late, ready, late_at=None):
            begin = min(LAG.values())
            order = order_of(name)
            assert set(do) == {(stage, step) for stage, step, _ in order}

            def iteration(i, live):
                at = {s: i - LAG[s] for s in live}
                for stage, step, args in order:
                    if stage in live:
                        if i is begin and (stage, step) == late_at and args in ((), (0,), (0, 0)):
                            late()
                        do[stage, step](at[stage], *args)
                if i is begin:
                    if late_at is None:
                        late()
                    ready()

            def alive(i):
                return [s for s in LAG if 0 <= i - LAG[s] < NB]

            first = max(LAG.values()) + 1
            last = NB + min(LAG.values())
            for i in range(begin, first):
                iteration(i, alive(i))
            with eng.Fori(first, last) as i:
                iteration(i, list(LAG))
            for i in range(last, NB + max(LAG.values())):
                iteration(i, alive(i))

        def bank_waits(uses, b, stage, step, *args):
            waits = []
            seq = [(s, n, g) for s, n, g in order_of("pe") if (s, n) in uses]
            at = seq.index((stage, step, args))
            i = b + LAG[stage]
            before = seq[:at]
            if not isinstance(i, int):
                live = [before[-1]] if before else []
            else:
                live = [u for u in before if 0 <= i - LAG[u[0]] < NB][-1:]
            for s, n, g in live:
                name, count = uses[s, n]
                waits.append((name, i - LAG[s], count(*g)))
            if not live:
                for s in {u[0] for u in seq}:
                    prior = [u for u in seq if u[0] == s][-1]
                    name, count = uses[s, prior[1]]
                    pb = i - 1 - LAG[s]
                    if isinstance(pb, int) and not 0 <= pb < NB:
                        if pb < 0:
                            continue
                        pb = NB - 1
                    waits.append((name, pb, count(*prior[2])))
            return waits

        def bank_free(eng, uses, b, stage, step, *args):
            for wait in bank_waits(uses, b, stage, step, *args):
                after(eng, *wait)

        def nothing():
            pass

        def mm3(out_ap, w_hi, w_lo, x_hi, x_lo):
            nc.tensor.matmul(out_ap, w_lo, x_hi, start=True, stop=False)
            nc.tensor.matmul(out_ap, w_hi, x_lo, start=False, stop=False)
            return nc.tensor.matmul(out_ap, w_hi, x_hi, start=False, stop=True)

        def as_f32(ap):
            return ap.bitcast(f32)


        @block.sync
        def _(sp):
            count = [0, 0]

            def const(dst, src, late=0, **kw):
                sp.dma_start(dst, src, **kw).then_inc((s_c, s_c2)[late], 16)
                count[late] += 1

            for L in range(2):
                with nc.allow_non_contiguous_dma("column forms of small vectors"):
                    const(rawc[L], a[f"L{L}_c"].rearrange("b d -> d b"), allow_slow_non_contiguous=True)
                const(wmod[L], a[f"L{L}_wmod"])
            const(ident[:, :], a["ident"])
            rows = a["L0_attn_w_qkv"].rearrange("(h c d) i -> c h d i", c=3, d=HD)
            for c in range(3):
                const(raw_qkv[:, c, :], rows[c])
            const(raw_qkv[:, 3, :], a["L0_attn_w_out"])
            const(nhalf[:, :], a["nhalf"])
            const(cosT[:, :], a["cosT"])
            const(sinT[:, :], a["sinT"])
            assert count[0] == N_CONST, count[0]

            def late_loads():
                def const2(dst, src, **kw):
                    const(dst, src, 1, **kw)

                row = lambda name: a[name].rearrange("(o n) -> o n", o=1)
                const2(raw0.rearrange("p (e h) -> p e h", e=NEX), a["L0_ffn_w0_kernel"].rearrange("e p h -> p e h"))
                const2(raw1.rearrange("p (e h) -> p e h", e=NEX), a["L0_ffn_w1_kernel"].rearrange("e p h -> p e h"))
                const2(raw_h, a["L1_attn_W_hidden"])
                const2(bh[:, :], a["L1_attn_b_hidden"].rearrange("(c p) -> p c", p=P), allow_slow_non_contiguous=True)
                for n in range(2):
                    const2(gam[:, n, :], a["L1_attn_os_gamma"][n:n + 1, :].to_broadcast([P, QK]))
                    const2(bet[:, n, :], a["L1_attn_os_beta"][n:n + 1, :].to_broadcast([P, QK]))
                const2(iota8[:, :], a["iota8"])
                const2(gate_w[:, :], a["L0_ffn_gate_kernel"])
                const2(eo[:, :, :, :], a["L0_ffn_wo_kernel"].rearrange("e (f p) d -> p e f d", p=P))
                const2(wqk[:, :], a["L1_attn_W_qk"])
                const2(bqk[:, :], row("L1_attn_b_qk").to_broadcast([P, QK]))
                const2(ln_gb[:, 0:1], a["L1_attn_ln_g"].rearrange("(p o) -> p o", o=1))
                const2(ln_gb[:, 1:2], a["L1_attn_ln_b"].rearrange("(p o) -> p o", o=1))
                const2(wout[:, :, :], a["L1_attn_W_out"].rearrange("(c p) d -> p c d", p=P))
                const2(bout[:, :], row("L1_attn_b_out").to_broadcast([P, D]))
                assert count[1] == N_LATE, count[1]
                sp.wait_ge(s_sv, SV_ONES)
                for n in range(PARTS):
                    sp.dma_start(ks[STACK + n:STACK + n + 1, :, :], parts[0:HEADS, n, :]).then_inc(s_ones, 16)
                mod_store(0)

            def mod_store(L):
                sp.wait_ge(s_sv, SV_MOD[L])
                sp.dma_start(mod_d[L], modr[L]).then_inc(s_md, 16)
                sp.wait_ge(s_md, 16 * (L + 1))

            def late():
                mod_store(1)

            def ready():
                sp.wait_ge(s_sv, SV_END)
                sp.wait_ge(s_sa, SA_END)
                sp.wait_ge(s_sg, SG_END)
                sp.wait_ge(s_sx, SX_END)

            def mod_cols(L, b, n):
                return mod_d[L, b, n * D:(n + 2) * D].rearrange("(n d) -> d n", d=D)

            def mod_row(L, b, n):
                return mod_d[L, b, n * D:(n + 1) * D].rearrange("(o d) -> o d", o=1).to_broadcast([P, D])

            def p_load(b):
                after_all(sp, ("p_lo", b - 1, 1))
                sp.dma_start(xp[:, :, :], x_d[b]).then_inc(sig["p_in"], 16)
                if isinstance(b, int) and b == 0:
                    late_loads()
                after_all(sp, ("p_hT", b - 1, 1))
                sp.dma_start(pmod[:, :], mod_cols(0, b, 0), allow_slow_non_contiguous=True)\
                    .then_inc(sig["p_in"], 16)

            def p_store(b, which):
                after_all(sp, ("p_part2", b, which + 1))
                if which == 1:
                    for n in range(PARTS):
                        sp.dma_start(parts_d[1].rearrange("h d a b s -> (h d) a b s")[:, :, n, :],
                                     parts[:, :, :]).then_inc(sig["p_stored1"], 16)
                    return
                after_all(sp, *((f"p_stack{g}", b - 1, 32) for g in range(GROUPS)))
                sp.dma_start(parts_d[0].rearrange("h d a b s -> (h d) a b s"),
                             parts[:, :, :].unsqueeze(1).to_broadcast([P, PARTS, PARTS, S]))\
                    .then_inc(sig["p_stored0"], 16)

            def p_stack(b, g):
                after_all(sp, ("p_stored0", b, 16), ("p_stored1", b, 16 * PARTS), ("a_sef", b - 1, 16 * (g + 1)))
                for n, dst in enumerate((qs, ks)):
                    sp.dma_start(dst[0:STACK, GH * g:GH * (g + 1), :],
                                 parts_d[n, GH * g:GH * (g + 1)].rearrange("h d a b s -> (d a b) h s"))\
                        .then_inc(sig[f"p_stack{g}"], 16)

            def a_load(b):
                after_all(sp, ("a_wog", b - 1, 1))
                sp.dma_start(ga[:, :], mod_row(0, b, 2)).then_inc(sig["a_in"], 16)

            def mrow_out(b, g):
                after_all(sp, ("a_mrow", b, g + 1))
                for n in range(PARTS):
                    sp.dma_start(qs[STACK + n:STACK + n + 1, GH * g:GH * (g + 1), :]
                                 .rearrange("o h (t s) -> o (h t) s", s=P),
                                 mrow[16 * n:16 * n + 16, :]).then_inc(sig["a_row"], 16)

            def b_load(b):
                after_all(sp, ("b_hT", b - 1, 1))
                sp.dma_start(bmod[:, :], mod_cols(0, b, 3), allow_slow_non_contiguous=True)\
                    .then_inc(sig["b_in"], 16)
                after_all(sp, ("b_x2", b - 1, 1))
                sp.dma_start(x1[:, :, :], x_d[b]).then_inc(sig["a_xin"], 16)
                sp.dma_start(gb0[:, :], mod_row(0, b, 5)).then_inc(sig["b_in"], 16)

            def c_load(b):
                after_all(sp, ("c_out", b - 1, 1))
                sp.dma_start(crow[:, :, :].rearrange("p n d -> p (n d)"), mod_d[1, b, 0:3 * D]
                             .rearrange("(o d) -> o d", o=1).to_broadcast([P, 3 * D])).then_inc(sig["c_in"], 16)
                sp.dma_start(cgb[:, :], mod_row(1, b, 5)).then_inc(sig["c_in"], 16)
                sp.dma_start(cmod[:, :], mod_cols(1, b, 3), allow_slow_non_contiguous=True)\
                    .then_inc(sig["c_in"], 16)
                sp.dma_start(b1[:, :], a["L1_ffn_b1"][b].rearrange("(c p) -> p c", p=P),
                             allow_slow_non_contiguous=True).then_inc(sig["c_in"], 16)
                sp.dma_start(b2[:, :], a["L1_ffn_b2"][b].rearrange("(o d) -> o d", o=1).to_broadcast([P, D]))\
                    .then_inc(sig["c_in"], 16)
                sp.dma_start(w1[:, :], a["L1_ffn_w1"][b]).then_inc(sig["c_in"], 16)
                sp.dma_start(w2[:, :, :], a["L1_ffn_w2"][b].rearrange("(c p) d -> p c d", p=P))\
                    .then_inc(sig["c_in"], 16)

            def c_outp(b):
                after_all(sp, ("c_out", b, 1))
                sp.dma_start(out_d[b], yout[:, :, :]).then_inc(sig["c_stored"], 16)

            walk(sp, "sp", {("P", "load"): p_load, ("P", "store"): p_store, ("P", "stack"): p_stack,
                      ("P", "mrow"): mrow_out, ("A", "load"): a_load, ("A", "mrow"): mrow_out,
                      ("B", "load"): b_load, ("C", "load"): c_load, ("C", "outp"): c_outp},
                 late, ready)
            sp.wait_ge(sig["c_stored"], 16 * NB)

        @block.tensor
        def _(pe):
            pe.wait_ge(s_c, 16 * N_CONST)
            for n in range(4):
                last = nc.tensor.transpose(m0[:, n * P:(n + 1) * P], raw_qkv[:, n, :], ident[:, :])
            last.then_inc(s_sx, 1)
            pe.wait_ge(s_sv, SV_SILU)
            for L in range(2):
                for half in range(2):
                    dst = (w0p, w1p, se[0], se[1])[2 * L + half]
                    last = nc.tensor.matmul(dst[0:NB, 0:3 * D], silc[L], wmod[L][:, half * 3 * D:(half + 1) * 3 * D],
                                            start=True, stop=True)
            last.then_inc(s_sx, 1)
            pe.wait_ge(s_sv, SV_SPLIT)

            def ready():
                pe.wait_ge(s_c2, 16 * N_LATE)
                pe.wait_ge(s_sv, SV_END)
                pe.wait_ge(s_sa, SA_END)
                pe.wait_ge(s_sg, SG_END)
                pe.wait_ge(s_ones, 16 * PARTS)

            def transposes(bank_ap, src, name, wait, uses, *step):
                def run(b, *g):
                    after(pe, wait[0], b, wait[1] + (g[0] if g else 0))
                    bank_free(pe, uses, b, *step, *g)
                    for t in range(NT):
                        last = nc.tensor.transpose(bank_ap[:, t * P:(t + 1) * P], src[:, t, :], ident[:, :])
                    last.then_inc(sig[name], 1)
                return run

            p_xT = transposes(m1, xpn, "p_xT", ("p_xn", 1), M1_USES, "P", "xT")
            b_xT = transposes(m0, xbn, "b_xT", ("b_xn", 1), M0_USES, "B", "xT")
            c_xT = transposes(m1, xcn, "c_xT", ("c_xn2", 1), M1_USES, "C", "xT")
            c_xT3 = transposes(m1, xcn, "c_xT3", ("c_xn3", 1), M1_USES, "C", "xT3")
            oT_t = transposes(m0, otok, "a_oT", ("a_o", GROUPS), M0_USES, "B", "oT")
            pvs4 = pvs[:, :].rearrange("p (t q) -> p t q", t=NT)

            def proj(b, n):
                after(pe, "p_lo", b, 1)
                bank_free(pe, M1_USES, b, "P", "proj", n)
                mm3(m1[:, :], wp_hi[:, n, :], wp_lo[:, n, :], hp_hi[:, :], hp_lo[:, :]).then_inc(sig["p_proj"], 1)

            def v(b):
                bank_free(pe, M1_USES, b, "P", "v")
                for t in range(NT):
                    at = slice(t * P, (t + 1) * P)
                    last = mm3(m1[:, at], hp_hi[:, at], hp_lo[:, at], wp_hi[:, 4, :], wp_lo[:, 4, :])
                last.then_inc(sig["p_v"], 1)

            def smax(b, g, n):
                h, t = GH * g + n // NT, n % NT
                if n == 0:
                    after(pe, f"p_stack{g}", b, 32)
                after(pe, "a_max", b, 16 * g + n)
                nc.tensor.matmul(sm[:, :], qs[0:STACK, h, t * P:(t + 1) * P], ks[0:STACK, h, :],
                                 start=True, stop=True).then_inc(sig["a_smf"], 1)

            def mT(stage):
                def run(b, g):
                    after_all(pe, ("a_mp", b, 4 * (g + 1)), *bank_waits(M0_USES, b, stage, "mT", g))
                    nc.tensor.transpose(m0[0:PARTS * 16, 0:P // 2].bitcast(bf16),
                                        mpart[:, :, :].rearrange("p n c -> p (n c)"),
                                        identb[:, :]).then_inc(sig["a_mT"], 1)
                return run

            def sexp(b, g, kt, j):
                n = 16 * g + 4 * kt + j
                if n % 16 == 0:
                    after(pe, "a_row", b, 16 * PARTS * (g + 1))
                after(pe, "a_exp", b, max(n - 1, 0))
                h = GH * g + j
                nc.tensor.matmul(se[n % 2][:, :], ks[:, h, kt * P:(kt + 1) * P], qs[:, h, :],
                                 start=True, stop=True).then_inc(sig["a_sef"], 1)

            def pvm(b, g, kt):
                if kt == 0:
                    after(pe, "a_pvs", b, g)
                    after(pe, "a_vc", b, 1)
                after(pe, "a_exp", b, 16 * g + 4 * kt + 4)
                for j in range(GH):
                    last = nc.tensor.matmul(pv[32 * j:32 * j + 32, :], vaug[:, kt, GH * g + j, :],
                                            probs[:, kt % 2, j, :], start=(kt == 0), stop=(kt == NT - 1))
                last.then_inc(sig["a_pv"], 1)

            def pvT(stage, step):
                def run(b, *g):
                    n = g[0] if g else GROUPS - 1
                    after(pe, "a_pvs", b, n + 1)
                    bank_free(pe, M0_USES, b, stage, step, *g)
                    for t in range(NT):
                        last = nc.tensor.transpose(m0[:, t * P:(t + 1) * P], pvs4[:, t, :], ident[:, :])
                    last.then_inc(sig["a_pvT"], 1)
                return run

            def y(b):
                after(pe, "a_ot", b, 1)
                after(pe, "a_wog", b, 1)
                bank_free(pe, M0_USES, b, "B", "y")
                for t in range(NT):
                    at = slice(t * P, (t + 1) * P)
                    last = nc.tensor.matmul(m0[:, at], oT[:, at], wog[:, :], start=True, stop=True)
                last.then_inc(sig["a_y"], 1)

            def gate(b):
                after(pe, "b_hT", b, 1)
                bank_free(pe, M0_USES, b, "B", "gate")
                for t in range(NT):
                    last = nc.tensor.matmul(m0[:, t * NEX:(t + 1) * NEX], hb[:, t * P:(t + 1) * P], gate_w[:, :],
                                            start=True, stop=True)
                last.then_inc(sig["b_gate"], 1)

            def unit(b, u):
                if u == 0:
                    after(pe, "b_lo", b, 1)
                at = slice(u * P, (u + 1) * P)
                after(pe, "b_u", b, u)
                mm3(w0p[:, :], e0_hi[:, at], e0_lo[:, at], hb_hi[:, :], hb_lo[:, :]).then_inc(sig["b_w0"], 1)
                after(pe, "b_mu", b, u)
                mm3(w1p[:, :], e1_hi[:, at], e1_lo[:, at], hb_hi[:, :], hb_lo[:, :]).then_inc(sig["b_w1"], 1)

            def down(b, e):
                after(pe, "b_mu", b, 2 * e + 2)
                bank_free(pe, M0_USES, b, "B", "down", e)
                for t in range(NT):
                    at = slice(t * P, (t + 1) * P)
                    for f in range(HALVES):
                        last = nc.tensor.matmul(m0[:, at], mu[:, (2 * e + f) % 4, at], eo[:, e, f, :],
                                                start=(f == 0), stop=(f == HALVES - 1))
                last.then_inc(sig["b_down"], 1)

            def qk(b, p):
                after(pe, "c_nT", b, 1)
                bank_free(pe, M1_USES, b, "C", "qk", p)
                for n in range(2):
                    at = slice((2 * p + n) * P, (2 * p + n + 1) * P)
                    last = nc.tensor.matmul(m1[:, n * QK:(n + 1) * QK], nt[:, at], wqk[:, :], start=True, stop=True)
                last.then_inc(sig["c_qk"], 1)

            def hid(b, c):
                after(pe, "c_lo", b, 1)
                bank_free(pe, M1_USES, b, "C", "hid", c)
                at = slice(c * P, (c + 1) * P)
                mm3(m1[:, :], wh_hi[:, at], wh_lo[:, at], n_hi[:, :], n_lo[:, :]).then_inc(sig["c_hp"], 1)

            def sim(b):
                after(pe, "c_kq", b, 2)
                bank_free(pe, M1_USES, b, "C", "sim")
                for n in range(2):
                    for t in range(NT):
                        last = nc.tensor.matmul(m1[:, n * QK:(n + 1) * QK], kq[:, 0, t, n * P:(n + 1) * P],
                                                kq[:, 1, t, :], start=(t == 0), stop=(t == NT - 1))
                last.then_inc(sig["c_sim"], 1)

            def c_out(b):
                after(pe, "c_vg", b, 2)
                after(pe, "c_wo", b, 1)
                bank_free(pe, M1_USES, b, "C", "out")
                for t in range(NT):
                    at = slice(t * P, (t + 1) * P)
                    for n in range(2):
                        last = nc.tensor.matmul(m1[:, at], vg[:, n, at], wos[:, n, :], start=(n == 0), stop=(n == 1))
                last.then_inc(sig["c_o"], 1)

            def up(b, c):
                if c == 0:
                    after(pe, "c_nT3", b, 1)
                    after(pe, "c_in", b, 112)
                bank_free(pe, M1_USES, b, "C", "up", c)
                at = slice(c * P, (c + 1) * P)
                nc.tensor.matmul(m1[:, :], w1[:, at], nt, start=True, stop=True).then_inc(sig["c_up"], 1)

            def dn(b):
                after(pe, "c_gl", b, FCH)
                bank_free(pe, M1_USES, b, "C", "dn")
                for t in range(NT):
                    at = slice(t * P, (t + 1) * P)
                    for c in range(FCH):
                        last = nc.tensor.matmul(m1[:, at], gl[:, c, at], w2[:, c, :], start=(c == 0),
                                                stop=(c == FCH - 1))
                last.then_inc(sig["c_dn"], 1)

            walk(pe, "pe", {("P", "xT"): p_xT, ("P", "proj"): proj, ("P", "v"): v, ("P", "max"): smax, ("P", "mT"): mT("P"),
                      ("A", "max"): smax, ("A", "mT"): mT("A"), ("A", "exp"): sexp, ("A", "pv"): pvm,
                      ("A", "pvT"): pvT("A", "pvT"), ("B", "pvlast"): lambda b: pvm(b, GROUPS - 1, NT - 1),
                      ("B", "pvT3"): pvT("B", "pvT3"), ("B", "oT"): oT_t, ("B", "y"): y, ("B", "xT"): b_xT,
                      ("B", "gate"): gate, ("B", "unit"): unit, ("B", "down"): down, ("C", "xT"): c_xT,
                      ("C", "qk"): qk, ("C", "hid"): hid, ("C", "sim"): sim, ("C", "out"): c_out,
                      ("C", "xT3"): c_xT3, ("C", "up"): up, ("C", "dn"): dn},
                 nothing, ready)

        @block.scalar
        def _(act):
            act.wait_ge(s_c, 16 * N_CONST)
            for L in range(2):
                nc.scalar.activation(tanc[L], rawc[L], ACT.Tanh, scale=0.5).then_inc(s_sa, 1)

            def late():
                act.wait_ge(s_c2, 16 * N_LATE)
                nc.scalar.activation(e0_hi[:, :], raw0, ACT.Copy).then_inc(s_sa, 1)
                nc.scalar.activation(e1_hi[:, :], raw1, ACT.Copy).then_inc(s_sa, 1)
                nc.scalar.activation(wh_hi[:, :], raw_h, ACT.Copy).then_inc(s_sa, 1)
                nc.scalar.activation(bhh[:, :], bh[:, :], ACT.Copy, scale=0.5).then_inc(s_sa, 1)
                for n in range(2):
                    nc.scalar.activation(gam[:, n, :], gam[:, n, :], ACT.Copy, scale=0.5).then_inc(s_sa, 1)

            def ready():
                act.wait_ge(s_sv, SV_END)
                act.wait_ge(s_sg, SG_END)
                act.wait_ge(s_sx, SX_END)

            def copy_in(name, src, dst, wait, free):
                def run(b):
                    after(act, wait, b, 1)
                    after(act, free, b - 1, 1)
                    nc.scalar.activation(dst, src, ACT.Copy).then_inc(sig[name], 1)
                return run

            def modulate(name, src, dst, mod, wait, ready, rounded=None):
                shift, scale = mod
                def run(b):
                    after(act, wait, b, 1)
                    after(act, *ready(b))
                    nc.scalar.activation(dst, src, ACT.Identity, bias=shift, scale=scale).then_inc(sig[name], 1)
                    if rounded:
                        dst_hi, name_hi, free = rounded
                        after(act, *free(b))
                        nc.scalar.activation(dst_hi[:, :], src, ACT.Identity, bias=shift, scale=scale)\
                            .then_inc(sig[name_hi], 1)
                return run

            def normalise(key, src, dst, wait, name, free):
                def run(b):
                    after(act, wait, b, 1)
                    after(act, *free(b))
                    for t in range(NT):
                        last = nc.scalar.activation(dst[:, t, :], src[:, t, :], ACT.Identity,
                                                    bias=shift_n[key][:, t:t + 1], scale=rstd[key][:, t:t + 1])
                    last.then_inc(sig[name], 1)
                return run

            def mrow_in(b, g):
                after(act, "a_mT", b, g + 1)
                after(act, "a_row", b, 16 * PARTS * g)
                nc.scalar.activation(mrow[:, :], m0[0:PARTS * 16, 0:P // 2].bitcast(bf16), ACT.Copy)\
                    .then_inc(sig["a_mrow"], 1)

            def exp(b, g, kt, j):
                n = 16 * g + 4 * kt + j
                after(act, "a_sef", b, n + 1)
                if j == 0:
                    after(act, "a_pv", b, max(4 * g + kt - 1, 0))
                nc.scalar.activation(probs[:, kt % 2, j, :], se[n % 2][:, :], ACT.Exp).then_inc(sig["a_exp"], 1)

            def pvcopy(b, g=GROUPS - 1):
                after(act, "a_pv", b, NT * (g + 1))
                after(act, "a_pvT", b, g)
                nc.scalar.activation(pvs[:, :], pv[:, :], ACT.Copy).then_inc(sig["a_pvs"], 1)

            def vcopy_out(b):
                after(act, "p_v", b, 1)
                after(act, "a_vc", b - 1, 1)
                nc.scalar.activation(vtok[:, :, :].rearrange("p t d -> p (t d)"), m1[:, :], ACT.Copy)\
                    .then_inc(sig["p_vn"], 1)

            def route(b):
                after(act, "b_dif", b, 1)
                nc.scalar.activation(pw[:, 1, :, :], pw[:, 0, :, :], ACT.Exp).then_inc(sig["b_e2"], 1)

            def unit(b, u):
                after(act, "b_w0", b, u + 1)
                after(act, "b_u", b, u)
                nc.scalar.activation(th[:, :], w0p[:, :], ACT.Tanh, scale=0.5).then_inc(sig["b_tanh"], 1)

            def qkt(b, p):
                after(act, "c_qz", b, p + 1)
                after(act, "c_qs", b, p)
                nc.scalar.activation(qt[:, :, :], qz[:, :, :], ACT.Tanh, scale=0.5).then_inc(sig["c_qt"], 1)

            def hid(b, c):
                n = HID_ORDER.index(c)
                after(act, "c_hp", b, n + 1)
                after(act, "c_hs", b, n)
                if n == 0:
                    after(act, "c_gl", b - 1, FCH)
                nc.scalar.activation(hth[:, :], m1[:, :], ACT.Tanh, scale=0.5, bias=bhh[:, c:c + 1])\
                    .then_inc(sig["c_ht"], 1)
                nc.scalar.activation(hz[:, :], m1[:, :], ACT.Identity, bias=bh[:, c:c + 1]).then_inc(sig["c_hz"], 1)

            def simexp(b):
                after(act, "c_nms", b, 1)
                after(act, "c_hs", b, HCH)
                for n in range(2):
                    nc.scalar.activation(ea[:, n, :], m1[:, n * QK:(n + 1) * QK], ACT.Exp, scale=1.0 / S,
                                         bias=cst[:, 1, n:n + 1], accum_out=cst[:, 2, n:n + 1])\
                        .then_inc(sig["c_ea"], 1)

            def up(b, c):
                after(act, "c_up", b, c + 1)
                after(act, "c_gl", b, c)
                if c == 0:
                    after(act, "c_u2", b - 1, FCH)
                    nc.scalar.activation(b1s[:, :], b1[:, :], ACT.Copy, scale=GELU_A ** 0.5).then_inc(sig["c_bs"], 1)
                nc.scalar.activation(uz[:, :], m1[:, :], ACT.Identity, bias=b1[:, c:c + 1]).then_inc(sig["c_uz"], 1)
                after(act, "c_bs", b, 1)
                nc.scalar.activation(u2[:, :], m1[:, :], ACT.Square, scale=GELU_A ** 0.5, bias=b1s[:, c:c + 1])\
                    .then_inc(sig["c_u2"], 1)

            def down(b, e):
                after(act, "b_down", b, e + 1)
                if e == 0:
                    after(act, "b_route", b, 7)
                    after(act, "b_t", b - 1, 1)
                elif e == 1:
                    after(act, "b_acc", b - 1, NEX - 1)
                else:
                    after(act, "b_acc", b, e - 1)
                for t in range(NT):
                    last = nc.scalar.activation((scaled if e else acc)[:, t, :], m0[:, t * D:(t + 1) * D], ACT.Copy,
                                                scale=pick[:, 5, t, e:e + 1])
                last.then_inc(sig["b_sc"], 1)

            def upg(b, c):
                after(act, "c_ub", b, c + 1)
                after(act, "c_wo", b, 1)
                nc.scalar.activation(ut[:, :], u2[:, :], ACT.Tanh, scale=GELU_C).then_inc(sig["c_ut"], 1)

            walk(act, "act", {
                ("P", "xn"): normalise("p", xp, xpn, "p_nm", "p_xn", lambda b: ("p_mv", b, 1)),
                ("B", "xn"): normalise("b", x1, xbn, "b_nm", "b_xn", lambda b: ("b_gate", b - 1, 1)),
                ("C", "xn"): normalise("c", x2, xcn, "c_nm1", "c_xn", lambda b: ("c_out", b - 1, 1)),
                ("C", "xn2"): normalise("c", hc, xcn, "c_nm2", "c_xn2", lambda b: ("c_h", b, 1)),
                ("C", "xn3"): normalise("c", x3, xcn, "c_nm3", "c_xn3", lambda b: ("c_x3", b, 1)),
                ("P", "hT"): modulate("p_hT", m1[:, :], hp, (pmod[:, 0:1], pmod[:, 1:2]), "p_xT",
                                      lambda b: ("p_in", b, 32), (hp_hi, "p_hi", lambda b: ("p_v", b - 1, 1))),
                ("P", "v"): vcopy_out, ("P", "mrow"): mrow_in, ("A", "mrow"): mrow_in, ("A", "exp"): exp,
                ("A", "pvs"): pvcopy, ("B", "pvs3"): pvcopy,
                ("B", "ot"): copy_in("a_ot", m0[:, :], oT[:, :], "a_oT", "a_y"),
                ("B", "hT"): modulate("b_hT", m0[:, :], hb, (bmod[:, 0:1], bmod[:, 1:2]), "b_xT",
                                      lambda b: ("b_in", b, 32), (hb_hi, "b_hi", lambda b: ("b_w1", b - 1, UNITS))),
                ("B", "route"): route, ("B", "unit"): unit, ("B", "down"): down,
                ("C", "nT"): modulate("c_nT", m1[:, :], nt, (ln_gb[:, 1:2], ln_gb[:, 0:1]), "c_xT",
                                      lambda b: ("c_xT", b, 1), (n_hi, "c_hi", lambda b: ("c_hp", b - 1, HCH))),
                ("C", "nT3"): modulate("c_nT3", m1[:, :], nt, (cmod[:, 0:1], cmod[:, 1:2]), "c_xT3",
                                       lambda b: ("c_in", b, 112)),
                ("C", "qkz"): qkt, ("C", "hid"): hid, ("C", "simexp"): simexp, ("C", "up"): up, ("C", "upg"): upg},
                 late, ready, ("P", "v"))

        @block.vector
        def _(dve):
            V = nc.vector
            done = [0]

            def link(ins):
                ins.then_inc(s_sv, 1)
                done[0] += 1
                dve.wait_ge(s_sv, done[0])

            link(V.memset(vaug[:, :, :, :], 0.0))
            link(V.memset(vaug[:, :, :, HD:HD + 1], 1.0))
            link(V.memset(parts[:, :, :], 1.0))
            assert done[0] == SV_ONES
            dve.wait_ge(s_c, 16 * N_CONST)
            link(V.tensor_copy(identb[:, :], ident[:, :]))
            dve.wait_ge(s_sa, 2)
            for L in range(2):
                link(V.scalar_tensor_tensor(out=tanc[L], in0=tanc[L], scalar=1.0, in1=rawc[L], op0=ALU.add,
                                            op1=ALU.mult))
                link(V.tensor_scalar(silc[L], tanc[L], 0.5, None, ALU.mult))
            assert done[0] == SV_SILU
            def mod_rows(L):
                r, t = modr[L], modt[L]
                for half in range(2):
                    link(V.tensor_copy(r[:, half * 3 * D:(half + 1) * 3 * D],
                                       (w0p, w1p, se[0], se[1])[2 * L + half][0:NB, 0:3 * D]))
                for n in (1, 4):
                    link(V.tensor_scalar(r[:, n * D:(n + 1) * D], r[:, n * D:(n + 1) * D], 1.0, None, ALU.add))
                for n in (2, 5):
                    gt, sg = r[:, n * D:(n + 1) * D], t[:, 0:D]
                    mg = t[:, D:2 * D]
                    link(V.tensor_scalar(sg, gt, 0.0, 2.0, ALU.is_ge, ALU.mult))
                    link(V.tensor_scalar(sg, sg, -1.0, None, ALU.add))
                    link(V.tensor_scalar(mg, gt, -1.0, None, ALU.mult))
                    link(V.tensor_tensor(mg, mg, gt, ALU.max))
                    link(V.tensor_scalar(mg, mg, 0.25, None, ALU.max))
                    link(V.tensor_tensor(gt, mg, sg, ALU.mult))
                assert done[0] == SV_MOD[L], (L, done[0])
            dve.wait_ge(s_sx, SX_END)
            mod_rows(0)
            link(V.tensor_copy(wqT[:, :, :].rearrange("p n c -> p (n c)"), m0[:, :]))
            link(V.tensor_copy(wo0T[:, :], wqT[:, 3, :]))
            for n in range(2):
                pair = wqT[:, n, :].rearrange("p (i two) -> p i two", two=2)
                turned = w2T[:, n, :].rearrange("p (i two) -> p i two", two=2)
                link(V.tensor_scalar(turned[:, :, 0:1], pair[:, :, 1:2], -1.0, None, ALU.mult))
                link(V.tensor_copy(turned[:, :, 1:2], pair[:, :, 0:1]))
            for n, src in enumerate((wqT[:, 0, :], w2T[:, 0, :], wqT[:, 1, :], w2T[:, 1, :], wqT[:, 2, :])):
                link(V.tensor_copy(wp_hi[:, n, :], src))
                link(V.tensor_tensor(wp_lo[:, n, :], src, as_f32(wp_hi[:, n, :]), ALU.subtract))
            assert done[0] == SV_SPLIT, done[0]

            def late():
                mod_rows(1)
                dve.wait_ge(s_sa, SA_END)
                link(V.tensor_tensor(wh_lo[:, :], raw_h, as_f32(wh_hi[:, :]), ALU.subtract))
                link(V.tensor_tensor(e0_lo[:, :], raw0, as_f32(e0_hi[:, :]), ALU.subtract))
                assert done[0] == SV_END, done[0]

            def ready():
                dve.wait_ge(s_c2, 16 * N_LATE)
                dve.wait_ge(s_sg, SG_END)
                dve.wait_ge(s_md, 32)

            def norm_stats(key, src, wait, name):
                def run(b):
                    for w in wait:
                        after(dve, w[0], b, w[1])
                    for t in range(NT):
                        last = V.bn_stats(stats[key][:, t, :], src[:, t, :])
                    last.then_inc(sig[name + "s"], 1)
                    after_all(dve, (name + "s", b, 1))
                    for t in range(NT):
                        last = V.bn_aggr(mv[key][:, t, :], stats[key][:, t, :])
                    last.then_inc(sig[name], 1)
                return run

            def rot(b, n):
                kind, part = n // 2, n % 2
                after(dve, "p_proj", b, n + 1)
                after(dve, "p_sum", b, kind)
                V.tensor_tensor((rot1, rot2)[part][:, :], m1[:, :], (cosT, sinT)[part][:, :], ALU.mult)\
                    .then_inc(sig["p_rot"], 1)

            def smax(b, g, n):
                after(dve, "a_smf", b, 16 * g + n + 1)
                if n == 0:
                    after(dve, "a_mp", b, max(4 * (g - 1), 0))
                V.tensor_reduce(negmax[:, g % 2, n:n + 1], sm[:, :], AX, ALU.max, negate=True)\
                    .then_inc(sig["a_max"], 1)

            def mparts(b, g):
                nm = negmax[:, g % 2, :]
                after(dve, "a_max", b, 16 * (g + 1))
                after(dve, "a_mT", b, g)
                V.tensor_copy(mpart[:, 0, :], nm).then_inc(sig["a_mp"], 1)
                after(dve, "a_mp", b, 4 * g + 1)
                V.tensor_tensor(mrem[:, :], nm, mpart[:, 0, :], ALU.subtract).then_inc(sig["a_mp"], 1)
                after(dve, "a_mp", b, 4 * g + 2)
                V.tensor_copy(mpart[:, 1, :], mrem[:, :]).then_inc(sig["a_mp"], 1)
                after(dve, "a_mp", b, 4 * g + 3)
                V.tensor_tensor(mpart[:, 2, :], mrem[:, :], mpart[:, 1, :], ALU.subtract).then_inc(sig["a_mp"], 1)

            def onorm(b, g=GROUPS - 1):
                after(dve, "a_pvT", b, g + 1)
                got = m0[:, :].rearrange("p (t j c) -> p t j c", t=NT, j=GH)
                r = rsum[:, :].rearrange("p (t j o) -> p t j o", t=NT, j=GH)
                V.reciprocal(r, got[:, :, :, HD:HD + 1]).then_inc(sig["a_rc"], 1)
                after(dve, "a_rc", b, g + 1)
                if g == 0:
                    after(dve, "a_oT", b - 1, 1)
                V.tensor_tensor(otok[:, :, GH * HD * g:GH * HD * (g + 1)].rearrange("p t (j d) -> p t j d", j=GH),
                                got[:, :, :, 0:HD], r.to_broadcast([P, NT, GH, HD]), ALU.mult)\
                    .then_inc(sig["a_o"], 1)

            def over_t(row):
                return row.unsqueeze(1).to_broadcast([P, NT, D])

            def bank_t(b_):
                return b_[:, :].rearrange("p (t d) -> p t d", t=NT)

            def do_x1(b):
                after(dve, "a_y", b, 1)
                after(dve, "a_xin", b, 16)
                V.tensor_tensor(x1[:, :, :], bank_t(m0), x1[:, :, :], ALU.add).then_inc(sig["a_x1"], 1)

            def do_wog(b):
                after(dve, "a_in", b, 16)
                after(dve, "a_y", b - 1, 1)
                V.tensor_tensor(wog[:, :], wo0T[:, :], ga[:, :], ALU.mult).then_inc(sig["a_wog"], 1)

            def do_logits(b):
                after(dve, "b_gate", b, 1)
                V.tensor_copy(logits[:, :, :].rearrange("p t n -> p (t n)"), m0[:, 0:NT * NEX])\
                    .then_inc(sig["b_lg"], 1)

            def do_top(b):
                after_all(dve, ("b_lg", b, 1))
                for t in range(NT):
                    last = V.max(top[:, t, :], logits[:, t, :])
                last.then_inc(sig["b_tops"], 1)
                after_all(dve, ("b_tops", b, 1))
                for t in range(NT):
                    last = V.max_index(topi[:, t, :], top[:, t, :], logits[:, t, :])
                last.then_inc(sig["b_top"], 1)
                V.tensor_tensor(pw[:, 0, :, :], top[:, :, 1:2], top[:, :, 0:1], ALU.subtract)\
                    .then_inc(sig["b_dif"], 1)

            def do_weights(b):
                n = [0]

                def link_b(ins):
                    ins.then_inc(sig["b_route"], 1)
                    n[0] += 1
                    after(dve, "b_route", b, n[0])

                bc = lambda ap: ap.to_broadcast([P, NT, NEX])
                after(dve, "b_e2", b, 1)
                after(dve, "b_top", b, 1)
                after(dve, "b_sc", b - 1, NEX)
                link_b(V.tensor_scalar(pw[:, 2, :, :], pw[:, 1, :, :], 1.0, 2.0, ALU.add, ALU.mult))
                link_b(V.reciprocal(pw[:, 3, :, :], pw[:, 2, :, :]))
                V.tensor_tensor(pw[:, 4, :, :], pw[:, 3, :, :], pw[:, 1, :, :], ALU.mult)
                io = iota8[:, :].unsqueeze(1).to_broadcast([P, NT, NEX])
                link_b(V.tensor_copy(pick[:, 4, :, :], topi[:, :, :]))
                V.tensor_tensor(pick[:, 0, :, :], io, bc(pick[:, 4, :, 0:1]), ALU.is_equal)
                link_b(V.tensor_tensor(pick[:, 1, :, :], io, bc(pick[:, 4, :, 1:2]), ALU.is_equal))
                V.tensor_tensor(pick[:, 2, :, :], pick[:, 0, :, :], bc(pw[:, 3, :, :]), ALU.mult)\
                    .then_inc(sig["b_route"], 1)
                V.tensor_tensor(pick[:, 3, :, :], pick[:, 1, :, :], bc(pw[:, 4, :, :]), ALU.mult)\
                    .then_inc(sig["b_route"], 1)
                n[0] += 2
                after(dve, "b_route", b, n[0])
                link_b(V.tensor_tensor(pick[:, 5, :, :], pick[:, 2, :, :], pick[:, 3, :, :], ALU.add))

            def unit(b, u):
                after(dve, "b_tanh", b, u + 1)
                after(dve, "b_mu", b, u)
                V.scalar_tensor_tensor(out=uu[:, :], in0=th[:, :], scalar=1.0, in1=w0p[:, :],
                                       op0=ALU.add, op1=ALU.mult).then_inc(sig["b_u"], 1)
                after(dve, "b_w1", b, u + 1)
                after(dve, "b_u", b, u + 1)
                after(dve, "b_down", b, max(u // 2 - 1, 0))
                V.tensor_tensor(mu[:, u % 4, :], uu[:, :], w1p[:, :], ALU.mult).then_inc(sig["b_mu"], 1)

            def do_x2(b):
                after(dve, "b_acc", b, NEX - 1)
                after(dve, "b_in", b, 32)
                V.tensor_tensor(acc[:, :, :], acc[:, :, :], over_t(gb0[:, :]), ALU.mult).then_inc(sig["b_t"], 1)
                after(dve, "b_t", b, 1)
                after(dve, "c_x3", b - 1, 1)
                V.tensor_tensor(x2[:, :, :], acc[:, :, :], x1[:, :, :], ALU.add).then_inc(sig["b_x2"], 1)

            def qkz(b, p):
                after(dve, "c_qk", b, p + 1)
                after(dve, "c_qs", b, p)
                if p == 1:
                    after(dve, "c_kq", b, 1)
                V.tensor_tensor(qz[:, :, :], m1[:, :].rearrange("p (n c) -> p n c", n=2),
                                bqk[:, :].unsqueeze(1).to_broadcast([P, 2, QK]), ALU.add).then_inc(sig["c_qz"], 1)

            def qks(b, p):
                after(dve, "c_qt", b, p + 1)
                V.scalar_tensor_tensor(out=qz[:, :, :], in0=qt[:, :, :], scalar=1.0, in1=qz[:, :, :], op0=ALU.add,
                                       op1=ALU.mult).then_inc(sig["c_qs"], 1)

            def hids(b, c):
                n = HID_ORDER.index(c)
                after(dve, "c_hz", b, n + 1)
                after(dve, "c_vg", b, n // 2)
                after(dve, "c_kq", b, 2)
                V.scalar_tensor_tensor(out=sil[n % 2], in0=hth[:, :], scalar=1.0, in1=hz[:, :], op0=ALU.add,
                                       op1=ALU.mult).then_inc(sig["c_hs"], 1)
                if n % 2:
                    after(dve, "c_hs", b, n + 1)
                    after(dve, "c_o", b - 1, 1)
                    V.tensor_tensor(vg[:, n // 2, :], sil[0], sil[1], ALU.mult).then_inc(sig["c_vg"], 1)

            def simmax(b):
                after(dve, "c_sim", b, 1)
                V.tensor_reduce(cst[:, 0, :], m1[:, :].rearrange("p (n c) -> p n c", n=2), AX, ALU.max, negate=True)\
                    .then_inc(sig["c_nm"], 1)
                after(dve, "c_nm", b, 1)
                V.tensor_scalar(cst[:, 1, :], cst[:, 0, :], 1.0 / S, None, ALU.mult).then_inc(sig["c_nms"], 1)

            def simsum(b):
                after(dve, "c_ea", b, 2)
                V.reciprocal(cst[:, 3, :], cst[:, 2, :]).then_inc(sig["c_r"], 1)
                after(dve, "c_r", b, 1)
                for n in range(2):
                    last = V.tensor_scalar(ea[:, n, :], ea[:, n, :], cst[:, 3, n:n + 1], 0.0, ALU.mult, ALU.add,
                                           accum_out=cst[:, 4, n:n + 1])
                last.then_inc(sig["c_rs"], 1)
                after(dve, "c_rs", b, 1)
                after(dve, "c_o", b - 1, 1)
                for n in range(2):
                    last = V.tensor_scalar(wos[:, n, :], wout[:, n, :], cst[:, 4, n:n + 1], 0.25, ALU.mult, ALU.mult)
                last.then_inc(sig["c_wo"], 1)

            def res(b):
                after(dve, "c_o", b, 1)
                after(dve, "c_lo", b, 1)
                after(dve, "c_qk", b, 2)
                V.tensor_tensor(tc[:, :, :], bank_t(m1), over_t(bout[:, :]), ALU.add).then_inc(sig["c_o1"], 1)

            def upa(b, c):
                after(dve, "c_u2", b, c + 1)
                V.scalar_tensor_tensor(out=u2[:, :], in0=u2[:, :], scalar=1.0, in1=uz[:, :], op0=ALU.add,
                                       op1=ALU.mult).then_inc(sig["c_ub"], 1)

            def upg(b, c):
                after(dve, "c_ut", b, c + 1)
                V.scalar_tensor_tensor(out=gl[:, c, :], in0=ut[:, :], scalar=1.0, in1=uz[:, :], op0=ALU.add,
                                       op1=ALU.mult).then_inc(sig["c_gl"], 1)

            def fin(b):
                after(dve, "c_dn", b, 1)
                V.scalar_tensor_tensor(out=tc[:, :, :], in0=bank_t(m1), scalar=0.5, in1=over_t(b2[:, :]),
                                       op0=ALU.mult, op1=ALU.add).then_inc(sig["c_y1"], 1)

            walk(dve, "dve", {
                ("P", "stats"): norm_stats("p", xp, [("p_in", 32)], "p_mv"),
                ("P", "rot"): rot, ("P", "max"): smax, ("P", "mparts"): mparts,
                ("A", "max"): smax, ("A", "mparts"): mparts, ("A", "onorm"): onorm, ("B", "onorm3"): onorm,
                ("B", "x1"): do_x1, ("A", "wog"): do_wog, ("B", "stats"): norm_stats("b", x1, [("a_x1", 1)], "b_mv"),
                ("B", "logits"): do_logits, ("B", "top"): do_top, ("B", "weights"): do_weights,
                ("B", "unit"): unit, ("B", "x2"): do_x2,
                ("C", "stats"): norm_stats("c", x2, [("b_x2", 1)], "c_mv"),
                ("C", "stats2"): norm_stats("c", hc, [("c_h", 1)], "c_mv2"),
                ("C", "qkz"): qkz, ("C", "qks"): qks, ("C", "hids"): hids, ("C", "simmax"): simmax,
                ("C", "simsum"): simsum, ("C", "res"): res,
                ("C", "stats3"): norm_stats("c", x3, [("c_x3", 1)], "c_mv3"),
                ("C", "upa"): upa, ("C", "upg"): upg, ("C", "fin"): fin}, late, ready, ("P", "max"))

        @block.gpsimd
        def _(pool):
            G = nc.gpsimd
            pool.wait_ge(s_c, 16 * N_CONST)
            pool.wait_ge(s_ones, 16 * PARTS)

            def late():
                pool.wait_ge(s_sa, SA_END)
                G.tensor_tensor(e1_lo[:, :], raw1, as_f32(e1_hi[:, :]), ALU.subtract).then_inc(s_sg, 1)

            def ready():
                pool.wait_ge(s_c2, 16 * N_LATE)
                pool.wait_ge(s_sv, SV_END)
                pool.wait_ge(s_sa, SA_END)
                pool.wait_ge(s_sx, SX_END)

            def deviation(key, wait, eps, name, nm):
                def run(b):
                    after_all(pool, (wait, b, 1))
                    G.tensor_scalar(rstd[key][:, :].unsqueeze(2), mv[key][:, :, 1:2], EPS, None, ALU.add)\
                        .then_inc(sig[eps], 1)
                    G.tensor_scalar(shift_n[key][:, :].unsqueeze(2), mv[key][:, :, 0:1], -1.0, None, ALU.mult)\
                        .then_inc(sig[eps], 1)
                    after(pool, eps, b, 2)
                    G.tensor_tensor(rstd[key][:, :], rstd[key][:, :], nhalf[:, :], ALU.pow).then_inc(sig[name], 1)
                    after(pool, name, b, 1)
                    G.tensor_tensor(shift_n[key][:, :], shift_n[key][:, :], rstd[key][:, :], ALU.mult)\
                        .then_inc(sig[nm], 1)
                return run

            def lower(src, hi_, dst, wait, name):
                def run(b):
                    after(pool, wait, b, 1)
                    G.tensor_tensor(dst[:, :], src, as_f32(hi_[:, :]), ALU.subtract).then_inc(sig[name], 1)
                return run

            def split(b, n):
                dst = parts
                after(pool, "p_rot", b, 2 * n + 2)
                if n == 1:
                    after(pool, "p_stored0", b, 16)
                else:
                    after(pool, "p_stored1", b - 1, 16 * PARTS)
                G.tensor_tensor(rem[:, :], rot1[:, :], rot2[:, :], ALU.add).then_inc(sig["p_sum"], 1)
                after_all(pool, ("p_sum", b, n + 1))
                G.tensor_copy(dst[:, 0, :], rem[:, :]).then_inc(sig["p_part0"], 1)
                after(pool, "p_part0", b, n + 1)
                G.tensor_tensor(rem[:, :], rem[:, :], dst[:, 0, :], ALU.subtract).then_inc(sig["p_rem"], 1)
                after_all(pool, ("p_rem", b, n + 1))
                G.tensor_copy(dst[:, 1, :], rem[:, :]).then_inc(sig["p_part1"], 1)
                after(pool, "p_part1", b, n + 1)
                G.tensor_tensor(dst[:, 2, :], rem[:, :], dst[:, 1, :], ALU.subtract).then_inc(sig["p_part2"], 1)

            def vcopy(b):
                after_all(pool, ("p_vn", b, 1), ("a_pv", b - 1, 16))
                G.tensor_copy(vaug[:, :, :, 0:HD], vtok[:, :, :].rearrange("p t (h d) -> p t h d", h=HEADS))\
                    .then_inc(sig["a_vc"], 1)

            def over_t(row):
                return row.unsqueeze(1).to_broadcast([P, NT, D])

            def mod(b):
                after(pool, "c_in", b, 112)
                after(pool, "c_xn", b, 1)
                after(pool, "c_stored", b - 1, 16)
                G.tensor_tensor(hc[:, :, :], xcn[:, :, :], over_t(crow[:, 1, :]), ALU.mult).then_inc(sig["c_m1"], 1)
                after(pool, "c_m1", b, 1)
                G.tensor_tensor(hc[:, :, :], hc[:, :, :], over_t(crow[:, 0, :]), ALU.add).then_inc(sig["c_h"], 1)

            def qkgb(b, p):
                after(pool, "c_qs", b, p + 1)
                if p == 0:
                    after(pool, "c_dn", b - 1, 1)
                at = slice(2 * p, 2 * p + 2)
                for n in range(2):
                    G.tensor_tensor(kq[:, n, at, :], qz[:, :, :], gam[:, n, :].unsqueeze(1).to_broadcast([P, 2, QK]),
                                    ALU.mult).then_inc(sig["c_g"], 1)
                after(pool, "c_g", b, 2 * p + 2)
                for n in range(2):
                    last = G.tensor_tensor(kq[:, n, at, :], kq[:, n, at, :],
                                           bet[:, n, :].unsqueeze(1).to_broadcast([P, 2, QK]), ALU.add)
                last.then_inc(sig["c_kq"], 1)

            def res(b):
                after(pool, "c_o1", b, 1)
                G.tensor_tensor(tc[:, :, :], tc[:, :, :], hc[:, :, :], ALU.add).then_inc(sig["c_res"], 1)
                after(pool, "c_res", b, 1)
                G.tensor_tensor(tc[:, :, :], tc[:, :, :], over_t(crow[:, 2, :]), ALU.mult).then_inc(sig["c_res"], 1)
                after(pool, "c_res", b, 2)
                after(pool, "b_x2", b, 1)
                G.tensor_tensor(x3[:, :, :], tc[:, :, :], x2[:, :, :], ALU.add).then_inc(sig["c_x3"], 1)

            def accumulate(b, e):
                after(pool, "b_sc", b, e + 1)
                after(pool, "b_acc", b, e - 1)
                G.tensor_tensor(acc[:, :, :], acc[:, :, :], scaled[:, :, :], ALU.add).then_inc(sig["b_acc"], 1)

            def fin(b):
                after(pool, "c_y1", b, 1)
                G.tensor_tensor(tc[:, :, :], tc[:, :, :], over_t(cgb[:, :]), ALU.mult).then_inc(sig["c_yg"], 1)
                after(pool, "c_yg", b, 1)
                G.tensor_tensor(yout[:, :, :], tc[:, :, :], x3[:, :, :], ALU.add).then_inc(sig["c_out"], 1)

            walk(pool, "pool", {
                ("P", "rstd"): deviation("p", "p_mv", "p_eps", "p_rstd", "p_nm"),
                ("P", "lo"): lower(hp, hp_hi, hp_lo, "p_hi", "p_lo"), ("P", "split"): split,
                ("A", "vcopy"): vcopy, ("B", "acc"): accumulate, ("B", "rstd"): deviation("b", "b_mv", "b_eps", "b_rstd", "b_nm"),
                ("B", "lo"): lower(hb, hb_hi, hb_lo, "b_hi", "b_lo"),
                ("C", "rstd"): deviation("c", "c_mv", "c_eps", "c_rstd", "c_nm1"), ("C", "mod"): mod,
                ("C", "rstd2"): deviation("c", "c_mv2", "c_eps2", "c_rstd2", "c_nm2"),
                ("C", "lo"): lower(nt, n_hi, n_lo, "c_hi", "c_lo"),
                ("C", "qkgb"): qkgb, ("C", "res"): res,
                ("C", "rstd3"): deviation("c", "c_mv3", "c_eps3", "c_rstd3", "c_nm3"),
                ("C", "fin"): fin}, late, ready)


N_CONST, N_LATE = 12, 17
SV_ONES = 3
SV_SILU = 8
SV_MOD = (24, 56)
SV_SPLIT = 40
SV_END = 58
SA_END = 8
SG_END = 1
SX_END = 2
PER_BATCH.update({n + "s": 1 for n in ("p_mv", "b_mv", "c_mv", "c_mv2", "c_mv3", "b_top")})

_INS = ['L0_attn_x', 'L0_attn_w_qkv', 'L0_attn_w_out', 'L0_ffn_gate_kernel', 'L0_ffn_w0_kernel', 'L0_ffn_w1_kernel',
        'L0_ffn_wo_kernel', 'L0_c', 'L0_wmod', 'L1_attn_ln_g', 'L1_attn_ln_b', 'L1_attn_W_hidden',
        'L1_attn_b_hidden', 'L1_attn_W_qk', 'L1_attn_b_qk', 'L1_attn_os_gamma', 'L1_attn_os_beta', 'L1_attn_W_out',
        'L1_attn_b_out', 'L1_ffn_w1', 'L1_ffn_b1', 'L1_ffn_w2', 'L1_ffn_b2', 'L1_c', 'L1_wmod']


def shape_constants():
    ids = np.arange(HD // 2, dtype=np.float32)
    theta = np.power(np.float32(10000.0), np.float32(2.0) * ids / np.float32(HD)).astype(np.float32)
    ang = (np.arange(S, dtype=np.float32)[:, None] / theta).astype(np.float32)
    rows = [np.repeat(f(ang).astype(np.float32), 2, axis=1).T for f in (np.cos, np.sin)]
    cosT, sinT = (np.ascontiguousarray(np.tile(r, (HEADS, 1))) for r in rows)
    return {"cosT": cosT, "sinT": sinT, "ident": np.eye(P, dtype=np.float32),
            "nhalf": np.full((P, NT), -0.5, np.float32),
            "iota8": np.tile(np.arange(NEX, dtype=np.float32), (P, 1))}


def kernel(**inputs):
    import concourse.bacc as bacc
    from concourse.bass_utils import run_bass_kernel_spmd

    nc = bacc.Bacc("TRN2", target_bir_lowering=False, num_devices=1)
    arrays, args = {}, {}
    given = {name: np.ascontiguousarray(inputs[name]) for name in _INS}
    for name, value in {**given, **shape_constants()}.items():
        arrays[f"in_{name}"] = value
        args[name] = nc.dram_tensor(f"in_{name}", value.shape, mybir.dt.from_np(value.dtype), kind="ExternalInput").ap()
    out = nc.dram_tensor("out", (NB, S, D), mybir.dt.float32, kind="ExternalOutput").ap()
    adaln_two_layers(nc, args, out)
    r = run_bass_kernel_spmd(nc, [arrays], core_ids=[0])
    return r.results[0]["out"]
```

```python
import numpy as np
import concourse.bass as bass
from concourse import mybir
from contextlib import ExitStack

NB, S, D = 8, 512, 128
P = 128
NT = S // P
HEADS, HD = 16, 8
GH = 4
GROUPS = HEADS // GH
PARTS = 3
STACK = HD * PARTS * PARTS
NEX, HID = 8, 256
HALVES = HID // P
UNITS = NEX * HALVES
QK = 256
HCH = 4
FCH = 4
EPS = 1e-5
HID_ORDER = (0, 2, 1, 3)
GELU_C, GELU_A = 0.7978845608028654, 0.044715

LAG = {"P": -1, "A": 0, "B": 1, "C": 2}

INSTANCES = {
    ("A", "exp"): [(g, kt, j) for g in range(GROUPS) for kt in range(NT) for j in range(GH)],
    ("A", "max"): [(g, n) for g in range(1, GROUPS) for n in range(16)],
    ("A", "pv"): [(g, kt) for g in range(GROUPS) for kt in range(NT)][:-1],
    ("A", "mparts"): [(g,) for g in range(1, GROUPS)],
    ("A", "mT"): [(g,) for g in range(1, GROUPS)],
    ("A", "mrow"): [(g,) for g in range(1, GROUPS)],
    ("A", "pvs"): [(g,) for g in range(GROUPS - 1)],
    ("A", "pvT"): [(g,) for g in range(GROUPS - 1)],
    ("A", "onorm"): [(g,) for g in range(GROUPS - 1)],
    ("B", "w0"): [(u,) for u in range(UNITS)],
    ("B", "w1"): [(u,) for u in range(UNITS)],
    ("B", "down"): [(e, h) for e in range(NEX) for h in range(2)],
    ("B", "acc"): [(e,) for e in range(1, NEX)],
    ("P", "proj"): [(n,) for n in range(4)],
    ("P", "rot"): [(n,) for n in range(4)],
    ("P", "split"): [(n,) for n in range(2)],
    ("P", "split2"): [(n,) for n in range(2)],
    ("P", "split3"): [(n,) for n in range(2)],
    ("P", "store"): [(n,) for n in range(2)],
    ("P", "stack"): [(g,) for g in range(GROUPS)],
    ("P", "max"): [(0, n) for n in range(16)],
    ("P", "mparts"): [(0,)], ("P", "mT"): [(0,)], ("P", "mrow"): [(0,)],
    ("C", "qk"): [(p,) for p in range(2)],
    ("C", "qkz"): [(p,) for p in range(2)],
    ("C", "qks"): [(p,) for p in range(2)],
    ("C", "qkgb"): [(p,) for p in range(2)],
    ("C", "hid"): [(c,) for c in HID_ORDER],
    ("C", "hids"): [(c,) for c in HID_ORDER],
    ("C", "up"): [(c,) for c in range(FCH)],
    ("C", "dn"): [(h,) for h in range(2)],
    ("C", "fin"): [(h,) for h in range(2)],
    ("C", "upa"): [(c,) for c in range(FCH)],
    ("C", "upg"): [(c,) for c in range(FCH)],
}

SLOTS = {
    ("P", "load"): dict(sp=(-248.2,)),
    ("P", "stats"): dict(dve=(2.95,)),
    ("P", "rstd"): dict(pool=(-44.9,)),
    ("P", "xn"): dict(act=(4.1,)),
    ("P", "xT"): dict(pe=(13.65,)),
    ("P", "hT"): dict(act=(13.7,)),
    ("P", "lo"): dict(pool=(17.2,)),
    ("P", "proj"): dict(pe=(28.35, 1.24)),
    ("P", "rot"): dict(dve=(28.55, 1.14)),
    ("P", "v"): dict(pe=(34.4,), act=(36.7,)),
    ("P", "split"): dict(pool=(31.1, 29.3), act=(30.9, 6.7)),
    ("P", "split2"): dict(pool=(39.05, 26.12), act=(31.9, 9.61)),
    ("P", "split3"): dict(pool=(58.8, 36.75)),
    ("P", "store"): dict(sp=(178.95, 1.26)),
    ("P", "stack"): dict(sp=(183.6, 27.82)),
    ("P", "max"): dict(pe=(46.4, 1.01), dve=(46.4, 0.96)),
    ("P", "mparts"): dict(dve=(67.35,)),
    ("P", "mT"): dict(pe=(216.5,)),
    ("P", "mrow"): dict(sp=(262.25,), act=(170.45,)),
    ("A", "exp"): dict(pe=(-0.3, 1.03), act=(-0.2, 1.03)),
    ("A", "max"): dict(pe=(-0.9, 1), dve=(-0.7, 0.99)),
    ("A", "pv"): dict(pe=(3.6, 4.15)),
    ("A", "mparts"): dict(dve=(15.1, 15.46)),
    ("A", "mT"): dict(pe=(15.25, 15.86)),
    ("A", "mrow"): dict(sp=(94.95, 48.17), act=(15.1, 15.6)),
    ("A", "pvs"): dict(act=(15.8, 17.11)),
    ("A", "pvT"): dict(pe=(17.15, 17.09)),
    ("A", "onorm"): dict(dve=(17.15, 17.21)),
    ("A", "load"): dict(sp=(-104.1,)),
    ("A", "vcopy"): dict(pool=(-114.6,)),
    ("A", "wog"): dict(dve=(263.15,)),
    ("B", "load"): dict(sp=(-265.3,)),
    ("B", "pvlast"): dict(pe=(-310.85,)),
    ("B", "pvs3"): dict(act=(-137.1,)),
    ("B", "pvT3"): dict(pe=(-208.05,)),
    ("B", "onorm3"): dict(dve=(-0.2,)),
    ("B", "oT"): dict(pe=(0.55,)),
    ("B", "ot"): dict(act=(-44.4,)),
    ("B", "y"): dict(pe=(5.6,)),
    ("B", "x1"): dict(dve=(7.2,)),
    ("B", "stats"): dict(dve=(7.55,)),
    ("B", "rstd"): dict(pool=(-38.2,)),
    ("B", "xn"): dict(act=(10.05,)),
    ("B", "xT"): dict(pe=(11.05,)),
    ("B", "hT"): dict(act=(11.7,)),
    ("B", "lo"): dict(pool=(-11.75,)),
    ("B", "gate"): dict(pe=(14.3,)),
    ("B", "logits"): dict(dve=(14.8,)),
    ("B", "top"): dict(dve=(15.45,)),
    ("B", "route"): dict(act=(18,)),
    ("B", "weights"): dict(dve=(24.3,)),
    ("B", "w0"): dict(pe=(16.8, 2.85), act=(16.55, 2.9), dve=(18.25, 2.78)),
    ("B", "w1"): dict(pe=(18.55, 2.77), dve=(19.45, 2.75)),
    ("B", "down"): dict(pe=(24.7, 2.83), act=(24.9, 2.81)),
    ("B", "acc"): dict(pool=(64.7, 19.37)),
    ("B", "x2"): dict(dve=(264.5,)),
    ("C", "load"): dict(sp=(-144.5,)),
    ("C", "loadu"): dict(sp=(-43,)),
    ("C", "loadd"): dict(sp=(11.5,)),
    ("C", "stats"): dict(dve=(0.55,)),
    ("C", "rstd"): dict(pool=(-93.7,)),
    ("C", "xn"): dict(act=(3.3,)),
    ("C", "mod"): dict(dve=(4.6,)),
    ("C", "stats2"): dict(dve=(5.4,)),
    ("C", "rstd2"): dict(pool=(-38.7,)),
    ("C", "xn2"): dict(act=(7.45,)),
    ("C", "xT"): dict(pe=(9.15,)),
    ("C", "nT"): dict(act=(11.6,)),
    ("C", "lo"): dict(pool=(14.05,)),
    ("C", "qk"): dict(pe=(12.9, 2.79)),
    ("C", "qkz"): dict(act=(11.95, 3.71), dve=(12.25, 3.04)),
    ("C", "qks"): dict(dve=(13.8, 2.24)),
    ("C", "qkgb"): dict(pool=(-2.4, 27.41), dve=(15.25, 1.16)),
    ("C", "hid"): dict(pe=(17.95, 1.74), act=(18, 1.84)),
    ("C", "hids"): dict(dve=(19, 2.08)),
    ("C", "sim"): dict(pe=(25.1,)),
    ("C", "simmax"): dict(dve=(25.35,)),
    ("C", "simexp"): dict(act=(27.25,)),
    ("C", "simsum"): dict(dve=(28.2,)),
    ("C", "out"): dict(pe=(32.3,)),
    ("C", "res"): dict(dve=(32.55,)),
    ("C", "stats3"): dict(dve=(35.35,)),
    ("C", "rstd3"): dict(pool=(65.05,)),
    ("C", "xn3"): dict(act=(37.8,)),
    ("C", "xT3"): dict(pe=(39.3,)),
    ("C", "nT3"): dict(act=(40.3,)),
    ("C", "up"): dict(pe=(43.4, 2.89), act=(43.65, 2.94)),
    ("C", "upa"): dict(dve=(44.75, 2.83)),
    ("C", "upg"): dict(act=(44.75, 3.61), dve=(45.5, 3.28)),
    ("C", "dn"): dict(pe=(66, 2.88)),
    ("C", "fin"): dict(dve=(129.25, 68.73)),
    ("C", "outp"): dict(sp=(307.8,)),
}


def order_of(engine):
    at = []
    for (stage, step), slots in SLOTS.items():
        if engine in slots:
            first, *every = slots[engine]
            for n, args in enumerate(INSTANCES.get((stage, step), [()])):
                at.append((first + n * (every[0] if every else 0), len(at), stage, step, args))
    return [(stage, step, args) for _, _, stage, step, args in sorted(at)]


M0_USES = {
    ("A", "mT"): ("a_mrow", lambda g: g + 1), ("P", "mT"): ("a_mrow", lambda g: g + 1),
    ("A", "pvT"): ("a_o", lambda g: g + 1), ("B", "pvT3"): ("a_o", lambda: GROUPS),
    ("B", "oT"): ("a_ot", lambda: 1), ("B", "y"): ("a_x1", lambda: 1),
    ("B", "xT"): ("b_hi", lambda: 1), ("B", "gate"): ("b_lg", lambda: 1),
    ("B", "down"): ("b_sc", lambda e, h: 2 * e + h + 1),
}
M1_USES = {
    ("P", "xT"): ("p_hi", lambda: 1), ("P", "proj"): ("p_rot", lambda n: n + 1), ("P", "v"): ("p_vn", lambda: 1),
    ("C", "xT"): ("c_hi", lambda: 1), ("C", "qk"): ("c_qz", lambda p: p + 1),
    ("C", "hid"): ("c_hz", lambda c: HID_ORDER.index(c) + 1), ("C", "sim"): ("c_ea", lambda: 2),
    ("C", "out"): ("c_o1", lambda: 1), ("C", "xT3"): ("c_nT3", lambda: 1), ("C", "up"): ("c_u2", lambda c: c + 1),
    ("C", "dn"): ("c_y1", lambda h: h + 1),
}

PER_BATCH = {
    "p_nm": 1, "b_nm": 1, "c_nm1": 1, "c_nm2": 1, "c_nm3": 1,
    "p_in": 16, "p_inm": 16, "p_mv": 1, "p_eps": 2, "p_rstd": 1, "p_xn": 1, "p_xT": 1, "p_hT": 1, "p_hi": 1, "p_lo": 1,
    "p_proj": 4, "p_rot": 4, "p_v": 1, "p_vn": 1, "p_sum": 2, "p_part0": 2, "p_rem": 2, "p_part1": 2, "p_part2": 2,
    "p_stored0": 16, "p_stored1": 16 * PARTS, "p_stack0": 32, "p_stack1": 32, "p_stack2": 32, "p_stack3": 32,
    "a_in": 16, "a_xin": 16, "a_wog": 1, "a_vc": 1, "a_smf": 64, "a_max": 64, "a_mp": 4 * GROUPS, "a_mT": GROUPS,
    "a_mrow": GROUPS,
    "a_row": 16 * PARTS * GROUPS, "a_sef": 64, "a_exp": 64, "a_pv": 16, "a_pvs": GROUPS, "a_pvT": GROUPS,
    "a_rc": GROUPS, "a_o": GROUPS, "a_oT": 1, "a_ot": 1, "a_y": 1, "a_x1": 1,
    "b_in": 32, "b_mv": 1, "b_eps": 2, "b_rstd": 1, "b_xn": 1, "b_xT": 1, "b_hT": 1, "b_hi": 1, "b_lo": 1,
    "b_gate": 1, "b_lg": 1, "b_top": 1, "b_dif": 1, "b_e2": 1, "b_route": 7, "b_w0": UNITS, "b_w1": UNITS,
    "b_tanh": UNITS, "b_u": UNITS, "b_mu": UNITS, "b_down": 2 * NEX, "b_sc": 2 * NEX, "b_acc": NEX - 1, "b_t": 1,
    "b_x2": 1,
    "c_in": 16, "c_inu": 48, "c_ind": 48, "c_mv": 1, "c_eps": 2, "c_rstd": 1, "c_xn": 1, "c_m1": 1, "c_h": 1,
    "c_mv2": 1, "c_eps2": 2,
    "c_rstd2": 1, "c_xn2": 1, "c_xT": 1, "c_nT": 1, "c_hi": 1, "c_lo": 1, "c_qk": 2, "c_qz": 2, "c_qt": 2,
    "c_qs": 2, "c_g": 2, "c_kq": 2, "c_gk": 2, "c_kk": 2, "c_hp": 4, "c_ht": 4, "c_hz": 4, "c_hs": 4, "c_vg": 2,
    "c_sim": 1, "c_nm": 1,
    "c_nms": 1, "c_ea": 2, "c_r": 1, "c_rs": 1, "c_wo": 1, "c_o": 1, "c_o1": 1, "c_res": 2, "c_x3": 1,
    "c_mv3": 1, "c_eps3": 2, "c_rstd3": 1, "c_xn3": 1, "c_xT3": 1, "c_nT3": 1, "c_up": 4, "c_uz": 4, "c_u2": 4,
    "c_bs": 1, "c_ub": 4, "c_ut": 4, "c_gl": 4,
    "c_dn": 2, "c_y1": 2, "c_yg": 2, "c_out": 2, "c_stored": 16,
}


def adaln_two_layers(nc, a, out):
    dt = mybir.dt
    f32, f32r, bf16, u32 = dt.float32, dt.float32r, dt.bfloat16, dt.uint32
    ALU = mybir.AluOpType
    ACT = mybir.ActivationFunctionType
    AX = mybir.AxisListType.X
    ctx = ExitStack()
    with ctx:
        def sb(name, shape, dtype=f32):
            return ctx.enter_context(nc.sbuf_tensor(name, shape, dtype))

        def bank(name):
            return ctx.enter_context(nc.psum_tensor(name, [P, 512], f32))

        sig = {name: ctx.enter_context(nc.semaphore(name)) for name in PER_BATCH}

        def after(eng, name, b, k):
            value = b * PER_BATCH[name] + k
            if isinstance(value, int) and value <= 0:
                return
            eng.wait_ge(sig[name], value)

        def after_all(eng, *waits):
            counts = [(sig[name], b * PER_BATCH[name] + k) for name, b, k in waits]
            counts = [(s, v if isinstance(v, int) else eng.to_reg(v)) for s, v in counts
                      if not isinstance(v, int) or v > 0]
            eng.wait_ge(s_c, 16 * N_CONST)
            for s, v in counts:
                eng.wait_ge(s, v)

        mod_d = nc.dram_tensor("mod_d", [2, NB, 6 * D], f32).ap()
        parts_d = nc.dram_tensor("parts_d", [2, HEADS, HD, PARTS, PARTS, S], bf16).ap()

        cosT, sinT = sb("cosT", [P, S]), sb("sinT", [P, S])
        ident, identb = sb("ident", [P, P]), sb("identb", [P, P], bf16)
        nhalf = sb("nhalf", [P, NT])
        iota8 = sb("iota8", [P, NEX])
        wp_hi, wp_lo = sb("wp_hi", [P, 5, P], f32r), sb("wp_lo", [P, 5, P], f32r)
        wo0T = sb("wo0T", [P, D])
        e0_hi, e0_lo = sb("e0_hi", [P, NEX * HID], f32r), sb("e0_lo", [P, NEX * HID], f32r)
        e1_hi, e1_lo = sb("e1_hi", [P, NEX * HID], f32r), sb("e1_lo", [P, NEX * HID], f32r)
        eo = sb("eo", [P, NEX, HALVES, D])
        gate_w = sb("gate_w", [P, NEX])
        wh_hi, wh_lo = sb("wh_hi", [P, HCH * P], f32r), sb("wh_lo", [P, HCH * P], f32r)
        wqk = sb("wqk", [P, QK])
        bh, bhh = sb("bh", [P, HCH]), sb("bhh", [P, HCH])
        bqk = sb("bqk", [P, QK])
        gam, bet = sb("gam", [P, 2, QK]), sb("bet", [P, 2, QK])
        ln_gb = sb("ln_gb", [P, 2])
        wout = sb("wout", [P, 2, D])
        bout = sb("bout", [P, D])

        xp = sb("xp", [P, NT, D])
        xpn = xp
        hp = xpn[:, :, :].rearrange("p t d -> p (t d)")
        hp_hi, hp_lo = sb("hp_hi", [P, S], f32r), sb("hp_lo", [P, S], f32r)
        pmod = sb("pmod", [P, 2])
        rot1, rot2, rem = sb("rot1", [P, S]), sb("rot2", [P, S]), sb("rem", [P, S])
        parts = sb("parts", [P, PARTS, S], bf16)
        vtok = sb("vtok", [P, NT, D])
        qs, ks = sb("qs", [STACK + PARTS, HEADS, S], bf16), sb("ks", [STACK + PARTS, HEADS, S], bf16)
        vaug = sb("vaug", [P, NT, HEADS, 32])
        probs = sb("probs", [P, 2, GH, S])
        ga = sb("ga", [P, D])
        wog = ga
        negmax, mrem = sb("negmax", [P, 2, 16]), sb("mrem", [P, 16])
        mpart = sb("mpart", [P, PARTS, 16], bf16)
        mrow = sb("mrow", [PARTS * 16, P], bf16)
        pvs, rsum, otok, x1 = sb("pvs", [P, S]), sb("rsum", [P, 16]), sb("otok", [P, NT, D]), sb("x1", [P, NT, D])
        oT = pvs
        xbn = sb("xbn", [P, NT, D])
        hb = xbn[:, :, :].rearrange("p t d -> p (t d)")
        hb_hi, hb_lo = sb("hb_hi", [P, S], f32r), sb("hb_lo", [P, S], f32r)
        bmod, gb0 = sb("bmod", [P, 2]), sb("gb0", [P, D])
        logits, top, topi = sb("logits", [P, NT, NEX]), sb("top", [P, NT, 8]), sb("topi", [P, NT, 8], u32)
        pick = sb("pick", [P, 6, NT, NEX])
        pw = sb("pw", [P, 5, NT, 1])
        th = sb("th", [P, S])
        mu = sb("mu", [P, 4, S])
        acc, scaled, x2 = sb("acc", [P, NT, D]), sb("scaled", [P, NT, D]), sb("x2", [P, NT, D])
        cmod, crow, cgb = sb("cmod", [P, 2]), sb("crow", [P, 3, D]), sb("cgb", [P, D])
        b1, b1s, b2 = sb("b1", [P, FCH]), sb("b1s", [P, FCH]), sb("b2", [P, D])
        w1, w2 = sb("w1", [P, FCH * P]), sb("w2", [P, FCH, D])
        xcn, hc = sb("xcn", [P, NT, D]), sb("hc", [P, NT, D])
        xdn, x3 = sb("xdn", [P, NT, D]), sb("x3", [P, NT, D])
        nt, nt3 = (z[:, :, :].rearrange("p t d -> p (t d)") for z in (xcn, xdn))
        n_hi, n_lo = sb("n_hi", [P, S], f32r), sb("n_lo", [P, S], f32r)
        qz, qt = sb("qz", [P, 2, QK]), sb("qt", [P, 2, QK])
        sil = [z[:, :, :].rearrange("p n c -> p (n c)") for z in (qz, qt)]
        kq = sb("kq", [P, 2, NT, QK])
        gl = kq[:, :, :, :].rearrange("p a t n -> p (a t n)").rearrange("p (c s) -> p c s", c=FCH)
        vg = sb("vg", [P, 2, S])
        cst = sb("cst", [P, 5, 2])
        wos = sb("wos", [P, 2, D])
        tc, tc3, yout = xcn, xdn, x3
        uz, u2 = sb("uz", [P, S]), sb("u2", [P, S])
        hth, hz = u2, uz
        ea = u2[:, :].rearrange("p (n c) -> p n c", n=2)
        stats = {n: sb(f"stats_{n}", [P, NT, 6]) for n in "pbcd"}
        mv = {n: sb(f"mv_{n}", [P, NT, 2]) for n in "pbcd"}
        rstd = {n: sb(f"rstd_{n}", [P, NT]) for n in "pbcd"}
        shift_n = {n: sb(f"shift_{n}", [P, NT]) for n in "pbcd"}

        sm = bank("scores_for_max")
        se = [bank("scores0"), bank("scores1")]
        pv = bank("weighted_values")
        w0p, w1p = bank("expert_gate"), bank("expert_up")
        m0, m1 = bank("shared_ab"), bank("shared_pc")

        s_c = ctx.enter_context(nc.semaphore("constants_loaded"))
        s_c2 = ctx.enter_context(nc.semaphore("late_constants_loaded"))
        s_sx = ctx.enter_context(nc.semaphore("setup_pe"))
        s_sv = ctx.enter_context(nc.semaphore("setup_vector"))
        s_sa = ctx.enter_context(nc.semaphore("setup_scalar"))
        s_sg = ctx.enter_context(nc.semaphore("setup_gpsimd"))
        s_md = ctx.enter_context(nc.semaphore("mod_stored"))
        s_ones = ctx.enter_context(nc.semaphore("ones_rows_loaded"))

        raw0 = probs[:, :, :, :].rearrange("p a g s -> p (a g s)")[:, 0:2048]
        raw1 = probs[:, :, :, :].rearrange("p a g s -> p (a g s)")[:, 2048:4096]
        raw_qkv = x1
        raw_h = otok[:, :, :].rearrange("p t d -> p (t d)")
        rawc = [acc[:, 0, 0:NB], acc[:, 1, 0:NB]]
        tanc = [acc[:, 2, 0:NB], acc[:, 3, 0:NB]]
        silc = [acc[:, 0, 64:64 + NB], acc[:, 1, 64:64 + NB]]
        wmod = [kq[:, 0, :, :].rearrange("p t n -> p (t n)")[:, 0:6 * D],
                kq[:, 1, :, :].rearrange("p t n -> p (t n)")[:, 0:6 * D]]
        mu_f = mu[:, :, :].rearrange("p a s -> p (a s)")
        modr = [mu_f[0:NB, L * 2 * S:L * 2 * S + 6 * D] for L in range(2)]
        modt = [scaled[0:NB, 0:2, :].rearrange("p t d -> p (t d)"), th[0:NB, 0:2 * D]]
        wqT, w2T = x2, hc

        x_d = a["L0_attn_x"].rearrange("b (t p) d -> b p t d", p=P)
        out_d = out.rearrange("b (t p) d -> b p t d", p=P)

        block = ctx.enter_context(nc.Block())

        def walk(eng, name, do, hooks, ready):
            begin = min(LAG.values())
            order, todo = order_of(name), dict(hooks)
            assert set(do) == {(stage, step) for stage, step, _ in order}

            def iteration(i, live):
                at = {s: i - LAG[s] for s in live}
                for stage, step, args in order:
                    if stage in live:
                        if i is begin and (stage, step) in todo:
                            todo.pop((stage, step))()
                        do[stage, step](at[stage], *args)
                if i is begin:
                    ready()

            def alive(i):
                return [s for s in LAG if 0 <= i - LAG[s] < NB]

            first = max(LAG.values()) + 1
            last = NB + min(LAG.values())
            for i in range(begin, first):
                iteration(i, alive(i))
            with eng.Fori(first, last) as i:
                iteration(i, list(LAG))
            for i in range(last, NB + max(LAG.values())):
                iteration(i, alive(i))

        def bank_waits(uses, b, stage, step, *args):
            waits = []
            seq = [(s, n, g) for s, n, g in order_of("pe") if (s, n) in uses]
            at = seq.index((stage, step, args))
            i = b + LAG[stage]
            before = seq[:at]
            if not isinstance(i, int):
                live = [before[-1]] if before else []
            else:
                live = [u for u in before if 0 <= i - LAG[u[0]] < NB][-1:]
            for s, n, g in live:
                name, count = uses[s, n]
                waits.append((name, i - LAG[s], count(*g)))
            if not live:
                for s in {u[0] for u in seq}:
                    prior = [u for u in seq if u[0] == s][-1]
                    name, count = uses[s, prior[1]]
                    pb = i - 1 - LAG[s]
                    if isinstance(pb, int) and not 0 <= pb < NB:
                        if pb < 0:
                            continue
                        pb = NB - 1
                    waits.append((name, pb, count(*prior[2])))
            return waits

        def bank_free(eng, uses, b, stage, step, *args):
            for wait in bank_waits(uses, b, stage, step, *args):
                after(eng, *wait)

        def mm3(out_ap, w_hi, w_lo, x_hi, x_lo):
            nc.tensor.matmul(out_ap, w_lo, x_hi, start=True, stop=False)
            nc.tensor.matmul(out_ap, w_hi, x_lo, start=False, stop=False)
            return nc.tensor.matmul(out_ap, w_hi, x_hi, start=False, stop=True)

        def as_f32(ap):
            return ap.bitcast(f32)


        @block.sync
        def _(sp):
            count = [0, 0]

            def const(dst, src, late=0, **kw):
                sp.dma_start(dst, src, **kw).then_inc((s_c, s_c2)[late], 16)
                count[late] += 1

            for L in range(2):
                with nc.allow_non_contiguous_dma("column forms of small vectors"):
                    const(rawc[L], a[f"L{L}_c"].rearrange("b d -> d b"), allow_slow_non_contiguous=True)
                const(wmod[L], a[f"L{L}_wmod"])
            const(ident[:, :], a["ident"])
            rows = a["L0_attn_w_qkv"].rearrange("(h c d) i -> c h d i", c=3, d=HD)
            for c in range(3):
                const(raw_qkv[:, c, :], rows[c])
            const(raw_qkv[:, 3, :], a["L0_attn_w_out"])
            const(nhalf[:, :], a["nhalf"])
            const(cosT[:, :], a["cosT"])
            const(sinT[:, :], a["sinT"])
            assert count[0] == N_CONST, count[0]

            def late_loads():
                def const2(dst, src, **kw):
                    const(dst, src, 1, **kw)

                row = lambda name: a[name].rearrange("(o n) -> o n", o=1)
                const2(raw0.rearrange("p (e h) -> p e h", e=NEX), a["L0_ffn_w0_kernel"].rearrange("e p h -> p e h"))
                const2(raw1.rearrange("p (e h) -> p e h", e=NEX), a["L0_ffn_w1_kernel"].rearrange("e p h -> p e h"))
                const2(raw_h, a["L1_attn_W_hidden"])
                const2(bh[:, :], a["L1_attn_b_hidden"].rearrange("(c p) -> p c", p=P), allow_slow_non_contiguous=True)
                for n in range(2):
                    const2(gam[:, n, :], a["L1_attn_os_gamma"][n:n + 1, :].to_broadcast([P, QK]))
                    const2(bet[:, n, :], a["L1_attn_os_beta"][n:n + 1, :].to_broadcast([P, QK]))
                const2(iota8[:, :], a["iota8"])
                const2(gate_w[:, :], a["L0_ffn_gate_kernel"])
                const2(eo[:, :, :, :], a["L0_ffn_wo_kernel"].rearrange("e (f p) d -> p e f d", p=P))
                const2(wqk[:, :], a["L1_attn_W_qk"])
                const2(bqk[:, :], row("L1_attn_b_qk").to_broadcast([P, QK]))
                const2(ln_gb[:, 0:1], a["L1_attn_ln_g"].rearrange("(p o) -> p o", o=1))
                const2(ln_gb[:, 1:2], a["L1_attn_ln_b"].rearrange("(p o) -> p o", o=1))
                const2(wout[:, :, :], a["L1_attn_W_out"].rearrange("(c p) d -> p c d", p=P))
                const2(bout[:, :], row("L1_attn_b_out").to_broadcast([P, D]))
                assert count[1] == N_LATE, count[1]
                sp.wait_ge(s_sv, SV_ONES)
                for n in range(PARTS):
                    sp.dma_start(ks[STACK + n:STACK + n + 1, :, :], parts[0:HEADS, n, :]).then_inc(s_ones, 16)
                mod_store(0)

            def mod_store(L):
                sp.wait_ge(s_sv, SV_MOD[L])
                sp.dma_start(mod_d[L], modr[L]).then_inc(s_md, 16)
                sp.wait_ge(s_md, 16 * (L + 1))

            def ready():
                mod_store(1)
                sp.wait_ge(s_sv, SV_END)
                sp.wait_ge(s_sa, SA_END)
                sp.wait_ge(s_sg, SG_END)
                sp.wait_ge(s_sx, SX_END)

            def mod_cols(L, b, n):
                return mod_d[L, b, n * D:(n + 2) * D].rearrange("(n d) -> d n", d=D)

            def mod_row(L, b, n):
                return mod_d[L, b, n * D:(n + 1) * D].rearrange("(o d) -> o d", o=1).to_broadcast([P, D])

            def p_load(b):
                after_all(sp, ("p_lo", b - 1, 1))
                sp.dma_start(xp[:, :, :], x_d[b]).then_inc(sig["p_in"], 16)
                if isinstance(b, int) and b == 0:
                    late_loads()
                after_all(sp, ("p_hT", b - 1, 1))
                sp.dma_start(pmod[:, :], mod_cols(0, b, 0), allow_slow_non_contiguous=True)\
                    .then_inc(sig["p_inm"], 16)

            def p_store(b, which):
                after_all(sp, ("p_part2", b, which + 1))
                if which == 1:
                    for n in range(PARTS):
                        sp.dma_start(parts_d[1].rearrange("h d a b s -> (h d) a b s")[:, :, n, :],
                                     parts[:, :, :]).then_inc(sig["p_stored1"], 16)
                    return
                after_all(sp, *((f"p_stack{g}", b - 1, 32) for g in range(GROUPS)))
                sp.dma_start(parts_d[0].rearrange("h d a b s -> (h d) a b s"),
                             parts[:, :, :].unsqueeze(1).to_broadcast([P, PARTS, PARTS, S]))\
                    .then_inc(sig["p_stored0"], 16)

            def p_stack(b, g):
                after_all(sp, ("p_stored0", b, 16), ("p_stored1", b, 16 * PARTS), ("a_sef", b - 1, 16 * (g + 1)))
                for n, dst in enumerate((qs, ks)):
                    sp.dma_start(dst[0:STACK, GH * g:GH * (g + 1), :],
                                 parts_d[n, GH * g:GH * (g + 1)].rearrange("h d a b s -> (d a b) h s"))\
                        .then_inc(sig[f"p_stack{g}"], 16)

            def a_load(b):
                after_all(sp, ("a_y", b - 1, 1))
                sp.dma_start(ga[:, :], mod_row(0, b, 2)).then_inc(sig["a_in"], 16)

            def mrow_out(b, g):
                after_all(sp, ("a_mrow", b, g + 1))
                for n in range(PARTS):
                    sp.dma_start(qs[STACK + n:STACK + n + 1, GH * g:GH * (g + 1), :]
                                 .rearrange("o h (t s) -> o (h t) s", s=P),
                                 mrow[16 * n:16 * n + 16, :]).then_inc(sig["a_row"], 16)

            def b_load(b):
                after_all(sp, ("b_hT", b - 1, 1))
                sp.dma_start(bmod[:, :], mod_cols(0, b, 3), allow_slow_non_contiguous=True)\
                    .then_inc(sig["b_in"], 16)
                after_all(sp, ("b_x2", b - 1, 1))
                sp.dma_start(x1[:, :, :], x_d[b]).then_inc(sig["a_xin"], 16)
                sp.dma_start(gb0[:, :], mod_row(0, b, 5)).then_inc(sig["b_in"], 16)

            def c_load(b):
                after_all(sp, ("c_res", b - 1, 2))
                sp.dma_start(crow[:, :, :].rearrange("p n d -> p (n d)"), mod_d[1, b, 0:3 * D]
                             .rearrange("(o d) -> o d", o=1).to_broadcast([P, 3 * D])).then_inc(sig["c_in"], 16)

            def c_loadu(b):
                after_all(sp, ("c_u2", b - 1, FCH))
                sp.dma_start(cmod[:, :], mod_cols(1, b, 3), allow_slow_non_contiguous=True)\
                    .then_inc(sig["c_inu"], 16)
                sp.dma_start(b1[:, :], a["L1_ffn_b1"][b].rearrange("(c p) -> p c", p=P),
                             allow_slow_non_contiguous=True).then_inc(sig["c_inu"], 16)
                sp.dma_start(w1[:, :], a["L1_ffn_w1"][b]).then_inc(sig["c_inu"], 16)

            def c_loadd(b):
                after_all(sp, ("c_yg", b - 1, 2))
                sp.dma_start(cgb[:, :], mod_row(1, b, 5)).then_inc(sig["c_ind"], 16)
                sp.dma_start(b2[:, :], a["L1_ffn_b2"][b].rearrange("(o d) -> o d", o=1).to_broadcast([P, D]))\
                    .then_inc(sig["c_ind"], 16)
                sp.dma_start(w2[:, :, :], a["L1_ffn_w2"][b].rearrange("(c p) d -> p c d", p=P))\
                    .then_inc(sig["c_ind"], 16)

            def c_outp(b):
                after_all(sp, ("c_out", b, 2))
                sp.dma_start(out_d[b], yout[:, :, :]).then_inc(sig["c_stored"], 16)

            walk(sp, "sp", {("P", "load"): p_load, ("P", "store"): p_store, ("P", "stack"): p_stack,
                      ("P", "mrow"): mrow_out, ("A", "load"): a_load, ("A", "mrow"): mrow_out,
                      ("B", "load"): b_load, ("C", "load"): c_load, ("C", "loadu"): c_loadu, ("C", "loadd"): c_loadd,
                      ("C", "outp"): c_outp},
                 {}, ready)
            sp.wait_ge(sig["c_stored"], 16 * NB)

        @block.tensor
        def _(pe):
            pe.wait_ge(s_c, 16 * N_CONST)
            for n in range(4):
                last = nc.tensor.transpose(m0[:, n * P:(n + 1) * P], raw_qkv[:, n, :], ident[:, :])
            last.then_inc(s_sx, 1)
            pe.wait_ge(s_sv, SV_SILU)
            for L in range(2):
                for half in range(2):
                    dst = (w0p, w1p, se[0], se[1])[2 * L + half]
                    last = nc.tensor.matmul(dst[0:NB, 0:3 * D], silc[L], wmod[L][:, half * 3 * D:(half + 1) * 3 * D],
                                            start=True, stop=True)
            last.then_inc(s_sx, 1)

            def weights_ready():
                pe.wait_ge(s_sv, SV_SPLIT)

            def ready():
                pe.wait_ge(s_c2, 16 * N_LATE)
                pe.wait_ge(s_sv, SV_END)
                pe.wait_ge(s_sa, SA_END)
                pe.wait_ge(s_sg, SG_END)
                pe.wait_ge(s_ones, 16 * PARTS)

            def transposes(bank_ap, src, name, wait, uses, *step):
                def run(b, *g):
                    after(pe, wait[0], b, wait[1] + (g[0] if g else 0))
                    bank_free(pe, uses, b, *step, *g)
                    for t in range(NT):
                        last = nc.tensor.transpose(bank_ap[:, t * P:(t + 1) * P], src[:, t, :], ident[:, :])
                    last.then_inc(sig[name], 1)
                return run

            p_xT = transposes(m1, xpn, "p_xT", ("p_xn", 1), M1_USES, "P", "xT")
            b_xT = transposes(m0, xbn, "b_xT", ("b_xn", 1), M0_USES, "B", "xT")
            c_xT = transposes(m1, xcn, "c_xT", ("c_xn2", 1), M1_USES, "C", "xT")
            c_xT3 = transposes(m1, xdn, "c_xT3", ("c_xn3", 1), M1_USES, "C", "xT3")
            oT_t = transposes(m0, otok, "a_oT", ("a_o", GROUPS), M0_USES, "B", "oT")
            pvs4 = pvs[:, :].rearrange("p (t q) -> p t q", t=NT)

            def proj(b, n):
                after(pe, "p_lo", b, 1)
                bank_free(pe, M1_USES, b, "P", "proj", n)
                mm3(m1[:, :], wp_hi[:, n, :], wp_lo[:, n, :], hp_hi[:, :], hp_lo[:, :]).then_inc(sig["p_proj"], 1)

            def v(b):
                bank_free(pe, M1_USES, b, "P", "v")
                for t in range(NT):
                    at = slice(t * P, (t + 1) * P)
                    last = mm3(m1[:, at], hp_hi[:, at], hp_lo[:, at], wp_hi[:, 4, :], wp_lo[:, 4, :])
                last.then_inc(sig["p_v"], 1)

            def smax(b, g, n):
                h, t = GH * g + n // NT, n % NT
                if n == 0:
                    after(pe, f"p_stack{g}", b, 32)
                after(pe, "a_max", b, 16 * g + n)
                nc.tensor.matmul(sm[:, :], qs[0:STACK, h, t * P:(t + 1) * P], ks[0:STACK, h, :],
                                 start=True, stop=True).then_inc(sig["a_smf"], 1)

            def mT(stage):
                def run(b, g):
                    after_all(pe, ("a_mp", b, 4 * (g + 1)), *bank_waits(M0_USES, b, stage, "mT", g))
                    nc.tensor.transpose(m0[0:PARTS * 16, 0:P // 2].bitcast(bf16),
                                        mpart[:, :, :].rearrange("p n c -> p (n c)"),
                                        identb[:, :]).then_inc(sig["a_mT"], 1)
                return run

            def sexp(b, g, kt, j):
                n = 16 * g + 4 * kt + j
                if n % 16 == 0:
                    after(pe, "a_row", b, 16 * PARTS * (g + 1))
                after(pe, "a_exp", b, max(n - 1, 0))
                h = GH * g + j
                nc.tensor.matmul(se[n % 2][:, :], ks[:, h, kt * P:(kt + 1) * P], qs[:, h, :],
                                 start=True, stop=True).then_inc(sig["a_sef"], 1)

            def pvm(b, g, kt):
                if kt == 0:
                    after(pe, "a_pvs", b, g)
                    after(pe, "a_vc", b, 1)
                after(pe, "a_exp", b, 16 * g + 4 * kt + 4)
                for j in range(GH):
                    last = nc.tensor.matmul(pv[32 * j:32 * j + 32, :], vaug[:, kt, GH * g + j, :],
                                            probs[:, kt % 2, j, :], start=(kt == 0), stop=(kt == NT - 1))
                last.then_inc(sig["a_pv"], 1)

            def pvT(stage, step):
                def run(b, *g):
                    n = g[0] if g else GROUPS - 1
                    after(pe, "a_pvs", b, n + 1)
                    bank_free(pe, M0_USES, b, stage, step, *g)
                    for t in range(NT):
                        last = nc.tensor.transpose(m0[:, t * P:(t + 1) * P], pvs4[:, t, :], ident[:, :])
                    last.then_inc(sig["a_pvT"], 1)
                return run

            def y(b):
                after(pe, "a_ot", b, 1)
                after(pe, "a_wog", b, 1)
                bank_free(pe, M0_USES, b, "B", "y")
                for t in range(NT):
                    at = slice(t * P, (t + 1) * P)
                    last = nc.tensor.matmul(m0[:, at], oT[:, at], wog[:, :], start=True, stop=True)
                last.then_inc(sig["a_y"], 1)

            def gate(b):
                after(pe, "b_hT", b, 1)
                bank_free(pe, M0_USES, b, "B", "gate")
                for t in range(NT):
                    last = nc.tensor.matmul(m0[:, t * NEX:(t + 1) * NEX], hb[:, t * P:(t + 1) * P], gate_w[:, :],
                                            start=True, stop=True)
                last.then_inc(sig["b_gate"], 1)

            def w0(b, u):
                if u == 0:
                    after(pe, "b_lo", b, 1)
                at = slice(u * P, (u + 1) * P)
                after(pe, "b_u", b, u)
                mm3(w0p[:, :], e0_hi[:, at], e0_lo[:, at], hb_hi[:, :], hb_lo[:, :]).then_inc(sig["b_w0"], 1)

            def w1_(b, u):
                at = slice(u * P, (u + 1) * P)
                after(pe, "b_mu", b, u)
                mm3(w1p[:, :], e1_hi[:, at], e1_lo[:, at], hb_hi[:, :], hb_lo[:, :]).then_inc(sig["b_w1"], 1)

            def down(b, e, h):
                after(pe, "b_mu", b, 2 * e + 2)
                bank_free(pe, M0_USES, b, "B", "down", e, h)
                for t in range(2 * h, 2 * h + 2):
                    at = slice(t * P, (t + 1) * P)
                    for f in range(HALVES):
                        last = nc.tensor.matmul(m0[:, at], mu[:, (2 * e + f) % 4, at], eo[:, e, f, :],
                                                start=(f == 0), stop=(f == HALVES - 1))
                last.then_inc(sig["b_down"], 1)

            def qk(b, p):
                after(pe, "c_nT", b, 1)
                bank_free(pe, M1_USES, b, "C", "qk", p)
                for n in range(2):
                    at = slice((2 * p + n) * P, (2 * p + n + 1) * P)
                    last = nc.tensor.matmul(m1[:, n * QK:(n + 1) * QK], nt[:, at], wqk[:, :], start=True, stop=True)
                last.then_inc(sig["c_qk"], 1)

            def hid(b, c):
                after(pe, "c_lo", b, 1)
                bank_free(pe, M1_USES, b, "C", "hid", c)
                at = slice(c * P, (c + 1) * P)
                mm3(m1[:, :], wh_hi[:, at], wh_lo[:, at], n_hi[:, :], n_lo[:, :]).then_inc(sig["c_hp"], 1)

            def sim(b):
                after(pe, "c_kq", b, 2)
                after(pe, "c_kk", b, 2)
                bank_free(pe, M1_USES, b, "C", "sim")
                for n in range(2):
                    for t in range(NT):
                        last = nc.tensor.matmul(m1[:, n * QK:(n + 1) * QK], kq[:, 0, t, n * P:(n + 1) * P],
                                                kq[:, 1, t, :], start=(t == 0), stop=(t == NT - 1))
                last.then_inc(sig["c_sim"], 1)

            def c_out(b):
                after(pe, "c_vg", b, 2)
                after(pe, "c_wo", b, 1)
                bank_free(pe, M1_USES, b, "C", "out")
                for t in range(NT):
                    at = slice(t * P, (t + 1) * P)
                    for n in range(2):
                        last = nc.tensor.matmul(m1[:, at], vg[:, n, at], wos[:, n, :], start=(n == 0), stop=(n == 1))
                last.then_inc(sig["c_o"], 1)

            def up(b, c):
                if c == 0:
                    after(pe, "c_nT3", b, 1)
                    after(pe, "c_inu", b, 48)
                bank_free(pe, M1_USES, b, "C", "up", c)
                at = slice(c * P, (c + 1) * P)
                nc.tensor.matmul(m1[:, :], w1[:, at], nt3, start=True, stop=True).then_inc(sig["c_up"], 1)

            def dn(b, h):
                after(pe, "c_gl", b, FCH)
                after(pe, "c_ind", b, 48)
                bank_free(pe, M1_USES, b, "C", "dn", h)
                for t in range(2 * h, 2 * h + 2):
                    at = slice(t * P, (t + 1) * P)
                    for c in range(FCH):
                        last = nc.tensor.matmul(m1[:, at], gl[:, c, at], w2[:, c, :], start=(c == 0),
                                                stop=(c == FCH - 1))
                last.then_inc(sig["c_dn"], 1)

            walk(pe, "pe", {("P", "xT"): p_xT, ("P", "proj"): proj, ("P", "v"): v, ("P", "max"): smax,
                      ("P", "mT"): mT("P"),
                      ("A", "max"): smax, ("A", "mT"): mT("A"), ("A", "exp"): sexp, ("A", "pv"): pvm,
                      ("A", "pvT"): pvT("A", "pvT"), ("B", "pvlast"): lambda b: pvm(b, GROUPS - 1, NT - 1),
                      ("B", "pvT3"): pvT("B", "pvT3"), ("B", "oT"): oT_t, ("B", "y"): y, ("B", "xT"): b_xT,
                      ("B", "gate"): gate, ("B", "w0"): w0, ("B", "w1"): w1_, ("B", "down"): down, ("C", "xT"): c_xT,
                      ("C", "qk"): qk, ("C", "hid"): hid, ("C", "sim"): sim, ("C", "out"): c_out,
                      ("C", "xT3"): c_xT3, ("C", "up"): up, ("C", "dn"): dn},
                 {("P", "proj"): weights_ready}, ready)

        @block.scalar
        def _(act):
            act.wait_ge(s_c, 16 * N_CONST)
            for L in range(2):
                nc.scalar.activation(tanc[L], rawc[L], ACT.Tanh, scale=0.5).then_inc(s_sa, 1)

            def late():
                act.wait_ge(s_ones, 16 * PARTS)
                act.wait_ge(s_c2, 16 * N_LATE)
                nc.scalar.activation(e0_hi[:, :], raw0, ACT.Copy).then_inc(s_sa, 1)
                nc.scalar.activation(e1_hi[:, :], raw1, ACT.Copy).then_inc(s_sa, 1)
                nc.scalar.activation(wh_hi[:, :], raw_h, ACT.Copy).then_inc(s_sa, 1)
                nc.scalar.activation(bhh[:, :], bh[:, :], ACT.Copy, scale=0.5).then_inc(s_sa, 1)
                for n in range(2):
                    nc.scalar.activation(gam[:, n, :], gam[:, n, :], ACT.Copy, scale=0.5).then_inc(s_sa, 1)

            def ready():
                act.wait_ge(s_sv, SV_END)
                act.wait_ge(s_sg, SG_END)
                act.wait_ge(s_sx, SX_END)

            def copy_in(name, src, dst, wait, free):
                def run(b):
                    after(act, wait, b, 1)
                    after(act, free, b - 1, 1)
                    nc.scalar.activation(dst, src, ACT.Copy).then_inc(sig[name], 1)
                return run

            def modulate(name, src, dst, mod, wait, ready, rounded=None):
                shift, scale = mod
                def run(b):
                    after(act, wait, b, 1)
                    after(act, *ready(b))
                    nc.scalar.activation(dst, src, ACT.Identity, bias=shift, scale=scale).then_inc(sig[name], 1)
                    if rounded:
                        dst_hi, name_hi, free = rounded
                        after(act, *free(b))
                        nc.scalar.activation(dst_hi[:, :], src, ACT.Identity, bias=shift, scale=scale)\
                            .then_inc(sig[name_hi], 1)
                return run

            def normalise(key, src, dst, wait, name, free):
                def run(b):
                    after(act, wait, b, 1)
                    after(act, *free(b))
                    for t in range(NT):
                        last = nc.scalar.activation(dst[:, t, :], src[:, t, :], ACT.Identity,
                                                    bias=shift_n[key][:, t:t + 1], scale=rstd[key][:, t:t + 1])
                    last.then_inc(sig[name], 1)
                return run

            def mrow_in(b, g):
                after(act, "a_mT", b, g + 1)
                after(act, "a_row", b, 16 * PARTS * g)
                nc.scalar.activation(mrow[:, :], m0[0:PARTS * 16, 0:P // 2].bitcast(bf16), ACT.Copy)\
                    .then_inc(sig["a_mrow"], 1)

            def exp(b, g, kt, j):
                n = 16 * g + 4 * kt + j
                after(act, "a_sef", b, n + 1)
                if j == 0:
                    after(act, "a_pv", b, max(4 * g + kt - 1, 0))
                nc.scalar.activation(probs[:, kt % 2, j, :], se[n % 2][:, :], ACT.Exp).then_inc(sig["a_exp"], 1)

            def pvcopy(b, g=GROUPS - 1):
                after(act, "a_pv", b, NT * (g + 1))
                after(act, "a_pvT", b, g)
                nc.scalar.activation(pvs[:, :], pv[:, :], ACT.Copy).then_inc(sig["a_pvs"], 1)

            def vcopy_out(b):
                after(act, "p_v", b, 1)
                after(act, "a_vc", b - 1, 1)
                nc.scalar.activation(vtok[:, :, :].rearrange("p t d -> p (t d)"), m1[:, :], ACT.Copy)\
                    .then_inc(sig["p_vn"], 1)

            def part0(b, n):
                after(act, "p_sum", b, n + 1)
                if n == 1:
                    after(act, "p_stored0", b, 16)
                else:
                    after(act, "p_stored1", b - 1, 16 * PARTS)
                nc.scalar.activation(parts[:, 0, :], rem[:, :], ACT.Copy).then_inc(sig["p_part0"], 1)

            def part1(b, n):
                after(act, "p_rem", b, n + 1)
                nc.scalar.activation(parts[:, 1, :], rem[:, :], ACT.Copy).then_inc(sig["p_part1"], 1)

            def route(b):
                after(act, "b_dif", b, 1)
                nc.scalar.activation(pw[:, 1, :, :], pw[:, 0, :, :], ACT.Exp).then_inc(sig["b_e2"], 1)

            def w0(b, u):
                after(act, "b_w0", b, u + 1)
                after(act, "b_u", b, u)
                nc.scalar.activation(th[:, :], w0p[:, :], ACT.Tanh, scale=0.5).then_inc(sig["b_tanh"], 1)

            def qkt(b, p):
                after(act, "c_qz", b, p + 1)
                after(act, "c_qs", b, p)
                nc.scalar.activation(qt[:, :, :], qz[:, :, :], ACT.Tanh, scale=0.5).then_inc(sig["c_qt"], 1)

            def hid(b, c):
                n = HID_ORDER.index(c)
                after(act, "c_hp", b, n + 1)
                after(act, "c_hs", b, n)
                if n == 0:
                    after(act, "c_gl", b - 1, FCH)
                nc.scalar.activation(hth[:, :], m1[:, :], ACT.Tanh, scale=0.5, bias=bhh[:, c:c + 1])\
                    .then_inc(sig["c_ht"], 1)
                nc.scalar.activation(hz[:, :], m1[:, :], ACT.Identity, bias=bh[:, c:c + 1]).then_inc(sig["c_hz"], 1)

            def simexp(b):
                after(act, "c_nms", b, 1)
                after(act, "c_hs", b, HCH)
                for n in range(2):
                    nc.scalar.activation(ea[:, n, :], m1[:, n * QK:(n + 1) * QK], ACT.Exp, scale=1.0 / S,
                                         bias=cst[:, 1, n:n + 1], accum_out=cst[:, 2, n:n + 1])\
                        .then_inc(sig["c_ea"], 1)

            def up(b, c):
                after(act, "c_up", b, c + 1)
                after(act, "c_gl", b, c)
                if c == 0:
                    after(act, "c_wo", b, 1)
                    after(act, "c_u2", b - 1, FCH)
                    nc.scalar.activation(b1s[:, :], b1[:, :], ACT.Copy, scale=GELU_A ** 0.5).then_inc(sig["c_bs"], 1)
                nc.scalar.activation(uz[:, :], m1[:, :], ACT.Identity, bias=b1[:, c:c + 1]).then_inc(sig["c_uz"], 1)
                after(act, "c_bs", b, 1)
                nc.scalar.activation(u2[:, :], m1[:, :], ACT.Square, scale=GELU_A ** 0.5, bias=b1s[:, c:c + 1])\
                    .then_inc(sig["c_u2"], 1)

            def down(b, e, h):
                after(act, "b_down", b, 2 * e + h + 1)
                if e == 0:
                    after(act, "b_route", b, 7)
                    after(act, "b_t", b - 1, 1)
                elif e == 1:
                    after(act, "b_acc", b - 1, NEX - 1)
                else:
                    after(act, "b_acc", b, e - 1)
                for t in range(2 * h, 2 * h + 2):
                    last = nc.scalar.activation((scaled if e else acc)[:, t, :], m0[:, t * D:(t + 1) * D], ACT.Copy,
                                                scale=pick[:, 5, t, e:e + 1])
                last.then_inc(sig["b_sc"], 1)

            def upg(b, c):
                after(act, "c_ub", b, c + 1)
                nc.scalar.activation(u2[:, :], u2[:, :], ACT.Tanh, scale=GELU_C).then_inc(sig["c_ut"], 1)

            walk(act, "act", {
                ("P", "xn"): normalise("p", xp, xpn, "p_nm", "p_xn", lambda b: ("p_mv", b, 1)),
                ("B", "xn"): normalise("b", x1, xbn, "b_nm", "b_xn", lambda b: ("b_gate", b - 1, 1)),
                ("C", "xn"): normalise("c", x2, xcn, "c_nm1", "c_xn", lambda b: ("c_x3", b - 1, 1)),
                ("C", "xn2"): normalise("c", hc, xcn, "c_nm2", "c_xn2", lambda b: ("c_h", b, 1)),
                ("C", "xn3"): normalise("d", x3, xdn, "c_nm3", "c_xn3", lambda b: ("c_out", b - 1, 2)),
                ("P", "hT"): modulate("p_hT", m1[:, :], hp, (pmod[:, 0:1], pmod[:, 1:2]), "p_xT",
                                      lambda b: ("p_inm", b, 16), (hp_hi, "p_hi", lambda b: ("p_v", b - 1, 1))),
                ("P", "split"): part0, ("P", "split2"): part1, ("P", "v"): vcopy_out, ("P", "mrow"): mrow_in,
                ("A", "mrow"): mrow_in, ("A", "exp"): exp,
                ("A", "pvs"): pvcopy, ("B", "pvs3"): pvcopy,
                ("B", "ot"): copy_in("a_ot", m0[:, :], oT[:, :], "a_oT", "a_y"),
                ("B", "hT"): modulate("b_hT", m0[:, :], hb, (bmod[:, 0:1], bmod[:, 1:2]), "b_xT",
                                      lambda b: ("b_in", b, 32), (hb_hi, "b_hi", lambda b: ("b_w1", b - 1, UNITS))),
                ("B", "route"): route, ("B", "w0"): w0, ("B", "down"): down,
                ("C", "nT"): modulate("c_nT", m1[:, :], nt, (ln_gb[:, 1:2], ln_gb[:, 0:1]), "c_xT",
                                      lambda b: ("c_xT", b, 1), (n_hi, "c_hi", lambda b: ("c_hp", b - 1, HCH))),
                ("C", "nT3"): modulate("c_nT3", m1[:, :], nt3, (cmod[:, 0:1], cmod[:, 1:2]), "c_xT3",
                                       lambda b: ("c_inu", b, 48)),
                ("C", "qkz"): qkt, ("C", "hid"): hid, ("C", "simexp"): simexp, ("C", "up"): up, ("C", "upg"): upg},
                 {("P", "v"): late}, ready)

        @block.vector
        def _(dve):
            V = nc.vector
            done = [0]

            def link(ins):
                ins.then_inc(s_sv, 1)
                done[0] += 1
                dve.wait_ge(s_sv, done[0])

            link(V.memset(vaug[:, :, :, :], 0.0))
            link(V.memset(vaug[:, :, :, HD:HD + 1], 1.0))
            link(V.memset(parts[:, :, :], 1.0))
            assert done[0] == SV_ONES
            dve.wait_ge(s_c, 16 * N_CONST)
            link(V.tensor_copy(identb[:, :], ident[:, :]))
            dve.wait_ge(s_sa, 2)
            for L in range(2):
                link(V.scalar_tensor_tensor(out=tanc[L], in0=tanc[L], scalar=1.0, in1=rawc[L], op0=ALU.add,
                                            op1=ALU.mult))
                link(V.tensor_scalar(silc[L], tanc[L], 0.5, None, ALU.mult))
            assert done[0] == SV_SILU
            def mod_rows(L):
                r, t = modr[L], modt[L]
                for half in range(2):
                    link(V.tensor_copy(r[:, half * 3 * D:(half + 1) * 3 * D],
                                       (w0p, w1p, se[0], se[1])[2 * L + half][0:NB, 0:3 * D]))
                for n in (1, 4):
                    link(V.tensor_scalar(r[:, n * D:(n + 1) * D], r[:, n * D:(n + 1) * D], 1.0, None, ALU.add))
                for n in (2, 5):
                    gt, sg = r[:, n * D:(n + 1) * D], t[:, 0:D]
                    mg = t[:, D:2 * D]
                    link(V.tensor_scalar(sg, gt, 0.0, 2.0, ALU.is_ge, ALU.mult))
                    link(V.tensor_scalar(sg, sg, -1.0, None, ALU.add))
                    link(V.tensor_scalar(mg, gt, -1.0, None, ALU.mult))
                    link(V.tensor_tensor(mg, mg, gt, ALU.max))
                    link(V.tensor_scalar(mg, mg, 0.25, None, ALU.max))
                    link(V.tensor_tensor(gt, mg, sg, ALU.mult))
                assert done[0] == SV_MOD[L], (L, done[0])

            def split_weights():
                dve.wait_ge(s_sx, SX_END)
                mod_rows(0)
                link(V.tensor_copy(wqT[:, :, :].rearrange("p n c -> p (n c)"), m0[:, :]))
                link(V.tensor_copy(wo0T[:, :], wqT[:, 3, :]))
                for n in range(2):
                    pair = wqT[:, n, :].rearrange("p (i two) -> p i two", two=2)
                    turned = w2T[:, n, :].rearrange("p (i two) -> p i two", two=2)
                    link(V.tensor_scalar(turned[:, :, 0:1], pair[:, :, 1:2], -1.0, None, ALU.mult))
                    link(V.tensor_copy(turned[:, :, 1:2], pair[:, :, 0:1]))
                for n, src in enumerate((wqT[:, 0, :], w2T[:, 0, :], wqT[:, 1, :], w2T[:, 1, :], wqT[:, 2, :])):
                    link(V.tensor_copy(wp_hi[:, n, :], src))
                    link(V.tensor_tensor(wp_lo[:, n, :], src, as_f32(wp_hi[:, n, :]), ALU.subtract))
                assert done[0] == SV_SPLIT, done[0]

            def late():
                mod_rows(1)
                dve.wait_ge(s_sa, SA_END)
                link(V.tensor_tensor(wh_lo[:, :], raw_h, as_f32(wh_hi[:, :]), ALU.subtract))
                link(V.tensor_tensor(e0_lo[:, :], raw0, as_f32(e0_hi[:, :]), ALU.subtract))
                assert done[0] == SV_END, done[0]

            def ready():
                dve.wait_ge(s_c2, 16 * N_LATE)
                dve.wait_ge(s_sg, SG_END)
                dve.wait_ge(s_md, 32)

            def norm_stats(key, src, wait, name):
                def run(b):
                    for w in wait:
                        after(dve, w[0], b, w[1])
                    for t in range(NT):
                        last = V.bn_stats(stats[key][:, t, :], src[:, t, :])
                    last.then_inc(sig[name + "s"], 1)
                    after_all(dve, (name + "s", b, 1))
                    for t in range(NT):
                        last = V.bn_aggr(mv[key][:, t, :], stats[key][:, t, :])
                    last.then_inc(sig[name], 1)
                return run

            def rot(b, n):
                kind, part = n // 2, n % 2
                after(dve, "p_proj", b, n + 1)
                after(dve, "p_sum", b, kind)
                V.tensor_tensor((rot1, rot2)[part][:, :], m1[:, :], (cosT, sinT)[part][:, :], ALU.mult)\
                    .then_inc(sig["p_rot"], 1)

            def smax(b, g, n):
                after(dve, "a_smf", b, 16 * g + n + 1)
                if n == 0:
                    after(dve, "a_mp", b, max(4 * (g - 1), 0))
                V.tensor_reduce(negmax[:, g % 2, n:n + 1], sm[:, :], AX, ALU.max, negate=True)\
                    .then_inc(sig["a_max"], 1)

            def mparts(b, g):
                nm = negmax[:, g % 2, :]
                after(dve, "a_max", b, 16 * (g + 1))
                after(dve, "a_mT", b, g)
                V.tensor_copy(mpart[:, 0, :], nm).then_inc(sig["a_mp"], 1)
                after(dve, "a_mp", b, 4 * g + 1)
                V.tensor_tensor(mrem[:, :], nm, mpart[:, 0, :], ALU.subtract).then_inc(sig["a_mp"], 1)
                after(dve, "a_mp", b, 4 * g + 2)
                V.tensor_copy(mpart[:, 1, :], mrem[:, :]).then_inc(sig["a_mp"], 1)
                after(dve, "a_mp", b, 4 * g + 3)
                V.tensor_tensor(mpart[:, 2, :], mrem[:, :], mpart[:, 1, :], ALU.subtract).then_inc(sig["a_mp"], 1)

            def onorm(b, g=GROUPS - 1):
                after(dve, "a_pvT", b, g + 1)
                got = m0[:, :].rearrange("p (t j c) -> p t j c", t=NT, j=GH)
                r = rsum[:, :].rearrange("p (t j o) -> p t j o", t=NT, j=GH)
                V.reciprocal(r, got[:, :, :, HD:HD + 1]).then_inc(sig["a_rc"], 1)
                after(dve, "a_rc", b, g + 1)
                if g == 0:
                    after(dve, "a_oT", b - 1, 1)
                V.tensor_tensor(otok[:, :, GH * HD * g:GH * HD * (g + 1)].rearrange("p t (j d) -> p t j d", j=GH),
                                got[:, :, :, 0:HD], r.to_broadcast([P, NT, GH, HD]), ALU.mult)\
                    .then_inc(sig["a_o"], 1)

            def over_t(row):
                return row.unsqueeze(1).to_broadcast([P, NT, D])

            def bank_t(b_):
                return b_[:, :].rearrange("p (t d) -> p t d", t=NT)

            def do_x1(b):
                after(dve, "a_y", b, 1)
                after(dve, "a_xin", b, 16)
                V.tensor_tensor(x1[:, :, :], bank_t(m0), x1[:, :, :], ALU.add).then_inc(sig["a_x1"], 1)

            def do_wog(b):
                after(dve, "a_in", b, 16)
                after(dve, "a_y", b - 1, 1)
                V.tensor_tensor(wog[:, :], wo0T[:, :], ga[:, :], ALU.mult).then_inc(sig["a_wog"], 1)

            def do_logits(b):
                after(dve, "b_gate", b, 1)
                V.tensor_copy(logits[:, :, :].rearrange("p t n -> p (t n)"), m0[:, 0:NT * NEX])\
                    .then_inc(sig["b_lg"], 1)

            def do_top(b):
                after_all(dve, ("b_lg", b, 1))
                for t in range(NT):
                    last = V.max(top[:, t, :], logits[:, t, :])
                last.then_inc(sig["b_tops"], 1)
                after_all(dve, ("b_tops", b, 1))
                for t in range(NT):
                    last = V.max_index(topi[:, t, :], top[:, t, :], logits[:, t, :])
                last.then_inc(sig["b_top"], 1)
                V.tensor_tensor(pw[:, 0, :, :], top[:, :, 1:2], top[:, :, 0:1], ALU.subtract)\
                    .then_inc(sig["b_dif"], 1)

            def do_weights(b):
                n = [0]

                def link_b(ins):
                    ins.then_inc(sig["b_route"], 1)
                    n[0] += 1
                    after(dve, "b_route", b, n[0])

                bc = lambda ap: ap.to_broadcast([P, NT, NEX])
                after(dve, "b_e2", b, 1)
                after(dve, "b_top", b, 1)
                after(dve, "b_sc", b - 1, 2 * NEX)
                link_b(V.tensor_scalar(pw[:, 2, :, :], pw[:, 1, :, :], 1.0, 2.0, ALU.add, ALU.mult))
                link_b(V.reciprocal(pw[:, 3, :, :], pw[:, 2, :, :]))
                V.tensor_tensor(pw[:, 4, :, :], pw[:, 3, :, :], pw[:, 1, :, :], ALU.mult)
                io = iota8[:, :].unsqueeze(1).to_broadcast([P, NT, NEX])
                link_b(V.tensor_copy(pick[:, 4, :, :], topi[:, :, :]))
                V.tensor_tensor(pick[:, 0, :, :], io, bc(pick[:, 4, :, 0:1]), ALU.is_equal)
                link_b(V.tensor_tensor(pick[:, 1, :, :], io, bc(pick[:, 4, :, 1:2]), ALU.is_equal))
                V.tensor_tensor(pick[:, 2, :, :], pick[:, 0, :, :], bc(pw[:, 3, :, :]), ALU.mult)\
                    .then_inc(sig["b_route"], 1)
                V.tensor_tensor(pick[:, 3, :, :], pick[:, 1, :, :], bc(pw[:, 4, :, :]), ALU.mult)\
                    .then_inc(sig["b_route"], 1)
                n[0] += 2
                after(dve, "b_route", b, n[0])
                link_b(V.tensor_tensor(pick[:, 5, :, :], pick[:, 2, :, :], pick[:, 3, :, :], ALU.add))

            def w0(b, u):
                after(dve, "b_tanh", b, u + 1)
                after(dve, "b_down", b, max(2 * (u // 2 - 1), 0))
                V.scalar_tensor_tensor(out=mu[:, u % 4, :], in0=th[:, :], scalar=1.0, in1=w0p[:, :],
                                       op0=ALU.add, op1=ALU.mult).then_inc(sig["b_u"], 1)

            def w1_(b, u):
                after(dve, "b_w1", b, u + 1)
                after(dve, "b_u", b, u + 1)
                V.tensor_tensor(mu[:, u % 4, :], mu[:, u % 4, :], w1p[:, :], ALU.mult).then_inc(sig["b_mu"], 1)

            def do_x2(b):
                after(dve, "b_acc", b, NEX - 1)
                after(dve, "b_in", b, 32)
                V.tensor_tensor(acc[:, :, :], acc[:, :, :], over_t(gb0[:, :]), ALU.mult).then_inc(sig["b_t"], 1)
                after(dve, "b_t", b, 1)
                after(dve, "c_x3", b - 1, 1)
                V.tensor_tensor(x2[:, :, :], acc[:, :, :], x1[:, :, :], ALU.add).then_inc(sig["b_x2"], 1)

            def mod(b):
                after(dve, "c_in", b, 16)
                after(dve, "c_xn", b, 1)
                after(dve, "c_res", b - 1, 1)
                V.tensor_tensor(hc[:, :, :], xcn[:, :, :], over_t(crow[:, 1, :]), ALU.mult).then_inc(sig["c_m1"], 1)
                after(dve, "c_m1", b, 1)
                V.tensor_tensor(hc[:, :, :], hc[:, :, :], over_t(crow[:, 0, :]), ALU.add).then_inc(sig["c_h"], 1)

            def kgb(b, p):
                after(dve, "c_qs", b, p + 1)
                if p == 0:
                    after(dve, "c_dn", b - 1, 2)
                at = slice(2 * p, 2 * p + 2)
                V.tensor_tensor(kq[:, 1, at, :], qz[:, :, :], gam[:, 1, :].unsqueeze(1).to_broadcast([P, 2, QK]),
                                ALU.mult).then_inc(sig["c_gk"], 1)
                after(dve, "c_gk", b, p + 1)
                V.tensor_tensor(kq[:, 1, at, :], kq[:, 1, at, :], bet[:, 1, :].unsqueeze(1).to_broadcast([P, 2, QK]),
                                ALU.add).then_inc(sig["c_kk"], 1)

            def qkz(b, p):
                after(dve, "c_qk", b, p + 1)
                after(dve, "c_qs", b, p)
                if p == 1:
                    after(dve, "c_kq", b, 1)
                    after(dve, "c_gk", b, 1)
                V.tensor_tensor(qz[:, :, :], m1[:, :].rearrange("p (n c) -> p n c", n=2),
                                bqk[:, :].unsqueeze(1).to_broadcast([P, 2, QK]), ALU.add).then_inc(sig["c_qz"], 1)

            def qks(b, p):
                after(dve, "c_qt", b, p + 1)
                V.scalar_tensor_tensor(out=qz[:, :, :], in0=qt[:, :, :], scalar=1.0, in1=qz[:, :, :], op0=ALU.add,
                                       op1=ALU.mult).then_inc(sig["c_qs"], 1)

            def hids(b, c):
                n = HID_ORDER.index(c)
                after(dve, "c_hz", b, n + 1)
                after(dve, "c_vg", b, n // 2)
                after(dve, "c_kq", b, 2)
                after(dve, "c_gk", b, 2)
                V.scalar_tensor_tensor(out=sil[n % 2], in0=hth[:, :], scalar=1.0, in1=hz[:, :], op0=ALU.add,
                                       op1=ALU.mult).then_inc(sig["c_hs"], 1)
                if n % 2:
                    after(dve, "c_hs", b, n + 1)
                    after(dve, "c_o", b - 1, 1)
                    V.tensor_tensor(vg[:, n // 2, :], sil[0], sil[1], ALU.mult).then_inc(sig["c_vg"], 1)

            def simmax(b):
                after(dve, "c_sim", b, 1)
                V.tensor_reduce(cst[:, 0, :], m1[:, :].rearrange("p (n c) -> p n c", n=2), AX, ALU.max, negate=True)\
                    .then_inc(sig["c_nm"], 1)
                after(dve, "c_nm", b, 1)
                V.tensor_scalar(cst[:, 1, :], cst[:, 0, :], 1.0 / S, None, ALU.mult).then_inc(sig["c_nms"], 1)

            def simsum(b):
                after(dve, "c_ea", b, 2)
                V.reciprocal(cst[:, 3, :], cst[:, 2, :]).then_inc(sig["c_r"], 1)
                after(dve, "c_r", b, 1)
                for n in range(2):
                    last = V.tensor_scalar(ea[:, n, :], ea[:, n, :], cst[:, 3, n:n + 1], 0.0, ALU.mult, ALU.add,
                                           accum_out=cst[:, 4, n:n + 1])
                last.then_inc(sig["c_rs"], 1)
                after(dve, "c_rs", b, 1)
                after(dve, "c_o", b - 1, 1)
                for n in range(2):
                    last = V.tensor_scalar(wos[:, n, :], wout[:, n, :], cst[:, 4, n:n + 1], 0.25, ALU.mult, ALU.mult)
                last.then_inc(sig["c_wo"], 1)

            def res(b):
                after(dve, "c_o", b, 1)
                after(dve, "c_lo", b, 1)
                after(dve, "c_qk", b, 2)
                V.tensor_tensor(tc[:, :, :], bank_t(m1), over_t(bout[:, :]), ALU.add).then_inc(sig["c_o1"], 1)
                after(dve, "c_o1", b, 1)
                V.tensor_tensor(tc[:, :, :], tc[:, :, :], hc[:, :, :], ALU.add).then_inc(sig["c_res"], 1)
                after(dve, "c_res", b, 1)
                V.tensor_tensor(tc[:, :, :], tc[:, :, :], over_t(crow[:, 2, :]), ALU.mult).then_inc(sig["c_res"], 1)
                after(dve, "c_res", b, 2)
                after(dve, "c_stored", b - 1, 16)
                V.tensor_tensor(x3[:, :, :], tc[:, :, :], x2[:, :, :], ALU.add).then_inc(sig["c_x3"], 1)

            def upa(b, c):
                after(dve, "c_u2", b, c + 1)
                V.scalar_tensor_tensor(out=u2[:, :], in0=u2[:, :], scalar=1.0, in1=uz[:, :], op0=ALU.add,
                                       op1=ALU.mult).then_inc(sig["c_ub"], 1)

            def upg(b, c):
                after(dve, "c_ut", b, c + 1)
                V.scalar_tensor_tensor(out=gl[:, c, :], in0=u2[:, :], scalar=1.0, in1=uz[:, :], op0=ALU.add,
                                       op1=ALU.mult).then_inc(sig["c_gl"], 1)

            def fin(b, h):
                after(dve, "c_dn", b, h + 1)
                t = slice(2 * h, 2 * h + 2)
                V.scalar_tensor_tensor(out=tc3[:, t, :], in0=bank_t(m1)[:, t, :], scalar=0.5,
                                       in1=b2[:, :].unsqueeze(1).to_broadcast([P, 2, D]),
                                       op0=ALU.mult, op1=ALU.add).then_inc(sig["c_y1"], 1)
                after(dve, "c_y1", b, h + 1)
                after(dve, "c_ind", b, 48)
                V.tensor_tensor(tc3[:, t, :], tc3[:, t, :], cgb[:, :].unsqueeze(1).to_broadcast([P, 2, D]), ALU.mult)\
                    .then_inc(sig["c_yg"], 1)
                after(dve, "c_yg", b, h + 1)
                V.tensor_tensor(yout[:, t, :], tc3[:, t, :], x3[:, t, :], ALU.add).then_inc(sig["c_out"], 1)

            walk(dve, "dve", {
                ("P", "stats"): norm_stats("p", xp, [("p_in", 16)], "p_mv"),
                ("P", "rot"): rot, ("P", "max"): smax, ("P", "mparts"): mparts,
                ("A", "max"): smax, ("A", "mparts"): mparts, ("A", "onorm"): onorm, ("B", "onorm3"): onorm,
                ("B", "x1"): do_x1, ("A", "wog"): do_wog, ("B", "stats"): norm_stats("b", x1, [("a_x1", 1)], "b_mv"),
                ("B", "logits"): do_logits, ("B", "top"): do_top, ("B", "weights"): do_weights,
                ("B", "w0"): w0, ("B", "w1"): w1_, ("B", "x2"): do_x2,
                ("C", "stats"): norm_stats("c", x2, [("b_x2", 1)], "c_mv"),
                ("C", "stats2"): norm_stats("c", hc, [("c_h", 1)], "c_mv2"),
                ("C", "qkz"): qkz, ("C", "qks"): qks, ("C", "hids"): hids, ("C", "simmax"): simmax,
                ("C", "simsum"): simsum, ("C", "res"): res,
                ("C", "stats3"): norm_stats("d", x3, [("c_x3", 1)], "c_mv3"),
                ("C", "upa"): upa, ("C", "upg"): upg, ("C", "fin"): fin, ("C", "mod"): mod, ("C", "qkgb"): kgb},
                 {("P", "rot"): split_weights, ("P", "max"): late}, ready)

        @block.gpsimd
        def _(pool):
            G = nc.gpsimd
            pool.wait_ge(s_c, 16 * N_CONST)

            def ready():
                pool.wait_ge(s_sa, SA_END)
                G.tensor_tensor(e1_lo[:, :], raw1, as_f32(e1_hi[:, :]), ALU.subtract).then_inc(s_sg, 1)
                pool.wait_ge(s_c2, 16 * N_LATE)
                pool.wait_ge(s_sv, SV_END)
                pool.wait_ge(s_sa, SA_END)
                pool.wait_ge(s_sx, SX_END)

            def deviation(key, wait, eps, name, nm):
                def run(b):
                    after_all(pool, (wait, b, 1))
                    G.tensor_scalar(rstd[key][:, :].unsqueeze(2), mv[key][:, :, 1:2], EPS, None, ALU.add)\
                        .then_inc(sig[eps], 1)
                    G.tensor_scalar(shift_n[key][:, :].unsqueeze(2), mv[key][:, :, 0:1], -1.0, None, ALU.mult)\
                        .then_inc(sig[eps], 1)
                    after(pool, eps, b, 2)
                    G.tensor_tensor(rstd[key][:, :], rstd[key][:, :], nhalf[:, :], ALU.pow).then_inc(sig[name], 1)
                    after(pool, name, b, 1)
                    G.tensor_tensor(shift_n[key][:, :], shift_n[key][:, :], rstd[key][:, :], ALU.mult)\
                        .then_inc(sig[nm], 1)
                return run

            def lower(src, hi_, dst, wait, name):
                def run(b):
                    after(pool, wait, b, 1)
                    G.tensor_tensor(dst[:, :], src, as_f32(hi_[:, :]), ALU.subtract).then_inc(sig[name], 1)
                return run

            def split(b, n):
                after(pool, "p_rot", b, 2 * n + 2)
                after(pool, "p_part2", b, n)
                G.tensor_tensor(rem[:, :], rot1[:, :], rot2[:, :], ALU.add).then_inc(sig["p_sum"], 1)

            def split2(b, n):
                after(pool, "p_part0", b, n + 1)
                G.tensor_tensor(rem[:, :], rem[:, :], parts[:, 0, :], ALU.subtract).then_inc(sig["p_rem"], 1)

            def split3(b, n):
                after(pool, "p_part1", b, n + 1)
                G.tensor_tensor(parts[:, 2, :], rem[:, :], parts[:, 1, :], ALU.subtract).then_inc(sig["p_part2"], 1)

            def vcopy(b):
                after_all(pool, ("p_vn", b, 1), ("a_pv", b - 1, 16))
                G.tensor_copy(vaug[:, :, :, 0:HD], vtok[:, :, :].rearrange("p t (h d) -> p t h d", h=HEADS))\
                    .then_inc(sig["a_vc"], 1)

            def over_t(row):
                return row.unsqueeze(1).to_broadcast([P, NT, D])

            def qgb(b, p):
                after(pool, "c_qs", b, p + 1)
                if p == 0:
                    after(pool, "c_dn", b - 1, 2)
                at = slice(2 * p, 2 * p + 2)
                G.tensor_tensor(kq[:, 0, at, :], qz[:, :, :], gam[:, 0, :].unsqueeze(1).to_broadcast([P, 2, QK]),
                                ALU.mult).then_inc(sig["c_g"], 1)
                after(pool, "c_g", b, p + 1)
                G.tensor_tensor(kq[:, 0, at, :], kq[:, 0, at, :], bet[:, 0, :].unsqueeze(1).to_broadcast([P, 2, QK]),
                                ALU.add).then_inc(sig["c_kq"], 1)

            def accumulate(b, e):
                after(pool, "b_sc", b, 2 * e + 2)
                after(pool, "b_acc", b, e - 1)
                G.tensor_tensor(acc[:, :, :], acc[:, :, :], scaled[:, :, :], ALU.add).then_inc(sig["b_acc"], 1)

            walk(pool, "pool", {
                ("P", "rstd"): deviation("p", "p_mv", "p_eps", "p_rstd", "p_nm"),
                ("P", "lo"): lower(hp, hp_hi, hp_lo, "p_hi", "p_lo"), ("P", "split"): split, ("P", "split2"): split2,
                ("P", "split3"): split3,
                ("A", "vcopy"): vcopy, ("B", "acc"): accumulate,
                ("B", "rstd"): deviation("b", "b_mv", "b_eps", "b_rstd", "b_nm"),
                ("B", "lo"): lower(hb, hb_hi, hb_lo, "b_hi", "b_lo"),
                ("C", "rstd"): deviation("c", "c_mv", "c_eps", "c_rstd", "c_nm1"),
                ("C", "rstd2"): deviation("c", "c_mv2", "c_eps2", "c_rstd2", "c_nm2"),
                ("C", "lo"): lower(nt, n_hi, n_lo, "c_hi", "c_lo"),
                ("C", "qkgb"): qgb,
                ("C", "rstd3"): deviation("d", "c_mv3", "c_eps3", "c_rstd3", "c_nm3"),
                }, {}, ready)


N_CONST, N_LATE = 12, 17
SV_ONES = 3
SV_SILU = 8
SV_MOD = (24, 56)
SV_SPLIT = 40
SV_END = 58
SA_END = 8
SG_END = 1
SX_END = 2
PER_BATCH.update({n + "s": 1 for n in ("p_mv", "b_mv", "c_mv", "c_mv2", "c_mv3", "b_top")})

_INS = ['L0_attn_x', 'L0_attn_w_qkv', 'L0_attn_w_out', 'L0_ffn_gate_kernel', 'L0_ffn_w0_kernel', 'L0_ffn_w1_kernel',
        'L0_ffn_wo_kernel', 'L0_c', 'L0_wmod', 'L1_attn_ln_g', 'L1_attn_ln_b', 'L1_attn_W_hidden',
        'L1_attn_b_hidden', 'L1_attn_W_qk', 'L1_attn_b_qk', 'L1_attn_os_gamma', 'L1_attn_os_beta', 'L1_attn_W_out',
        'L1_attn_b_out', 'L1_ffn_w1', 'L1_ffn_b1', 'L1_ffn_w2', 'L1_ffn_b2', 'L1_c', 'L1_wmod']


def shape_constants():
    ids = np.arange(HD // 2, dtype=np.float32)
    theta = np.power(np.float32(10000.0), np.float32(2.0) * ids / np.float32(HD)).astype(np.float32)
    ang = (np.arange(S, dtype=np.float32)[:, None] / theta).astype(np.float32)
    rows = [np.repeat(f(ang).astype(np.float32), 2, axis=1).T for f in (np.cos, np.sin)]
    cosT, sinT = (np.ascontiguousarray(np.tile(r, (HEADS, 1))) for r in rows)
    return {"cosT": cosT, "sinT": sinT, "ident": np.eye(P, dtype=np.float32),
            "nhalf": np.full((P, NT), -0.5, np.float32),
            "iota8": np.tile(np.arange(NEX, dtype=np.float32), (P, 1))}


def kernel(**inputs):
    import concourse.bacc as bacc
    from concourse.bass_utils import run_bass_kernel_spmd

    nc = bacc.Bacc("TRN2", target_bir_lowering=False, num_devices=1)
    arrays, args = {}, {}
    given = {name: np.ascontiguousarray(inputs[name]) for name in _INS}
    for name, value in {**given, **shape_constants()}.items():
        arrays[f"in_{name}"] = value
        args[name] = nc.dram_tensor(f"in_{name}", value.shape, mybir.dt.from_np(value.dtype), kind="ExternalInput").ap()
    out = nc.dram_tensor("out", (NB, S, D), mybir.dt.float32, kind="ExternalOutput").ap()
    adaln_two_layers(nc, args, out)
    r = run_bass_kernel_spmd(nc, [arrays], core_ids=[0])
    return r.results[0]["out"]
```
